# Optimizing a Trainium2 kernel written in Bass

```python
import numpy as np
import jax
import jax.numpy as jnp

def _softmax(x, axis=-1):
    return jax.nn.softmax(x, axis=axis)

def _gelu(x):
    return jax.nn.gelu(x, approximate=True)

def _silu(x):
    return jax.nn.silu(x)

def _sigmoid(x):
    return jax.nn.sigmoid(x)

def _layernorm(x, axis=-1, eps=1e-05):
    m = jnp.mean(x, axis=axis, keepdims=True)
    v = jnp.var(x, axis=axis, keepdims=True)
    return (x - m) / jnp.sqrt(v + eps)

def _scatter_add(tgt, idx, src, axis=0):
    return tgt.at[idx].add(src)

def _segment_sum(src, seg, n):
    return jax.ops.segment_sum(src, seg, n)
kernel_name = 'mk_conv_preact_d4_conv_nchw64_r2_c9aec5'

def setup_inputs(seed: int=0):
    np.random.seed(seed)
    _w = jnp.asarray

    def _rec_inputs():
        import jax
        import jax.numpy as jnp
        _gk = jax.random.key(seed)
        x = 1.648e-05 + 1 * jax.random.normal(jax.random.fold_in(_gk, 1), (4, 32, 96, 96), jnp.float32)
        return x
    x = _rec_inputs()

    def _L0_conv_setup():
        import jax, jax.numpy as jnp
        import numpy as np
        BLOCK, HALO, HEADS = (8, 3, 4)
        WIN = BLOCK + 2 * HALO

        def _unfold_halo(t, nh, nw):
            B, C = (t.shape[0], t.shape[1])
            tp = jnp.pad(t, ((0, 0), (0, 0), (HALO, HALO), (HALO, HALO)))
            ri = (jnp.arange(nh) * BLOCK)[:, None] + jnp.arange(WIN)
            ci = (jnp.arange(nw) * BLOCK)[:, None] + jnp.arange(WIN)
            p = tp[:, :, ri, :]
            p = p[:, :, :, :, ci]
            p = p.transpose(0, 2, 4, 3, 5, 1)
            return p.reshape(B * nh * nw, WIN * WIN, C)
        key = jax.random.key(seed)
        k1, k2, k3, k4 = jax.random.split(key, 4)
        B, C, H, W = (4, 32, 96, 96)
        d = C // HEADS
        return {'x': jax.random.normal(k1, (B, C, H, W), dtype=jnp.float32), 'w_qkv': jax.random.normal(k2, (3 * C, C), dtype=jnp.float32) * 0.05, 'rel_h': jax.random.normal(k3, (1, WIN, 1, d // 2), dtype=jnp.float32), 'rel_w': jax.random.normal(k4, (1, 1, WIN, d // 2), dtype=jnp.float32)}
    _L0_conv_all = _L0_conv_setup()
    _L0_conv_in = {k: v for k, v in _L0_conv_all.items() if k in ('w_qkv', 'rel_h', 'rel_w')}
    del _L0_conv_all

    def _L1_conv_setup():
        import jax, jax.numpy as jnp
        import numpy as np
        B, C, F, T = (4, 32, 257, 128)
        H, OUT = (128, 32)

        def _lstm(y, W_ih, W_hh, b_ih, b_hh):
            N, Tl, _ = y.shape
            Hd = W_hh.shape[1]
            x_gates = jnp.einsum('ntc,gc->ntg', y, W_ih) + b_ih + b_hh

            def step(carry, xg):
                h, c = carry
                g = xg + h @ W_hh.T
                i, f, gg, o = jnp.split(g, 4, axis=-1)
                c = jax.nn.sigmoid(f) * c + jax.nn.sigmoid(i) * jnp.tanh(gg)
                h = jax.nn.sigmoid(o) * jnp.tanh(c)
                return ((h, c), h)
            h0 = jnp.zeros((N, Hd), y.dtype)
            _, hs = jax.lax.scan(step, (h0, h0), jnp.swapaxes(x_gates, 0, 1))
            return jnp.swapaxes(hs, 0, 1)
        key = jax.random.key(seed)
        ks = jax.random.split(key, 7)
        w = lambda k, shape: jax.random.normal(k, shape, dtype=jnp.float32) * 0.05
        return {'x': jax.random.normal(ks[0], (B, C, F, T), dtype=jnp.float32), 'W_ih': w(ks[1], (4 * H, C)), 'W_hh': w(ks[2], (4 * H, H)), 'b_ih': w(ks[3], (4 * H,)), 'b_hh': w(ks[4], (4 * H,)), 'W_lin': w(ks[5], (OUT, H)), 'b_lin': w(ks[6], (OUT,))}
    _L1_conv_all = _L1_conv_setup()
    _L1_conv_in = {k: v for k, v in _L1_conv_all.items() if k in ('W_ih', 'W_hh', 'b_ih', 'b_hh', 'W_lin', 'b_lin')}
    del _L1_conv_all

    def _L2_conv_setup():
        import jax, jax.numpy as jnp
        import numpy as np
        B, C, H, W = (4, 32, 64, 64)
        KS = 3
        PAD = 1
        N = KS * KS

        def conv2d(x, w, b=None, stride=1, padding=0):
            out = jax.lax.conv_general_dilated(x, w, (stride, stride), [(padding, padding), (padding, padding)], dimension_numbers=('NCHW', 'OIHW', 'NCHW'))
            if b is not None:
                out = out + b[None, :, None, None]
            return out
        key = jax.random.key(seed)
        ks = jax.random.split(key, 6)
        scale = 0.05
        return {'x': jax.random.normal(ks[0], (B, C, H, W), jnp.float32), 'p_w': jax.random.normal(ks[1], (2 * N, C, 3, 3), jnp.float32) * scale, 'p_b': jax.random.normal(ks[2], (2 * N,), jnp.float32) * scale, 'm_w': jax.random.normal(ks[3], (N, C, 3, 3), jnp.float32) * scale, 'm_b': jax.random.normal(ks[4], (N,), jnp.float32) * scale, 'conv_w': jax.random.normal(ks[5], (C, C, KS, KS), jnp.float32) * (1.0 / np.sqrt(C * N))}
    _L2_conv_all = _L2_conv_setup()
    _L2_conv_in = {k: v for k, v in _L2_conv_all.items() if k in ('p_w', 'p_b', 'm_w', 'm_b', 'conv_w')}
    del _L2_conv_all

    def _L3_conv_setup():
        import jax, jax.numpy as jnp
        import numpy as np
        BS = 8

        def _catalan_number(n):
            if n <= 1:
                return 1
            dp = [0] * (n + 1)
            dp[0] = dp[1] = 1
            for i in range(2, n + 1):
                for j in range(i):
                    dp[i] += dp[j] * dp[i - 1 - j]
            return dp[n]

        def _make_catalan_matrix(n):
            cats = [_catalan_number(i) for i in range(2 * n)]
            Mraw = np.array([[cats[i + j] for j in range(n)] for i in range(n)], dtype=np.float64)
            Q, _ = np.linalg.qr(Mraw)
            return Q.astype(np.float32)
        key = jax.random.key(seed)
        x = jax.random.normal(key, (16, 32, 256, 256), dtype=jnp.float32)
        M = jnp.asarray(_make_catalan_matrix(BS))
        return {'x': x, 'M': M}
    _L3_conv_all = _L3_conv_setup()
    _L3_conv_in = {k: v for k, v in _L3_conv_all.items() if k in ('M',)}
    del _L3_conv_all
    return {'x': x, 'L0_conv_w_qkv': _L0_conv_in['w_qkv'], 'L0_conv_rel_h': _L0_conv_in['rel_h'], 'L0_conv_rel_w': _L0_conv_in['rel_w'], 'L1_conv_W_ih': _L1_conv_in['W_ih'], 'L1_conv_W_hh': _L1_conv_in['W_hh'], 'L1_conv_b_ih': _L1_conv_in['b_ih'], 'L1_conv_b_hh': _L1_conv_in['b_hh'], 'L1_conv_W_lin': _L1_conv_in['W_lin'], 'L1_conv_b_lin': _L1_conv_in['b_lin'], 'L2_conv_p_w': _L2_conv_in['p_w'], 'L2_conv_p_b': _L2_conv_in['p_b'], 'L2_conv_m_w': _L2_conv_in['m_w'], 'L2_conv_m_b': _L2_conv_in['m_b'], 'L2_conv_conv_w': _L2_conv_in['conv_w'], 'L3_conv_M': _L3_conv_in['M']}

def reference(x, L0_conv_w_qkv, L0_conv_rel_h, L0_conv_rel_w, L1_conv_W_ih, L1_conv_W_hh, L1_conv_b_ih, L1_conv_b_hh, L1_conv_W_lin, L1_conv_b_lin, L2_conv_p_w, L2_conv_p_b, L2_conv_m_w, L2_conv_m_b, L2_conv_conv_w, L3_conv_M):
    import jax
    import jax.numpy as jnp

    def _L0_conv_ref(x, w_qkv, rel_h, rel_w):
        import jax, jax.numpy as jnp
        import numpy as np
        BLOCK, HALO, HEADS = (8, 3, 4)
        WIN = BLOCK + 2 * HALO

        def _unfold_halo(t, nh, nw):
            B, C = (t.shape[0], t.shape[1])
            tp = jnp.pad(t, ((0, 0), (0, 0), (HALO, HALO), (HALO, HALO)))
            ri = (jnp.arange(nh) * BLOCK)[:, None] + jnp.arange(WIN)
            ci = (jnp.arange(nw) * BLOCK)[:, None] + jnp.arange(WIN)
            p = tp[:, :, ri, :]
            p = p[:, :, :, :, ci]
            p = p.transpose(0, 2, 4, 3, 5, 1)
            return p.reshape(B * nh * nw, WIN * WIN, C)
        B, C, H, W = x.shape
        d = C // HEADS
        nh, nw = (H // BLOCK, W // BLOCK)
        qkv = jnp.einsum('bchw,oc->bohw', x, w_qkv)
        q, k, v = jnp.split(qkv, 3, axis=1)
        q = q.reshape(B, C, nh, BLOCK, nw, BLOCK).transpose(0, 2, 4, 3, 5, 1)
        q = q.reshape(B * nh * nw, BLOCK * BLOCK, C) * d ** (-0.5)
        k = _unfold_halo(k, nh, nw)
        v = _unfold_halo(v, nh, nw)
        q = q.reshape(-1, BLOCK * BLOCK, HEADS, d).transpose(0, 2, 1, 3).reshape(-1, BLOCK * BLOCK, d)
        v = v.reshape(-1, WIN * WIN, HEADS, d).transpose(0, 2, 1, 3).reshape(-1, WIN * WIN, d)
        k = k.reshape(-1, WIN, WIN, HEADS, d).transpose(0, 3, 1, 2, 4).reshape(-1, WIN, WIN, d)
        kh, kw = (k[..., :d // 2], k[..., d // 2:])
        k = jnp.concatenate([kh + rel_h, kw + rel_w], axis=-1).reshape(-1, WIN * WIN, d)
        sim = jnp.einsum('bid,bjd->bij', q, k)
        attn = jax.nn.softmax(sim, axis=-1)
        out = jnp.einsum('bij,bjd->bid', attn, v)
        out = out.reshape(B, nh, nw, HEADS, BLOCK, BLOCK, d)
        out = out.transpose(0, 3, 6, 1, 4, 2, 5).reshape(B, HEADS * d, nh * BLOCK, nw * BLOCK)
        return out

    def _L1_conv_ref(x, W_ih, W_hh, b_ih, b_hh, W_lin, b_lin):
        import jax, jax.numpy as jnp
        import numpy as np
        B, C, F, T = (4, 32, 257, 128)
        H, OUT = (128, 32)

        def _lstm(y, W_ih, W_hh, b_ih, b_hh):
            N, Tl, _ = y.shape
            Hd = W_hh.shape[1]
            x_gates = jnp.einsum('ntc,gc->ntg', y, W_ih) + b_ih + b_hh

            def step(carry, xg):
                h, c = carry
                g = xg + h @ W_hh.T
                i, f, gg, o = jnp.split(g, 4, axis=-1)
                c = jax.nn.sigmoid(f) * c + jax.nn.sigmoid(i) * jnp.tanh(gg)
                h = jax.nn.sigmoid(o) * jnp.tanh(c)
                return ((h, c), h)
            h0 = jnp.zeros((N, Hd), y.dtype)
            _, hs = jax.lax.scan(step, (h0, h0), jnp.swapaxes(x_gates, 0, 1))
            return jnp.swapaxes(hs, 0, 1)
        b, c, f, t = x.shape
        y = x.transpose(0, 2, 3, 1).reshape(b * f, t, c)
        h = _lstm(y, W_ih, W_hh, b_ih, b_hh)
        out = h @ W_lin.T + b_lin
        return out.reshape(b, f, t, -1).transpose(0, 3, 1, 2)

    def _L2_conv_ref(x, p_w, p_b, m_w, m_b, conv_w):
        import jax, jax.numpy as jnp
        import numpy as np
        B, C, H, W = (4, 32, 64, 64)
        KS = 3
        PAD = 1
        N = KS * KS

        def conv2d(x, w, b=None, stride=1, padding=0):
            out = jax.lax.conv_general_dilated(x, w, (stride, stride), [(padding, padding), (padding, padding)], dimension_numbers=('NCHW', 'OIHW', 'NCHW'))
            if b is not None:
                out = out + b[None, :, None, None]
            return out
        b, c, h, w = x.shape
        offset = conv2d(x, p_w, p_b, 1, 1)
        m = jax.nn.sigmoid(conv2d(x, m_w, m_b, 1, 1))
        xp = jnp.pad(x, ((0, 0), (0, 0), (PAD, PAD), (PAD, PAD)))
        Hp, Wp = (h + 2 * PAD, w + 2 * PAD)
        pnx, pny = jnp.meshgrid(jnp.arange(-1, 2), jnp.arange(-1, 2), indexing='ij')
        p_n = jnp.concatenate([pnx.ravel(), pny.ravel()]).astype(x.dtype)
        base_x = jnp.broadcast_to(jnp.arange(1, h + 1)[:, None, None], (h, w, N))
        base_y = jnp.broadcast_to(jnp.arange(1, w + 1)[None, :, None], (h, w, N))
        base = jnp.concatenate([base_x, base_y], axis=-1).astype(x.dtype)
        p = jnp.transpose(offset, (0, 2, 3, 1)) + p_n + base[None]
        px, py = (p[..., :N], p[..., N:])
        qf = jnp.floor(jax.lax.stop_gradient(p))
        qx_lt = jnp.clip(qf[..., :N], 0, Hp - 1).astype(jnp.int32)
        qy_lt = jnp.clip(qf[..., N:], 0, Wp - 1).astype(jnp.int32)
        qx_rb = jnp.clip(qf[..., :N] + 1, 0, Hp - 1).astype(jnp.int32)
        qy_rb = jnp.clip(qf[..., N:] + 1, 0, Wp - 1).astype(jnp.int32)
        pxc = jnp.clip(px, 0, Hp - 1)
        pyc = jnp.clip(py, 0, Wp - 1)
        g_lt = (1 + (qx_lt - pxc)) * (1 + (qy_lt - pyc))
        g_rb = (1 - (qx_rb - pxc)) * (1 - (qy_rb - pyc))
        g_lb = (1 + (qx_lt - pxc)) * (1 - (qy_rb - pyc))
        g_rt = (1 - (qx_rb - pxc)) * (1 + (qy_lt - pyc))
        xp_flat = xp.reshape(b, c, Hp * Wp)

        def gather(qx, qy):
            idx = (qx * Wp + qy).reshape(b, -1)
            out = jax.vmap(lambda xf, i: xf[:, i])(xp_flat, idx)
            return out.reshape(b, c, h, w, N)
        x_off = g_lt[:, None] * gather(qx_lt, qy_lt) + g_rb[:, None] * gather(qx_rb, qy_rb) + g_lb[:, None] * gather(qx_lt, qy_rb) + g_rt[:, None] * gather(qx_rb, qy_lt)
        x_off = x_off * jnp.transpose(m, (0, 2, 3, 1))[:, None]
        x_off = x_off.reshape(b, c, h, w, KS, KS)
        x_off = jnp.transpose(x_off, (0, 1, 2, 4, 3, 5)).reshape(b, c, h * KS, w * KS)
        return conv2d(x_off, conv_w, None, stride=KS, padding=0)

    def _L3_conv_ref(x, M):
        import jax, jax.numpy as jnp
        import numpy as np
        BS = 8

        def _catalan_number(n):
            if n <= 1:
                return 1
            dp = [0] * (n + 1)
            dp[0] = dp[1] = 1
            for i in range(2, n + 1):
                for j in range(i):
                    dp[i] += dp[j] * dp[i - 1 - j]
            return dp[n]

        def _make_catalan_matrix(n):
            cats = [_catalan_number(i) for i in range(2 * n)]
            Mraw = np.array([[cats[i + j] for j in range(n)] for i in range(n)], dtype=np.float64)
            Q, _ = np.linalg.qr(Mraw)
            return Q.astype(np.float32)
        B, C, H, W = x.shape
        n = BS
        xb = x.reshape(B, C, H // n, n, W // n, n)
        out = jnp.einsum('ik,bcpkql,jl->bcpiqj', M, xb, M)
        return out.reshape(B, C, H, W)

    def _gn(v, G=32, eps=1e-05):
        B_, C_, H_, W_ = v.shape
        g = v.reshape(B_, G, C_ // G, H_, W_)
        m = jnp.mean(g, axis=(2, 3, 4), keepdims=True)
        s = jnp.var(g, axis=(2, 3, 4), keepdims=True)
        return ((g - m) / jnp.sqrt(s + eps)).reshape(v.shape)

    def _ln_c(v, eps=1e-06):
        m = jnp.mean(v, axis=1, keepdims=True)
        s = jnp.var(v, axis=1, keepdims=True)
        return (v - m) / jnp.sqrt(s + eps)

    def _ln_t(v, eps=1e-05):
        m = jnp.mean(v, axis=-1, keepdims=True)
        s = jnp.var(v, axis=-1, keepdims=True)
        return (v - m) / jnp.sqrt(s + eps)

    def _to_tokens(v):
        B_, C_, H_, W_ = v.shape
        return v.reshape(B_, C_, H_ * W_).transpose(0, 2, 1)

    def _from_tokens(t, like):
        B_, C_, H_, W_ = like.shape
        return t.transpose(0, 2, 1).reshape(B_, C_, H_, W_)
    x = x + _L0_conv_ref(_gn(x), L0_conv_w_qkv, L0_conv_rel_h, L0_conv_rel_w)
    x = x + _L1_conv_ref(_gn(x), L1_conv_W_ih, L1_conv_W_hh, L1_conv_b_ih, L1_conv_b_hh, L1_conv_W_lin, L1_conv_b_lin)
    x = x + _L2_conv_ref(_gn(x), L2_conv_p_w, L2_conv_p_b, L2_conv_m_w, L2_conv_m_b, L2_conv_conv_w)
    x = x + _L3_conv_ref(_gn(x), L3_conv_M)
    return x

_drawn_inputs = setup_inputs


def setup_inputs(seed=0):
    import zlib

    import numpy as np

    out = dict(_drawn_inputs(seed))
    spreads = {}
    factors = {'L0_conv_rel_h': 8.0,
     'L0_conv_rel_w': 8.0,
     'L1_conv_W_hh': 5.095,
     'L1_conv_b_ih': 6.837,
     'L1_conv_b_hh': 5.571,
     'L2_conv_m_b': 7.388}
    for name, (base, spread) in spreads.items():
        noise = np.random.default_rng([zlib.crc32(name.encode()), seed]).standard_normal(out[name].shape)
        drawn = base * np.exp(spread * noise) if base else spread * noise
        out[name] = jnp.asarray(drawn.astype(out[name].dtype))
    for name, factor in factors.items():
        out[name] = (out[name] * factor).astype(out[name].dtype)
    return out
```

```python
from contextlib import ExitStack
import concourse.bass as bass
from concourse import mybir

F32 = mybir.dt.float32
BF16 = mybir.dt.bfloat16
I32 = mybir.dt.int32
U32 = mybir.dt.uint32
ALU = mybir.AluOpType
ACT = mybir.ActivationFunctionType
AX = mybir.AxisListType

P = 128
B, C, H, W = 4, 32, 96, 96
HALO = 3
XROWS = HALO + H + 21
GN_EPS = 1e-5


def instance_stats(eng, x_rows, stats, mean_var, sem, start):
    flat = x_rows.rearrange("p h w -> p (h w)")
    n = H * W // 512
    for i in range(n):
        eng.bn_stats(stats[:, 6 * i:6 * i + 6], flat[:, 512 * i:512 * (i + 1)]).then_inc(sem, 1)
    eng.wait_ge(sem, start + n)
    eng.bn_aggr(mean_var, stats[:, 0:6 * n]).then_inc(sem, 1)
    return start + n + 1




def wait_apart(eng, sem, value, passed):
    eng.wait_ge(sem, value)
    eng.sem_inc(passed, 1)


BLOCK = 8
WIN = BLOCK + 2 * HALO
HEADS = 4
D = C // HEADS
NB = 6
KEYS = WIN * WIN
HKEYS = KEYS // 2
QS = BLOCK * BLOCK
NHB = H // BLOCK
SCOLS = NB * BLOCK + 2 * HALO
NTERM = 6
ROWS = NTERM * 2 * D
NFILL = 6
MISC = 13


def halo_attention_layer(nc, x, w_q, w_k, w_v, rel, head_mask, head_rows, identity, k_parts, q_parts):
    ctx = ExitStack()
    with ctx:
        def sb(name, shape, dt=F32):
            return ctx.enter_context(nc.sbuf_tensor("l0_" + name, shape, dt))

        def sem(name):
            return ctx.enter_context(nc.semaphore("l0_" + name))

        stats = sb("stats", [P, 6 * (H * W // 512)])
        mv = sb("mv", [P, 2])
        std = sb("std", [P, 1])
        rstd = sb("rstd", [P, 1])
        shift = sb("shift", [P, 1])
        eps = sb("eps", [P, 1])
        wq = sb("wq", [P, P])
        wk = sb("wk", [P, P])
        wv = sb("wv", [P, P])
        relb = sb("relb", [P, WIN, WIN])
        hmask = sb("hmask", [P, 2])
        ident = sb("ident", [P, P])
        strip = sb("strip", [P, 2, WIN, SCOLS])
        xwin = sb("xwin", [P, 2, NB, KEYS])
        k32 = sb("k32", [P, NB, KEYS])
        kp = sb("kp", [P, 3, NB, KEYS], BF16)
        q32 = sb("q32", [P, NB, 2, QS])
        qp = sb("qp", [P, 3, NB, 2, QS], BF16)
        kst = sb("kst", [P, 2, 2, 2, 2, NB, KEYS], BF16)
        qst = sb("qst", [P, 2, 2, 2, 2, NB, 2, QS], BF16)
        v = sb("v", [HKEYS, 2, NB * 2, B, HEADS, 2 * D])
        pt = sb("pt", [HKEYS, 2, 2, 2, 2, 2 * QS])
        mx = sb("mx", [P, 2, 2, NB])
        mparts = sb("mparts", [2 * NB, 2, 2, P], BF16)
        osb = sb("osb", [P, 2, B, BLOCK * NB * BLOCK])
        hrows = sb("hrows", [P, 2, C])
        quot = sb("quot", [P, BLOCK * NB * BLOCK // 2])

        def ps(name):
            return ctx.enter_context(nc.psum_tensor("l0_" + name, [P, 512], F32))

        s_ps = [ps(f"s{i}") for i in range(2)]
        st_ps = [ctx.enter_context(nc.psum_tensor(f"l0_st{i}", [P, 1024], F32)) for i in range(2)]
        pv_ps = ps("pv")
        misc_ps = ps("misc")

        consts_in = sem("consts_in")
        w_zero = sem("w_zero")
        pool_passed = sem("pool_passed")
        sp_passed = sem("sp_passed")
        fills_set = sem("fills_set")
        pv_zero = sem("pv_zero")
        eps_set = sem("eps_set")
        dve_prep = sem("dve_prep")
        pads_mean = sem("pads_mean")
        std_ready = sem("std_ready")
        strip_ready = sem("strip_ready")
        win_ready = sem("win_ready")
        misc_done = sem("misc_done")
        misc_read = sem("misc_read")
        k32_ready = sem("k32_ready")
        q32_ready = sem("q32_ready")
        split_step = sem("split_step")
        k_split = sem("k_split")
        q_split = sem("q_split")
        v_ready = sem("v_ready")
        parts_stored = sem("parts_stored")
        stacked = [[sem(f"stacked{i}{j}") for j in range(2)] for i in range(2)]
        s_filled = sem("s_filled")
        s_read = sem("s_read")
        m_split = sem("m_split")
        m_placed = [sem(f"m_placed{i}") for i in range(B)]
        st_done = sem("st_done")
        exp_done = sem("exp_done")
        pv_done = sem("pv_done")
        pv_read = sem("pv_read")
        recip_done = sem("recip_done")
        quot_done = sem("quot_done")
        x_added = sem("x_added")

        EARLY = 12
        LOADS = 4
        STORES = 9
        USES = ([("k", 0), ("k", 1), ("k", 2)], [("q", 0), ("v", 0)], [("v", 1), ("v", 2)], [("o", 0), ("o", 1)])
        K_RUNS = ((0, 3), (3, 2), (5, 1))
        Q_TERMS = ((0, 0), (0, 1), (0, 2), (1, 3), (1, 4), (2, 5))
        x_img = x[:, HALO:HALO + H, :]

        def use_number(G, b, i):
            return G * MISC + (EARLY + sum(1 + len(USES[a]) for a in range(b)) + i)

        block = ctx.enter_context(nc.Block())

        @block.sync
        def _(sp):
            sp.wait_ge(w_zero, 3)
            for b in range(B):
                for dst, src in ((wq, w_q), (wk, w_k), (wv, w_v)):
                    sp.dma_start(dst[C * b:C * (b + 1), C * b:C * (b + 1)], src).then_inc(consts_in, 16)
            for dst, src in ((relb[:, :, :].rearrange("p i j -> p (i j)"), rel), (hmask[:, :], head_mask), (ident[:, :], identity),
                             (hrows[:, :, :].rearrange("p k c -> p (k c)"), head_rows)):
                sp.dma_start(dst, src).then_inc(consts_in, 16)

            def store_parts(G, half, reused=None):
                if reused is not None:
                    for load in range(2):
                        wait_apart(sp, stacked[half][load], 16 * LOADS * reused, sp_passed)
                sp.wait_ge(q_split, G + 1)
                for i in range(3):
                    sp.dma_start(k_parts[half, :, i, :, :], kp[:, i, :, :]).then_inc(parts_stored, 16)
                for i, term in Q_TERMS:
                    sp.dma_start(q_parts[half, :, term, :, :], qp[:, i, :, :, :]).then_inc(parts_stored, 16)

            def load_stacks(G, half, load, used):
                wait_apart(sp, parts_stored, 16 * STORES * (G + 1), sp_passed)
                if used is not None:
                    sp.wait_ge(st_done, used)
                groups = slice(4 * load, 4 * load + 4)
                for term, n in K_RUNS:
                    sp.dma_start(kst[2 * D * term:2 * D * (term + n), half, load].rearrange("p b a k n -> p (b a) (k n)"),
                                 k_parts[half, groups, 0:n].rearrange("g t r n -> (t r) g n")).then_inc(stacked[half][load], 16)
                sp.dma_start(qst[0:ROWS, half, load].rearrange("p b a k s q -> p (b a) (k s q)"),
                             q_parts[half, groups].rearrange("g t r n -> (t r) g n")).then_inc(stacked[half][load], 16)

            def place_maxima(U, par, half, b):
                sp.wait_ge(m_split, 2 * U + 2)
                for i in range(2):
                    sp.dma_start(qst[ROWS + i:ROWS + i + 1, half, b // 2, b % 2],
                                 mparts[0:2 * NB, par, i, :]).then_inc(m_placed[b], 16)

            store_parts(0, 0)
            for load in range(2):
                load_stacks(0, 0, load, None)
            store_parts(1, 1)
            place_maxima(0, 0, 0, 0)
            with sp.Fori(0, NHB) as hb:
                for half in range(2):
                    G = hb * 2 + half
                    for b in range(B):
                        U = G * B + b
                        if b % 2 == 0:
                            load_stacks(G + 1, 1 - half, b // 2, G * 12)
                        place_maxima(U + 1, (b + 1) % 2, (half + (b + 1) // B) % 2, (b + 1) % B)
                    store_parts(G + 2, half, reused=hb + 1)
            for load in range(2):
                sp.wait_ge(stacked[0][load], 16 * LOADS * (NHB + 1))
                sp.wait_ge(stacked[1][load], 16 * LOADS * NHB)
            for b in range(B):
                sp.wait_ge(m_placed[b], 32 * (2 * NHB + (b < 1)))
            sp.wait_ge(parts_stored, 16 * STORES * (2 * NHB + 2))

        @block.gpsimd
        def _(pool):
            for w in (wq, wk, wv):
                pool.memset(w[:, :], 0.0).then_inc(w_zero, 1)
            pool.memset(eps[:, :], GN_EPS).then_inc(eps_set, 1)
            pool.memset(strip[:, :, :, :], 0.0).then_inc(fills_set, 1)
            pool.memset(v[:, :, :, :, :, :], 1.0).then_inc(fills_set, 1)
            pool.wait_ge(fills_set, 2)
            pool.memset(kst[ROWS:ROWS + 2].rearrange("p h l b a k n -> p (h l b a k n)"), 1.0).then_inc(fills_set, 1)
            pool.wait_ge(fills_set, 3)
            pool.memset(osb[:, 1], 1.0).then_inc(fills_set, 1)

            def windows(G, half):
                wait_apart(pool, strip_ready, G + 1, pool_passed)
                for blk in range(NB):
                    ins = pool.tensor_copy(xwin[:, half, blk, :].rearrange("p (i j) -> p i j", j=WIN),
                                           strip[:, half, :, BLOCK * blk:BLOCK * blk + WIN])
                ins.then_inc(win_ready, 1)

            def split(G, src, parts, done):
                start = G * 8 + (0 if src is k32 else 4)
                flat = src[:, :, :] if src is k32 else src[:, :, :, :]
                for i, (out, ins) in enumerate((
                        (parts[:, 0], None), (flat, parts[:, 0]), (parts[:, 1], None), (parts[:, 2], parts[:, 1]))):
                    if i:
                        wait_apart(pool, split_step, start + i, pool_passed)
                    if ins is None:
                        pool.tensor_copy(out, flat).then_inc(split_step, 1)
                    else:
                        pool.tensor_tensor(out, flat, ins, ALU.subtract).then_inc(split_step, 1)
                pool.wait_ge(split_step, start + 4)
                pool.sem_inc(done, 1)

            def splits(G):
                if not (isinstance(G, int) and G == 0):
                    pool.wait_ge(parts_stored, 16 * STORES * G)
                wait_apart(pool, k32_ready, 3 * G + 3, pool_passed)
                split(G, k32, kp, k_split)
                wait_apart(pool, q32_ready, 2 * G + 2, pool_passed)
                split(G, q32, qp, q_split)

            for half in range(2):
                windows(half, half)
            for G in range(2):
                splits(G)
            pool.wait_ge(misc_done, 7)
            windows(2, 0)
            with pool.Fori(0, NHB) as hb:
                for half in range(2):
                    G = hb * 2 + half
                    splits(G + 2)
                    pool.wait_ge(misc_done, use_number(G, 2, len(USES[2])) + 1)
                    windows(G + 3, 1 - half)

        @block.scalar
        def _(act):
            act.wait_ge(eps_set, 1)
            act.wait_ge(dve_prep, 19)
            act.activation(std[:, :], mv[:, 1:2], ACT.Sqrt, bias=eps[:, :]).then_inc(std_ready, 1)
            act.wait_ge(consts_in, 16 * 16)
            act.sem_inc(exp_done, 1)
            act.sem_inc(misc_read, 1)
            act.wait_ge(fills_set, 4)
            act.wait_ge(pads_mean, 4)

            def load(hb, half):
                to, of = (slice(HALO, SCOLS), slice(0, SCOLS - HALO)) if half == 0 else \
                         (slice(0, SCOLS - HALO), slice(W - (SCOLS - HALO), W))
                act.activation(strip[:, half, :, to], x[:, bass.ds(hb * BLOCK, WIN), of], ACT.Identity,
                               bias=shift[:, 0:1], scale=rstd[:, 0:1]).then_inc(strip_ready, 1)

            def read_q(G, n):
                act.wait_ge(misc_done, n + 1)
                act.wait_ge(q_split, G)
                for slot in range(2):
                    ins = act.activation(q32[:, :, slot, :], misc_ps[:, 0:NB * QS].rearrange("p (k q) -> p k q", q=QS),
                                         ACT.Copy, scale=hmask[:, slot:slot + 1])
                    ins.then_inc(q32_ready, 1)
                act.wait_ge(q32_ready, 2 * G + 2)
                act.sem_inc(misc_read, 1)

            def read_v(G, half, i, n):
                act.wait_ge(misc_done, n + 1)
                act.wait_ge(fills_set, 4)
                if not isinstance(G, int):
                    act.wait_ge(pv_done, G * 12 - 11)
                act.activation(v[:, half, 4 * i:4 * i + 4, :, :, 0:D].rearrange("p t b h d -> p t (b h) d"),
                               misc_ps[0:HKEYS, :].rearrange("p (t m d) -> p t m d", t=4, d=D), ACT.Copy).then_inc(v_ready, 1)
                act.wait_ge(v_ready, 3 * G + i + 1)
                act.sem_inc(misc_read, 1)

            def exps(st, slot):
                act.wait_ge(st_done, st + 1)
                act.wait_ge(pv_done, st)
                act.activation(pt[:, slot].rearrange("p k a c n -> p (k a c n)"), st_ps[slot][0:HKEYS, :], ACT.Exp).then_inc(exp_done, 1)

            for half in range(2):
                load(0, half)
            read_q(0, 3)
            for i in range(3):
                read_v(0, 0, i, 4 + i)
            read_q(1, 10)
            act.wait_ge(win_ready, 1)
            load(1, 0)
            with act.Fori(0, NHB) as hb:
                for half in range(2):
                    G = hb * 2 + half
                    for b in range(B):
                        U = G * B + b
                        for s in range(3):
                            exps(U * 3 + s, (b + s) % 2)
                            if s < len(USES[b]):
                                kind, i = USES[b][s]
                                if kind == "v":
                                    read_v(G + 1, 1 - half, i, use_number(G, b, s + 1))
                                if kind == "q":
                                    read_q(G + 2, use_number(G, b, s + 1))
                    act.wait_ge(win_ready, G + 2)
                    load(hb + (1 + half), 1 - half)

        @block.vector
        def _(dve):
            dve.memset(pv_ps[:, :], 0.0).then_inc(pv_zero, 1)
            n = instance_stats(dve, x_img, stats, mv[:, :], dve_prep, 0)
            dve.wait_ge(std_ready, 1)
            dve.wait_ge(dve_prep, n)
            dve.reciprocal(rstd[:, :], std[:, :]).then_inc(pads_mean, 1)
            dve.wait_ge(pads_mean, 1)
            dve.scalar_tensor_tensor(out=shift[:, :], in0=mv[:, 0:1], scalar=-1.0, in1=rstd[:, :],
                                     op0=ALU.mult, op1=ALU.mult).then_inc(pads_mean, 1)
            for rows in (slice(0, HALO), slice(HALO + H, XROWS)):
                dve.tensor_scalar(x[:, rows, :], x[:, rows, :], 0.0, mv[:, 0:1], ALU.mult, ALU.add).then_inc(pads_mean, 1)
            dve.wait_ge(consts_in, 16 * 16)
            dve.sem_inc(s_read, 2)

            def read_k(G, i, n):
                dve.wait_ge(misc_done, n + 1)
                if i == 0:
                    dve.wait_ge(k_split, G)
                dve.tensor_tensor(k32[:, 2 * i:2 * i + 2, :], misc_ps[:, 0:2 * KEYS].rearrange("p (k n) -> p k n", n=KEYS),
                                  relb[:, :, :].rearrange("p i j -> p (i j)").unsqueeze(1).to_broadcast([P, 2, KEYS]),
                                  ALU.add).then_inc(k32_ready, 1)
                dve.wait_ge(k32_ready, 3 * G + i + 1)
                dve.sem_inc(misc_read, 1)

            def row_max(U, par, j):
                f = U * NFILL + j
                dve.wait_ge(s_filled, f + 1)
                dve.tensor_reduce(mx[:, par, j // 3, 2 * (j % 3):2 * (j % 3) + 2],
                                  s_ps[j % 2][:, 0:2 * KEYS].rearrange("p (k n) -> p k n", n=KEYS), AX.X, ALU.max).then_inc(s_read, 1)

            def split_max(U, par, n, b_last, placed):
                dve.wait_ge(misc_done, n + 1)
                if placed is not None:
                    dve.wait_ge(m_placed[b_last], placed)
                src = misc_ps[0:2 * NB, 0:P]
                dve.tensor_scalar(mparts[:, par, 0, :], src, -1.0, None, ALU.mult).then_inc(m_split, 1)
                dve.wait_ge(m_split, 2 * U + 1)
                dve.scalar_tensor_tensor(out=mparts[:, par, 1, :], in0=src, scalar=-1.0, in1=mparts[:, par, 0, :],
                                         op0=ALU.mult, op1=ALU.subtract).then_inc(m_split, 1)
                dve.wait_ge(m_split, 2 * U + 2)
                dve.sem_inc(misc_read, 1)

            def read_sums(G, U, half, b):
                dve.wait_ge(misc_done, G * MISC + EARLY)
                dve.wait_ge(pv_done, U * 3 + 4)
                dve.tensor_copy(osb[:, half, b, :].rearrange("p (i k j) -> p k i j", i=BLOCK, j=BLOCK),
                                pv_ps[:, 0:NB * QS].rearrange("p (k i j) -> p k i j", i=BLOCK, j=BLOCK)).then_inc(pv_read, 1)

            def add_attention(hb, G, half, i, n):
                N = BLOCK * NB * BLOCK // 2
                dve.wait_ge(misc_done, n + 1)
                if i == 0:
                    dve.wait_ge(strip_ready, G + 4 - half)
                k = G * 2 + i
                dve.reciprocal(quot[:, :], misc_ps[:, N:2 * N]).then_inc(recip_done, 1)
                dve.wait_ge(recip_done, k + 1)
                dve.tensor_tensor(quot[:, :], quot[:, :], misc_ps[:, 0:N], ALU.mult).then_inc(quot_done, 1)
                dve.wait_ge(quot_done, k + 1)
                dve.sem_inc(misc_read, 1)
                rows = x_img[:, bass.ds(hb * BLOCK + i * (BLOCK // 2), BLOCK // 2), NB * BLOCK * half:NB * BLOCK * (half + 1)]
                dve.tensor_tensor(rows, quot[:, :].rearrange("p (i c) -> p i c", i=BLOCK // 2), rows, ALU.add).then_inc(x_added, 1)
                dve.wait_ge(x_added, k + 1)

            for i in range(3):
                read_k(0, i, i)
            for i in range(3):
                read_k(1, i, 7 + i)
            for U in range(2):
                for j in range(NFILL):
                    row_max(U, U, j)
            split_max(0, 0, 11, None, None)

            def body(hb, first=False):
                for half in range(2):
                    G = hb * 2 + half
                    for b in range(B):
                        U = G * B + b
                        for s in range(3):
                            row_max(U + 2, b % 2, 2 * s)
                            row_max(U + 2, b % 2, 2 * s + 1)
                            if s == 0:
                                split_max(U + 1, (b + 1) % 2, use_number(G, b, 0), (b + 3) % B,
                                          G * 32 + 32 * (b > 0))
                            if s < len(USES[b]):
                                (kind, i), n = USES[b][s], use_number(G, b, s + 1)
                                if kind == "k":
                                    read_k(G + 2, i, n)
                                elif kind == "o" and first and half == 0:
                                    dve.wait_ge(misc_done, n + 1)
                                    dve.sem_inc(misc_read, 1)
                                elif kind == "o":
                                    add_attention(hb - (1 - half), G - 1, 1 - half, i, n)
                        read_sums(G, U, half, b)

            body(0, first=True)
            with dve.Fori(1, NHB) as hb:
                body(hb)
            for i in range(2):
                add_attention(NHB - 1, 2 * NHB - 1, 1, i, 2 * NHB * MISC + EARLY + i)

        @block.tensor
        def _(pe):
            pe.wait_ge(consts_in, 16 * 16)
            pe.wait_ge(fills_set, 4)
            pe.wait_ge(pv_zero, 1)
            pe.sem_inc(pv_done, 1)

            def use(kind, half, i, n):
                pe.wait_ge(misc_read, n + 1)
                if kind == "v":
                    for t in range(4):
                        blk, chunk = (4 * i + t) // 2, t % 2
                        mm = pe.matmul(misc_ps[0:HKEYS, P * t:P * (t + 1)], xwin[:, half, blk, HKEYS * chunk:HKEYS * (chunk + 1)],
                                       wv[:, :], start=True, stop=True)
                elif kind == "o":
                    N = BLOCK * NB * BLOCK // 2
                    for k in range(2):
                        for b in range(B):
                            mm = pe.matmul(misc_ps[C * b:C * (b + 1), N * k:N * (k + 1)], hrows[:, k, :],
                                           osb[:, half, b, N * i:N * (i + 1)], start=True, stop=True)
                elif kind == "k":
                    mm = pe.matmul(misc_ps[:, 0:2 * KEYS], wk[:, :], xwin[:, half, 2 * i:2 * i + 2, :], start=True, stop=True)
                else:
                    for blk in range(NB):
                        mm = pe.matmul(misc_ps[:, QS * blk:QS * (blk + 1)], wq[:, :],
                                       strip[:, half, HALO:HALO + BLOCK, HALO + BLOCK * blk:HALO + BLOCK * (blk + 1)],
                                       start=True, stop=True)
                mm.then_inc(misc_done, 1)

            def maxima(U, par, n):
                pe.wait_ge(misc_read, n + 1)
                pe.wait_ge(s_read, U * NFILL + NFILL + 2)
                pe.transpose(misc_ps[0:2 * NB, 0:P], mx[:, par].rearrange("p a k -> p (a k)"), ident[:, :]).then_inc(misc_done, 1)

            def fill(U, half, b, j, uses):
                if j == 0 and b % 2 == 0:
                    pe.wait_ge(stacked[half][b // 2], 16 * LOADS * uses)
                f = U * NFILL + j
                pe.wait_ge(s_read, f + 1)
                for k in range(2):
                    blk = 2 * (j % 3) + k
                    mm = pe.matmul(s_ps[j % 2][:, KEYS * k:KEYS * (k + 1)],
                                   qst[0:ROWS, half, b // 2, b % 2, j // 3, blk].rearrange("p s q -> p (s q)"),
                                   kst[0:ROWS, half, b // 2, b % 2, j // 3, blk, :], start=True, stop=True)
                mm.then_inc(s_filled, 1)

            def turned_scores(st, slot, half, b, s, placed):
                if placed is not None:
                    pe.wait_ge(m_placed[b], placed)
                pe.wait_ge(exp_done, st)
                for k in range(2):
                    blk = 2 * s + k
                    for pair in range(2):
                        for chunk in range(2):
                            at = 512 * k + P * (2 * pair + chunk)
                            mm = pe.matmul(st_ps[slot][0:HKEYS, at:at + P],
                                           kst[0:ROWS + 2, half, b // 2, b % 2, pair, blk, HKEYS * chunk:HKEYS * (chunk + 1)],
                                           qst[0:ROWS + 2, half, b // 2, b % 2, pair, blk].rearrange("p s q -> p (s q)"), start=True, stop=True)
                mm.then_inc(st_done, 1)

            def sums(G, U, half, b, s, slot):
                if s == 0:
                    pe.wait_ge(v_ready, 3 * G + 3)
                    pe.wait_ge(pv_read, U)
                pe.wait_ge(exp_done, U * 3 + s + 2)
                for k in range(2):
                    blk = 2 * s + k
                    for chunk in range(2):
                        for h in range(HEADS):
                            mm = pe.matmul(pv_ps[32 * h:32 * h + 2 * D, QS * blk:QS * (blk + 1)],
                                           v[:, half, 2 * blk + chunk, b, h, :],
                                           pt[:, slot, k, h // 2, chunk, QS * (h % 2):QS * (h % 2 + 1)],
                                           start=(chunk == 0), stop=(chunk == 1))
                mm.then_inc(pv_done, 1)

            for half in range(2):
                pe.wait_ge(win_ready, half + 1)
                for i in range(3):
                    use("k", half, i, 7 * half + i)
                use("q", half, 0, 7 * half + 3)
                if half == 0:
                    for i in range(3):
                        use("v", 0, i, 4 + i)
            for U in range(2):
                for j in range(NFILL):
                    fill(U, 0, U, j, 1)
            maxima(0, 0, 11)
            turned_scores(0, 0, 0, 0, 0, 32)

            with pe.Fori(0, NHB) as hb:
                for half in range(2):
                    G = hb * 2 + half
                    for b in range(B):
                        U = G * B + b
                        for s in range(3):
                            later = half + (b + 2) // B
                            for j in (2 * s, 2 * s + 1):
                                fill(U + 2, later % 2, (b + 2) % B, j, hb + (1 + later // 2))
                            if s == 0:
                                maxima(U + 1, (b + 1) % 2, use_number(G, b, 0))
                            if s < 2:
                                turned_scores(U * 3 + s + 1, (b + s + 1) % 2, half, b, s + 1, None)
                            else:
                                turned_scores(U * 3 + 3, (b + 1) % 2, (half + (b + 1) // B) % 2, (b + 1) % B, 0,
                                              G * 32 + 32 * (1 + (b + 1) // B))
                            if s < len(USES[b]):
                                kind, i = USES[b][s]
                                if kind == "k" and i == 0:
                                    pe.wait_ge(win_ready, G + 3)
                                if kind == "o" and i == 0:
                                    pe.wait_ge(pv_read, G * B)
                                use(kind, 1 - half if kind in "vo" else half, i, use_number(G, b, s + 1))
                            sums(G, U, half, b, s, (b + s) % 2)
            pe.wait_ge(pv_read, 2 * NHB * B)
            for i in range(2):
                use("o", 1, i, 2 * NHB * MISC + EARLY + i)


def lstm_layer(nc, x, w_ih_rep, w_hh_t, bias_ih, bias_hh, w_lin_t, b_lin_rep):
    HID = 128
    STEPS = 4
    CHUNK = 24
    NCH = W // CHUNK
    ctx = ExitStack()
    with ctx:
        def sb(name, shape, dt=F32):
            return ctx.enter_context(nc.sbuf_tensor("l1_" + name, shape, dt))

        def sem(name):
            return ctx.enter_context(nc.semaphore("l1_" + name))

        stats = sb("stats", [P, 6 * (H * W // 512)])
        mv = sb("mv", [P, 2])
        std = sb("std", [P, 1])
        rstd = sb("rstd", [P, 1])
        eps = sb("eps", [P, 1])
        xn = sb("xn", [P, 2, CHUNK, H])
        part = sb("part", [P, 2, 3, CHUNK, H], BF16)
        xs = sb("xs", [P, B, W, H], BF16)
        wih = sb("wih", [P, 4 * HID])
        wp = sb("wp", [P, 3, 4 * HID], BF16)
        wa = sb("wa", [P, 4 * HID], BF16)
        wb = sb("wb", [P, 4 * HID], BF16)
        whh = sb("whh", [HID, 4 * HID])
        bi = sb("bi", [HID, 4])
        bh = sb("bh", [HID, 4])
        bias = sb("bias", [HID, 4])
        wlin = sb("wlin", [HID, C])
        blin = sb("blin", [P, 1])
        gate = sb("gate", [HID, 2, 4, 2 * H])
        prod = sb("prod", [HID, 2, 2, 2 * H])
        cell = sb("cell", [HID, 2, 2 * H])
        tcell = sb("tcell", [HID, 2, 2 * H])
        hid = sb("hid", [HID, 2, 2, 2 * H])
        gates_ps = [ctx.enter_context(nc.psum_tensor(f"l1_g{i}", [P, 512], F32)) for i in range(6)]
        lin_ps = [ctx.enter_context(nc.psum_tensor(f"l1_l{i}", [P, 512], F32)) for i in range(2)]

        weights_in = sem("weights_in")
        dve_prep = sem("dve_prep")
        eps_set = sem("eps_set")
        std_ready = sem("std_ready")
        part_cast = sem("part_cast")
        part_ready = sem("part_ready")
        stacked = [sem(f"stacked{i}") for i in range(NCH)]
        state_zero = sem("state_zero")
        gates_done = [sem(f"gates_done{c}") for c in range(2)]
        gates_act = [sem(f"gates_act{c}") for c in range(2)]
        prods_done = [sem(f"prods_done{c}") for c in range(2)]
        cell_done = [sem(f"cell_done{c}") for c in range(2)]
        tanh_done = [sem(f"tanh_done{c}") for c in range(2)]
        hid_done = [sem(f"hid_done{c}") for c in range(2)]
        lin_done = sem("lin_done")
        lin_added = sem("lin_added")

        PREP = 19 + 1 + 2 * NCH + 11
        SLICE = [2, 0, 1, 3]
        FUNC = [ACT.Tanh, ACT.Sigmoid, ACT.Sigmoid, ACT.Sigmoid]
        x_img = x[:, HALO:HALO + H, :]

        def gate_ps(c, g):
            return gates_ps[3 * c + max(g - 1, 0)][:, (g == 1) * 2 * H:((g == 1) + 1) * 2 * H]

        block = ctx.enter_context(nc.Block())

        @block.sync
        def _(sp):
            for dst, src in ((wih, w_ih_rep), (whh, w_hh_t), (bi, bias_ih), (bh, bias_hh),
                             (wlin, w_lin_t), (blin, b_lin_rep)):
                sp.dma_start(dst[:, :], src).then_inc(weights_in, 16)
            for k in range(NCH):
                sp.wait_ge(part_ready, k + 1)
                for b in range(B):
                    for row, piece in enumerate((0, 1, 2, 0)):
                        sp.dma_start(xs[32 * row:32 * row + 32, b, CHUNK * k:CHUNK * (k + 1), :],
                                     part[32 * b:32 * b + 32, k % 2, piece, :, :]).then_inc(stacked[k], 16)
            for k in range(NCH):
                sp.wait_ge(stacked[k], 16 * 16)

        @block.gpsimd
        def _(pool):
            pool.memset(eps[:, :], GN_EPS).then_inc(eps_set, 1)
            pool.memset(cell[:, :, :], 0.0).then_inc(state_zero, 1)
            pool.memset(hid[:, :, :, :], 0.0).then_inc(state_zero, 1)

        @block.scalar
        def _(act):
            act.wait_ge(eps_set, 1)
            act.wait_ge(dve_prep, 19)
            act.activation(std[:, :], mv[:, 1:2], ACT.Sqrt, bias=eps[:, :]).then_inc(std_ready, 1)
            for k in range(NCH):
                act.wait_ge(dve_prep, 20 + 2 * k + 1)
                if k >= 2:
                    act.wait_ge(stacked[k - 2], 16 * 16)
                act.activation(part[:, k % 2, 0], xn[:, k % 2], ACT.Copy).then_inc(part_cast, 1)
                act.wait_ge(dve_prep, 20 + 2 * k + 2)
                act.activation(part[:, k % 2, 1], xn[:, k % 2], ACT.Copy).then_inc(part_cast, 1)
            act.wait_ge(dve_prep, PREP)

            def gates(i, c):
                for g in range(4):
                    act.wait_ge(gates_done[c], 4 * i + max(g + 1, 2))
                    if g == 0:
                        act.wait_ge(hid_done[c], i + 1)
                    act.activation(gate[:, c, g, :], gate_ps(c, g), FUNC[g],
                                   bias=bias[:, SLICE[g]:SLICE[g] + 1]).then_inc(gates_act[c], 1)

            def cells(i, c):
                act.wait_ge(cell_done[c], i + 1)
                act.activation(tcell[:, c, :], cell[:, c, :], ACT.Tanh).then_inc(tanh_done[c], 1)

            with act.Fori(0, W, STEPS) as t:
                for s in range(STEPS):
                    for c in range(2):
                        gates(t + s, c)
                        cells(t + s, c)

        @block.vector
        def _(dve):
            n = instance_stats(dve, x_img, stats, mv[:, :], dve_prep, 0)
            dve.wait_ge(std_ready, 1)
            dve.reciprocal(rstd[:, :], std[:, :]).then_inc(dve_prep, 1)
            n += 1
            dve.wait_ge(dve_prep, n)
            xt = x_img.rearrange("p f t -> p t f")
            for k in range(NCH):
                if k >= 2:
                    dve.wait_ge(part_ready, k - 1)
                dve.tensor_scalar(xn[:, k % 2], xt[:, CHUNK * k:CHUNK * (k + 1), :], mv[:, 0:1], rstd[:, 0:1],
                                  ALU.subtract, ALU.mult).then_inc(dve_prep, 1)
                n += 1
                dve.wait_ge(dve_prep, n)
                dve.wait_ge(part_cast, 2 * k + 1)
                dve.tensor_tensor(xn[:, k % 2], xn[:, k % 2], part[:, k % 2, 0], ALU.subtract).then_inc(dve_prep, 1)
                n += 1
                dve.wait_ge(dve_prep, n)
                dve.wait_ge(part_cast, 2 * k + 2)
                dve.tensor_tensor(part[:, k % 2, 2], xn[:, k % 2], part[:, k % 2, 1], ALU.subtract).then_inc(part_ready, 1)

            def then(ins):
                nonlocal n
                ins.then_inc(dve_prep, 1)
                n += 1
                dve.wait_ge(dve_prep, n)

            dve.wait_ge(weights_in, 96)
            then(dve.tensor_tensor(bias[:, :], bi[:, :], bh[:, :], ALU.add))
            then(dve.tensor_copy(wp[:, 0], wih[:, :]))
            then(dve.tensor_tensor(wih[:, :], wih[:, :], wp[:, 0], ALU.subtract))
            then(dve.tensor_copy(wp[:, 1], wih[:, :]))
            then(dve.tensor_tensor(wp[:, 2], wih[:, :], wp[:, 1], ALU.subtract))
            then(dve.tensor_copy(wa[0:96, :], wp[0:96, 0]))
            then(dve.tensor_copy(wa[96:128, :], wp[96:128, 1]))
            then(dve.tensor_copy(wb[0:32, :], wp[0:32, 2]))
            then(dve.tensor_copy(wb[32:64, :], wp[32:64, 1]))
            then(dve.tensor_copy(wb[64:96, :], wp[64:96, 1]))
            then(dve.memset(wb[96:128, :], 0.0))
            assert n == PREP
            dve.wait_ge(state_zero, 2)

            def cell_ops(i, c):
                dve.wait_ge(gates_act[c], 4 * i + 6)
                dve.tensor_tensor(prod[:, c, 0], gate[:, c, 0], gate[:, c, 1], ALU.mult).then_inc(prods_done[c], 1)
                dve.wait_ge(gates_act[c], 4 * i + 7)
                dve.tensor_tensor(prod[:, c, 1], gate[:, c, 2], cell[:, c], ALU.mult).then_inc(prods_done[c], 1)
                dve.wait_ge(prods_done[c], 2 * i + 2)
                dve.tensor_tensor(cell[:, c], prod[:, c, 0], prod[:, c, 1], ALU.add).then_inc(cell_done[c], 1)

            def hid_ops(i, c, s):
                dve.wait_ge(gates_act[c], 4 * i + 8)
                dve.wait_ge(tanh_done[c], i + 1)
                dve.tensor_tensor(hid[:, c, (s + 1) % 2], gate[:, c, 3], tcell[:, c], ALU.mult).then_inc(hid_done[c], 1)

            def add_linear(group, j):
                dve.wait_ge(lin_done, 2 * STEPS * (group + 1))
                cols = x_img[:, :, bass.ds(group * STEPS, STEPS)]
                ps = lin_ps[j][:, 0:STEPS * H].rearrange("p (t f) -> p f t", f=H)
                dve.scalar_tensor_tensor(out=cols, in0=ps, scalar=blin[:, 0:1], in1=cols,
                                         op0=ALU.add, op1=ALU.add).then_inc(lin_added, 1)

            def body(k, first=False):
                for j in range(2):
                    group = k * 2 + j
                    for s in range(STEPS):
                        for c in range(2):
                            cell_ops(group * STEPS + s, c)
                            hid_ops(group * STEPS + s, c, s)
                        if s == 1 and not (first and j == 0):
                            add_linear(group - 1, 1 - j)

            body(0, first=True)
            with dve.Fori(1, W // (2 * STEPS)) as k:
                body(k)
            add_linear(W // STEPS - 1, 1)

        @block.tensor
        def _(pe):
            for k in range(NCH):
                pe.wait_ge(stacked[k], 16 * 16)
            pe.wait_ge(dve_prep, PREP)
            pe.wait_ge(state_zero, 2)

            def step_gates(i, c, s):
                xin = xs[:, 2 * c:2 * c + 2, bass.ds(i, 1), :]
                for g in range(4):
                    w = slice(HID * SLICE[g], HID * (SLICE[g] + 1))
                    if g != 1:
                        pe.wait_ge(gates_act[c], 4 * i + max(g + 1, 2))
                    pe.matmul(gate_ps(c, g), wa[:, w], xin, start=True, stop=False)
                    pe.matmul(gate_ps(c, g), wb[:, w], xin, start=False, stop=False)
                    if g == 0:
                        pe.wait_ge(hid_done[c], i + 1)
                    pe.matmul(gate_ps(c, g), whh[:, w], hid[:, c, s % 2], start=False, stop=True).then_inc(gates_done[c], 1)

            def linear(i, c, s, j):
                pe.wait_ge(hid_done[c], i + 2)
                for b in (2 * c, 2 * c + 1):
                    mm = pe.matmul(lin_ps[j][32 * b:32 * b + 32, s * H:(s + 1) * H], wlin[:, :],
                                   hid[:, c, (s + 1) % 2, (b % 2) * H:(b % 2 + 1) * H], start=True, stop=True)
                mm.then_inc(lin_done, 1)

            def body(k, first=False):
                for j in range(2):
                    for s in range(STEPS):
                        i = (k * 2 + j) * STEPS + s
                        step_gates(i, 0, s)
                        if s > 0:
                            linear(i - 1, 1, s - 1, j)
                        elif not (first and j == 0):
                            linear(i - 1, 1, STEPS - 1, 1 - j)
                        step_gates(i, 1, s)
                        if s == 0:
                            pe.wait_ge(lin_added, k * 2 + j + 1)
                        linear(i, 0, s, j)

            pe.sem_inc(lin_added, 2)
            for c in range(2):
                pe.sem_inc(hid_done[c], 1)
                pe.sem_inc(gates_act[c], 4)
            body(0, first=True)
            with pe.Fori(1, W // (2 * STEPS)) as k:
                body(k)
            linear(W - 1, 1, STEPS - 1, 1)


NTAP = 9
PADW = W + 2
NOFF = 2 * NTAP
NOUT = NOFF + NTAP
GROUP = 4
TILEW = 32
NCOL = W // TILEW
NGROUP = H // GROUP
NPREP = NGROUP + 2
NTILE = NPREP * NCOL
TABROWS = GROUP * NPREP
STRIDE = TABROWS * PADW


def deformable_layer(nc, x, conv_w, pix_bias, pix_base, group_step, batch_base, identity, out_w, table):
    ROWS = GROUP + 2
    SW = PADW + 1
    TURNS = GROUP + 1
    COPIES = 2 * GROUP
    STEPS = 14
    PREP = 18 + 1 + 1 + 1
    ctx = ExitStack()
    with ctx:
        def sb(name, shape, dt=F32):
            return ctx.enter_context(nc.sbuf_tensor("l2_" + name, shape, dt))

        def sem(name):
            return ctx.enter_context(nc.semaphore("l2_" + name))

        stats = sb("stats", [P, 6 * (H * W // 512)])
        mv = sb("mv", [P, 2])
        std = sb("std", [P, 1])
        rstd = sb("rstd", [P, 1])
        shift = sb("shift", [P, 1])
        eps = sb("eps", [P, 1])
        ident = sb("ident", [P, P])
        cw = sb("cw", [P, NTAP, B * NOUT])
        pbias = sb("pbias", [P, NOUT])
        base = sb("base", [P, NCOL, NOFF])
        step4 = sb("step4", [P, NCOL, NOFF])
        bbase = sb("bbase", [P, B, NTAP])
        wout = sb("wout", [3 * C, 3, C])
        strip = sb("strip", [P, 2, ROWS, SW])
        tab = sb("tab", [PADW, 2, GROUP, B, 4 * C])
        ot = sb("ot", [B * NOUT, NCOL, P])
        raw = sb("raw", [P, NCOL, B, NOUT])
        pos = sb("pos", [P, NCOL, B, NOFF])
        posi = sb("posi", [P, NCOL, B, NOFF], I32)
        flo = sb("flo", [P, NCOL, B, NOFF])
        gt = sb("gt", [P, NCOL, B, NOFF])
        frac = sb("frac", [P, NCOL, B, NOFF])
        rest = sb("rest", [P, NCOL, B, NOFF])
        mask = sb("mask", [P, NCOL, B, NTAP])
        mx0 = sb("mx0", [P, NCOL, B, NTAP])
        mx1 = sb("mx1", [P, NCOL, B, NTAP])
        idxf = sb("idxf", [P, NCOL, B, NTAP])
        index = sb("index", [P, NTILE, B * NTAP], I32)
        weight = sb("weight", [P, NTILE, B, NTAP, 4])
        tidx = sb("tidx", [P, NCOL, B * NTAP], I32)
        RING = B
        got = sb("got", [P, RING, NTAP, 4 * C])
        red = sb("red", [P, 2, NTAP, 2 * C])
        samp = sb("samp", [P, 2, NTAP, C])
        sampt = sb("sampt", [3 * C, 2, 3, P])

        def ps(name):
            return ctx.enter_context(nc.psum_tensor("l2_" + name, [P, 512], F32))

        off_ps = ps("off")
        offt_ps = ps("offt")
        tab_ps = [ps(f"tab{i}") for i in range(2)]
        samp_ps = [ps(f"samp{i}") for i in range(2)]
        out_ps = [ps("out0"), ps("out1"), off_ps]

        consts_in = sem("consts_in")
        cw_zero = sem("cw_zero")
        pool_passed = sem("pool_passed")
        dve_prep = sem("dve_prep")
        pads_zero = sem("pads_zero")
        pads_mean = sem("pads_mean")
        eps_set = sem("eps_set")
        std_ready = sem("std_ready")
        strip_ready = sem("strip_ready")
        off_done = sem("off_done")
        off_out = sem("off_out")
        offt_done = sem("offt_done")
        raw_done = sem("raw_done")
        mask_done = sem("mask_done")
        chain = sem("chain")
        tab_turned = sem("tab_turned")
        tab_copied = sem("tab_copied")
        tab_stored = [sem(f"tab_stored{i}") for i in range(2)]
        tidx_ready = sem("tidx_ready")
        gathered = [sem(f"gathered{i}") for i in range(RING)]
        weighted = sem("weighted")
        reduced = sem("reduced")
        summed = sem("summed")
        x_added = sem("x_added")
        samp_turned = sem("samp_turned")
        sampt_ready = sem("sampt_ready")
        convolved = sem("convolved")

        x_img = x[:, HALO:HALO + H, :]
        x_pad = x[:, HALO - 1:XROWS, :]

        block = ctx.enter_context(nc.Block())

        @block.sync
        def _(sp):
            sp.wait_ge(cw_zero, 1)
            for b in range(B):
                sp.dma_start(cw[C * b:C * (b + 1), :, NOUT * b:NOUT * (b + 1)],
                             conv_w.rearrange("c (t o) -> c t o", t=NTAP)).then_inc(consts_in, 16)
            for dst, src in ((pbias[:, :], pix_bias), (base[:, :, :], pix_base.rearrange("p (c n) -> p c n", c=NCOL)),
                             (step4[:, :, :], group_step.rearrange("p (c n) -> p c n", c=NCOL)),
                             (bbase[:, :, :], batch_base.rearrange("p (b n) -> p b n", b=B)),
                             (ident[:, :], identity), (wout[:, :, :], out_w.rearrange("k (g o) -> k g o", g=3))):
                sp.dma_start(dst, src).then_inc(consts_in, 16)

            def store_table(g, j):
                sp.wait_ge(tab_copied, COPIES * (g + 2))
                for b in range(B):
                    sp.dma_start(table[b].rearrange("(r s) k -> s r k", s=PADW)[:, bass.ds(g * GROUP, GROUP), :],
                                 tab[:, j, :, b, :]).then_inc(tab_stored[j], 16)

            with sp.Fori(0, NPREP // 2) as g2:
                store_table(g2 * 2, 0)
                store_table(g2 * 2 + 1, 1)

        @block.gpsimd
        def _(pool):
            pool.memset(cw[:, :, :], 0.0).then_inc(cw_zero, 1)
            pool.memset(eps[:, :], GN_EPS).then_inc(eps_set, 1)
            pool.memset(strip[:, :, :, :], 0.0).then_inc(pads_zero, 1)
            for j in range(2):
                pool.wait_ge(tab_stored[j], 16 * B * (NPREP // 2 + 1))
            rows = table.rearrange("b r k -> (b r) k")

            with pool.Fori(0, NGROUP) as g:
                for c in range(NCOL):
                    t = g * NCOL + c
                    wait_apart(pool, tidx_ready, t + 1, pool_passed)
                    for b in range(B):
                        wait_apart(pool, reduced, t * B + b + 1, pool_passed)
                        for n in range(NTAP):
                            at = tidx[:, c, b * NTAP + n:b * NTAP + n + 1].bitcast(U32)
                            pool.indirect_dma_start(
                                out=got[:, b, n, :], out_offset=None, in_=rows,
                                in_offset=bass.IndirectOffsetOnAxis(ap=at, axis=0)).then_inc(gathered[b], 16)

        @block.scalar
        def _(act):
            act.wait_ge(eps_set, 1)
            act.wait_ge(dve_prep, 19)
            act.activation(std[:, :], mv[:, 1:2], ACT.Sqrt, bias=eps[:, :]).then_inc(std_ready, 1)
            act.wait_ge(dve_prep, PREP)
            act.wait_ge(pads_zero, 1)
            act.wait_ge(pads_mean, 2)
            act.sem_inc(off_out, 1)
            act.sem_inc(tab_copied, COPIES)
            for j in range(2):
                act.sem_inc(tab_stored[j], 16 * B)

            def prepare(g, j):
                act.wait_ge(tab_turned, TURNS * g)
                act.activation(strip[:, j, :, 1:1 + W], x_pad[:, bass.ds(g * GROUP, ROWS), :], ACT.Identity,
                               bias=shift[:, 0:1], scale=rstd[:, 0:1]).then_inc(strip_ready, 1)

            def table_rows(g2, g, j):
                act.wait_ge(tab_stored[j], 16 * B * (g2 + 1))
                for r in range(TURNS):
                    act.wait_ge(tab_turned, TURNS * (g + 1) + r + 1)
                    src = tab_ps[(j * TURNS + r) % 2][0:PADW, 0:2 * P].rearrange("p (s b c) -> p b s c", s=2, b=B)
                    if r > 0:
                        act.activation(tab[:, j, r - 1, :, 2 * C:4 * C].rearrange("p b (s c) -> p b s c", s=2), src,
                                       ACT.Copy).then_inc(tab_copied, 1)
                    if r < GROUP:
                        act.activation(tab[:, j, r, :, 0:2 * C].rearrange("p b (s c) -> p b s c", s=2), src,
                                       ACT.Copy).then_inc(tab_copied, 1)

            def offsets(g):
                act.wait_ge(off_done, g + 1)
                act.wait_ge(offt_done, g + 1)
                act.activation(ot[:, :, :], off_ps[0:B * NOUT, 0:NCOL * P].rearrange("p (c n) -> p c n", n=P),
                               ACT.Copy).then_inc(off_out, 1)

            def masks(g):
                act.wait_ge(raw_done, g + 2)
                act.wait_ge(chain, STEPS * g + 1)
                act.activation(mask[:, :, :, :], raw[:, :, :, NOFF:NOUT], ACT.Sigmoid).then_inc(mask_done, 1)

            prepare(0, 0)
            with act.Fori(0, NPREP // 2) as g2:
                for j in range(2):
                    g = g2 * 2 + j
                    prepare(g + 1, 1 - j)
                    offsets(g)
                    table_rows(g2, g, j)
                    masks(g)

            with act.Fori(0, NGROUP) as g:
                for c in range(NCOL):
                    for b in range(B):
                        u = (g * NCOL + c) * B + b
                        act.wait_ge(samp_turned, u + 1)
                        act.wait_ge(convolved, u + 1)
                        act.activation(sampt[:, b % 2, :, :], samp_ps[b % 2][0:3 * C, 0:3 * P].rearrange("p (g n) -> p g n", g=3),
                                       ACT.Copy).then_inc(sampt_ready, 1)

        @block.vector
        def _(dve):
            n = instance_stats(dve, x_img, stats, mv[:, :], dve_prep, 0)
            dve.wait_ge(std_ready, 1)
            dve.reciprocal(rstd[:, :], std[:, :]).then_inc(dve_prep, 1)
            dve.wait_ge(dve_prep, n + 1)
            dve.scalar_tensor_tensor(out=shift[:, :], in0=mv[:, 0:1], scalar=-1.0, in1=rstd[:, :],
                                     op0=ALU.mult, op1=ALU.mult).then_inc(dve_prep, 1)
            dve.tensor_scalar(x[:, 0:HALO, :], x[:, 0:HALO, :], 0.0, mv[:, 0:1], ALU.mult, ALU.add).then_inc(pads_mean, 1)
            dve.tensor_scalar(x[:, HALO + H:XROWS, :], x[:, HALO + H:XROWS, :], 0.0, mv[:, 0:1],
                              ALU.mult, ALU.add).then_inc(pads_mean, 1)
            dve.wait_ge(consts_in, 16 * 10)
            dve.sem_inc(raw_done, 1)
            dve.sem_inc(chain, 1)

            def both(one):
                return one.unsqueeze(2).to_broadcast([P, NCOL, B, one.shape[2]])

            def group_math(g):
                start = g * STEPS + 1
                k = 0

                def step(ins):
                    nonlocal k
                    ins.then_inc(chain, 1)
                    k += 1
                    dve.wait_ge(chain, start + k)

                dve.wait_ge(offt_done, g + 2)
                turned = offt_ps[:, 0:NCOL * P].rearrange("p (c n) -> p c n", n=P)[:, :, 0:B * NOUT].rearrange(
                    "p c (b o) -> p c b o", b=B)
                bias = pbias[:, :].unsqueeze(1).unsqueeze(1).to_broadcast([P, NCOL, B, NOUT])
                dve.tensor_tensor(raw[:, :, :, :], turned, bias, ALU.add).then_inc(raw_done, 1)
                dve.wait_ge(raw_done, g + 2)
                step(dve.tensor_tensor(pos[:, :, :, :], raw[:, :, :, 0:NOFF], both(base[:, :, :]), ALU.add))
                step(dve.tensor_scalar(pos[:, :, :, :], pos[:, :, :, :], 0.0, float(PADW - 1), ALU.max, ALU.min))
                step(dve.tensor_copy(posi[:, :, :, :], pos[:, :, :, :]))
                step(dve.tensor_copy(flo[:, :, :, :], posi[:, :, :, :]))
                step(dve.tensor_tensor(gt[:, :, :, :], flo[:, :, :, :], pos[:, :, :, :], ALU.is_gt))
                step(dve.tensor_tensor(flo[:, :, :, :], flo[:, :, :, :], gt[:, :, :, :], ALU.subtract))
                step(dve.tensor_tensor(frac[:, :, :, :], pos[:, :, :, :], flo[:, :, :, :], ALU.subtract))
                step(dve.tensor_scalar(rest[:, :, :, :], frac[:, :, :, :], -1.0, 1.0, ALU.mult, ALU.add))
                step(dve.scalar_tensor_tensor(out=idxf[:, :, :, :], in0=flo[:, :, :, 0:NTAP], scalar=float(PADW),
                                              in1=flo[:, :, :, NTAP:NOFF], op0=ALU.mult, op1=ALU.add))
                tiles = bass.ds(g * NCOL, NCOL)
                step(dve.tensor_tensor(index[:, tiles, :].rearrange("p c (b n) -> p c b n", b=B), idxf[:, :, :, :],
                                       bbase[:, :, :].unsqueeze(1).to_broadcast([P, NCOL, B, NTAP]), ALU.add))
                dve.wait_ge(mask_done, g + 1)
                step(dve.tensor_tensor(mx0[:, :, :, :], mask[:, :, :, :], rest[:, :, :, 0:NTAP], ALU.mult))
                step(dve.tensor_tensor(mx1[:, :, :, :], mask[:, :, :, :], frac[:, :, :, 0:NTAP], ALU.mult))
                for q, (mx, fy) in enumerate(((mx0, rest), (mx0, frac), (mx1, rest), (mx1, frac))):
                    for c in range(NCOL):
                        ins = dve.tensor_tensor(weight[:, bass.ds(g * NCOL + c, 1), :, :, q].rearrange("p o b n -> p (o b) n"),
                                                mx[:, c], fy[:, c, :, NTAP:NOFF], ALU.mult)
                step(ins)
                step(dve.tensor_tensor(base[:, :, :], base[:, :, :], step4[:, :, :], ALU.add))
                assert k == STEPS

            with dve.Fori(0, NPREP) as g:
                group_math(g)

            dve.sem_inc(reduced, RING)
            done = STEPS * NPREP + 1

            def tile_index(t, c):
                dve.tensor_copy(tidx[:, c, :], index[:, bass.ds(t, 1), :].rearrange("p o n -> p (o n)")).then_inc(tidx_ready, 1)

            def unit(t, c, b):
                u = t * B + b
                dve.wait_ge(gathered[b], 16 * NTAP * (t + 1))
                corners = got[:, b, :, :].rearrange("p n (k c) -> p (n k) c", c=C)
                w = weight[:, bass.ds(t, 1), b, :, :].rearrange("p o n k -> p (o n k)").unsqueeze(2).to_broadcast([P, NTAP * 4, C])
                dve.tensor_tensor(corners, corners, w, ALU.mult).then_inc(weighted, 1)
                dve.wait_ge(weighted, u + 1)
                dve.tensor_tensor(red[:, b % 2], got[:, b, :, 0:2 * C], got[:, b, :, 2 * C:4 * C], ALU.add).then_inc(reduced, 1)
                dve.wait_ge(reduced, u + 1 + RING)
                dve.tensor_tensor(samp[:, b % 2], red[:, b % 2, :, 0:C], red[:, b % 2, :, C:2 * C], ALU.add).then_inc(summed, 1)

            tile_index(0, 0)
            with dve.Fori(0, NGROUP) as g:
                for c in range(NCOL):
                    t = g * NCOL + c
                    tile_index(t + 1, (c + 1) % NCOL)
                    for b in range(B):
                        if b >= 2:
                            dve.wait_ge(samp_turned, t * B + b - 1)
                        unit(t, c, b)
                    dve.wait_ge(convolved, t * B + B + 2)
                    rows = x_img[:, bass.ds(g * GROUP, GROUP), TILEW * c:TILEW * (c + 1)]
                    dve.tensor_tensor(rows, out_ps[c][:, 0:P].rearrange("p (h w) -> p h w", w=TILEW), rows,
                                      ALU.add).then_inc(x_added, 1)

        @block.tensor
        def _(pe):
            pe.wait_ge(consts_in, 16 * 10)
            pe.wait_ge(dve_prep, PREP)
            pe.sem_inc(tab_turned, TURNS)
            pe.sem_inc(offt_done, 1)

            def group(g, j):
                pe.wait_ge(strip_ready, g + 1)
                pe.wait_ge(off_out, g + 1)
                dst = off_ps[0:B * NOUT, 0:NCOL * P]
                for tap in range(NTAP):
                    dy, dx = tap // 3, tap % 3
                    src = strip[:, j, dy:dy + GROUP, dx:dx + W].rearrange("p h (c w) -> p c h w", w=TILEW)
                    mm = pe.matmul(dst, cw[:, tap, :], src, start=(tap == 0), stop=(tap == NTAP - 1))
                mm.then_inc(off_done, 1)
                for r in range(TURNS):
                    pe.wait_ge(tab_copied, COPIES * g + (7, 8, 9, 11, 13)[r])
                    for s in range(2):
                        mm = pe.transpose(tab_ps[(j * TURNS + r) % 2][0:PADW, P * s:P * (s + 1)],
                                          strip[:, j, r, s:s + PADW], ident[:, :])
                    mm.then_inc(tab_turned, 1)
                pe.wait_ge(off_out, g + 2)
                pe.wait_ge(raw_done, g + 1)
                for c in range(NCOL):
                    mm = pe.transpose(offt_ps[:, P * c:P * c + B * NOUT], ot[:, c, :], ident[0:B * NOUT, 0:B * NOUT])
                mm.then_inc(offt_done, 1)

            with pe.Fori(0, NPREP // 2) as g2:
                group(g2 * 2, 0)
                group(g2 * 2 + 1, 1)

            pe.sem_inc(convolved, 2)
            with pe.Fori(0, NGROUP) as g:
                for c in range(NCOL):
                    t = g * NCOL + c
                    for b in range(B):
                        u = t * B + b
                        pe.wait_ge(summed, u + 1)
                        for q in range(3):
                            mm = pe.transpose(samp_ps[b % 2][0:3 * C, P * q:P * (q + 1)],
                                              samp[:, b % 2, 3 * q:3 * q + 3, :].rearrange("p n c -> p (n c)"), ident[:, :])
                        mm.then_inc(samp_turned, 1)
                        pe.wait_ge(sampt_ready, u + 1)
                        for q in range(3):
                            mm = pe.matmul(out_ps[c][C * b:C * (b + 1), 0:P], wout[:, q, :], sampt[:, b % 2, q, :],
                                           start=(q == 0), stop=(q == 2))
                        mm.then_inc(convolved, 1)


def block_transform_layer(nc, x, m_left, m_right, same_block, identity, out):
    BS = 8
    PAIR = 2 * BS
    NPAIR = W // PAIR
    NROW = H // BS
    FIRST = 4
    PREP = 18 + 1 + 1 + 1 + 2
    ctx = ExitStack()
    with ctx:
        def sb(name, shape, dt=F32):
            return ctx.enter_context(nc.sbuf_tensor("l3_" + name, shape, dt))

        def sem(name):
            return ctx.enter_context(nc.semaphore("l3_" + name))

        stats = sb("stats", [P, 6 * (H * W // 512)])
        mv = sb("mv", [P, 2])
        std = sb("std", [P, 1])
        rstd = sb("rstd", [P, 1])
        shift = sb("shift", [P, 1])
        eps = sb("eps", [P, 1])
        ml = sb("ml", [P, P])
        mr = sb("mr", [P, P])
        same = sb("same", [P, P])
        kron = sb("kron", [P, P])
        ident = sb("ident", [P, P])
        xr = sb("xr", [P, 2, NPAIR, P])
        xt = sb("xt", [P, 2, NPAIR, P])
        t_ps = [[ctx.enter_context(nc.psum_tensor(f"l3_t{j}{i}", [P, 512], F32)) for i in range(2)] for j in range(2)]
        o_ps = [[ctx.enter_context(nc.psum_tensor(f"l3_o{j}{i}", [P, 512], F32)) for i in range(2)] for j in range(2)]

        consts_in = sem("consts_in")
        dve_prep = sem("dve_prep")
        eps_set = sem("eps_set")
        std_ready = sem("std_ready")
        row_normed = sem("row_normed")
        row_turned = sem("row_turned")
        turned_out = sem("turned_out")
        row_multiplied = sem("row_multiplied")
        row_added = sem("row_added")
        stored = sem("stored")

        x_img = x[:, HALO:HALO + H, :]
        x_below = x[:, HALO:XROWS, :]
        out_rows = out.rearrange("b c h w -> (b c) h w")
        HALVES = ((0, FIRST), (FIRST, NPAIR))

        block = ctx.enter_context(nc.Block())

        @block.sync
        def _(sp):
            for dst, src in ((ml, m_left), (mr, m_right), (same, same_block), (ident, identity)):
                sp.dma_start(dst[:, :], src).then_inc(consts_in, 16)
            with sp.Fori(0, NROW) as r:
                sp.wait_ge(row_added, 2 * r + 6)
                sp.dma_start(out_rows[:, bass.ds(r * BS, BS), :], x_img[:, bass.ds(r * BS, BS), :]).then_inc(stored, 16)
            sp.wait_ge(stored, 16 * NROW)

        @block.gpsimd
        def _(pool):
            pool.memset(eps[:, :], GN_EPS).then_inc(eps_set, 1)

        @block.scalar
        def _(act):
            act.wait_ge(eps_set, 1)
            act.wait_ge(dve_prep, 19)
            act.activation(std[:, :], mv[:, 1:2], ACT.Sqrt, bias=eps[:, :]).then_inc(std_ready, 1)
            act.wait_ge(dve_prep, PREP)

            def normalise(r, j):
                act.wait_ge(row_turned, r + 1)
                rows = x_below[:, bass.ds(r * BS, BS), :].rearrange("p h (c w) -> p c h w", w=PAIR)
                act.activation(xr[:, j].rearrange("p c (h w) -> p c h w", w=PAIR), rows, ACT.Identity, bias=shift[:, 0:1],
                               scale=rstd[:, 0:1]).then_inc(row_normed, 1)

            def evacuate(r, j):
                act.wait_ge(row_turned, r + 3)
                act.wait_ge(row_multiplied, r + 1)
                for i, (a, b) in enumerate(HALVES):
                    act.activation(xt[:, j, a:b, :], t_ps[j][i][:, 0:P * (b - a)].rearrange("p (c n) -> p c n", n=P),
                                   ACT.Copy).then_inc(turned_out, 1)

            normalise(0, 0)
            with act.Fori(0, NROW // 2) as pair:
                r = pair * 2
                normalise(r + 1, 1)
                evacuate(r, 0)
                normalise(r + 2, 0)
                evacuate(r + 1, 1)

        @block.vector
        def _(dve):
            n = instance_stats(dve, x_img, stats, mv[:, :], dve_prep, 0)

            def then(ins):
                nonlocal n
                ins.then_inc(dve_prep, 1)
                n += 1
                dve.wait_ge(dve_prep, n)

            dve.wait_ge(std_ready, 1)
            then(dve.reciprocal(rstd[:, :], std[:, :]))
            then(dve.scalar_tensor_tensor(out=shift[:, :], in0=mv[:, 0:1], scalar=-1.0, in1=rstd[:, :],
                                          op0=ALU.mult, op1=ALU.mult))
            dve.wait_ge(consts_in, 64)
            then(dve.tensor_tensor(kron[:, :], ml[:, :], mr[:, :], ALU.mult))
            then(dve.tensor_tensor(kron[:, :], kron[:, :], same[:, :], ALU.mult))
            assert n == PREP
            dve.sem_inc(row_added, 4)

            def add(r, j):
                dve.wait_ge(row_multiplied, r + 3)
                for i, (a, b) in enumerate(HALVES):
                    rows = x_img[:, bass.ds(r * BS, BS), PAIR * a:PAIR * b].rearrange("p h (c w) -> p c h w", w=PAIR)
                    ps = o_ps[j][i][:, 0:P * (b - a)].rearrange("p (c h w) -> p c h w", h=BS, w=PAIR)
                    dve.wait_ge(row_normed, r + 1)
                    dve.tensor_tensor(rows, ps, rows, ALU.add).then_inc(row_added, 1)

            with dve.Fori(0, NROW // 2) as pair:
                r = pair * 2
                add(r, 0)
                add(r + 1, 1)

        @block.tensor
        def _(pe):
            pe.wait_ge(dve_prep, PREP)
            pe.wait_ge(consts_in, 64)
            pe.sem_inc(row_turned, 2)
            pe.sem_inc(row_multiplied, 2)
            pe.sem_inc(turned_out, 4)

            def turn(r, j):
                pe.wait_ge(row_normed, r + 1)
                pe.wait_ge(turned_out, 2 * r + 2)
                for c in range(NPAIR):
                    i = c // FIRST
                    mm = pe.transpose(t_ps[j][i][:, P * (c - FIRST * i):P * (c - FIRST * i + 1)],
                                      xr[:, j, c, :], ident[:, :])
                mm.then_inc(row_turned, 1)

            def multiply(r, j):
                pe.wait_ge(turned_out, 2 * r + 6)
                pe.wait_ge(row_added, 2 * r + 2)
                for c in range(NPAIR):
                    i = c // FIRST
                    mm = pe.matmul(o_ps[j][i][:, P * (c - FIRST * i):P * (c - FIRST * i + 1)],
                                   xt[:, j, c, :], kron[:, :], start=True, stop=True)
                mm.then_inc(row_multiplied, 1)

            turn(0, 0)
            with pe.Fori(0, NROW // 2) as pair:
                r = pair * 2
                turn(r + 1, 1)
                multiply(r, 0)
                turn(r + 2, 0)
                multiply(r + 1, 1)


def network(nc, x_in, l0, l1, l2, l3, out):
    table = nc.dram_tensor("sample_table", [B, STRIDE, 4 * C], F32, kind="Internal").ap()
    k_parts = nc.dram_tensor("k_parts", [2, P // (2 * D), 3, 2 * D, NB * KEYS], BF16, kind="Internal").ap()
    q_parts = nc.dram_tensor("q_parts", [2, P // (2 * D), NTERM, 2 * D, NB * 2 * QS], BF16, kind="Internal").ap()
    with ExitStack() as ctx:
        x = ctx.enter_context(nc.sbuf_tensor("x", [P, XROWS, W], F32))
        x_loaded = ctx.enter_context(nc.semaphore("x_loaded"))
        pads_set = ctx.enter_context(nc.semaphore("pads_set"))
        with nc.Block() as block:
            @block.gpsimd
            def _(pool):
                pool.memset(x[:, 0:HALO, :], 0.0).then_inc(pads_set, 1)
                pool.memset(x[:, HALO + H:XROWS, :], 0.0).then_inc(pads_set, 1)
                pool.wait_ge(pads_set, 2)

            @block.sync
            def _(sp):
                sp.dma_start(x[:, HALO:HALO + H, :], x_in.rearrange("b c h w -> (b c) h w")).then_inc(x_loaded, 16)
                sp.wait_ge(x_loaded, 16)
        halo_attention_layer(nc, x, *l0, k_parts, q_parts)
        lstm_layer(nc, x, *l1)
        deformable_layer(nc, x, *l2, table)
        block_transform_layer(nc, x, *l3, out)


def kernel(**inputs):
    import numpy as np
    import concourse.bacc as bacc
    from concourse.bass_utils import run_bass_kernel_spmd

    a = {k: np.asarray(v) for k, v in inputs.items()}
    nc = bacc.Bacc("TRN2", target_bir_lowering=False, num_devices=1)
    arrays = {}

    def put(name, array):
        array = np.ascontiguousarray(array)
        arrays[name] = array
        return nc.dram_tensor(name, array.shape, mybir.dt.from_np(array.dtype), kind="ExternalInput").ap()

    identity = put("identity", np.eye(P, dtype=np.float32))
    p = np.arange(P)

    w_qkv = a["L0_conv_w_qkv"]
    rel_h = np.broadcast_to(a["L0_conv_rel_h"][0], (WIN, WIN, D // 2))
    rel_w = np.broadcast_to(a["L0_conv_rel_w"][0], (WIN, WIN, D // 2))
    rel = np.concatenate([rel_h, rel_w], axis=-1).transpose(2, 0, 1).reshape(D, KEYS)
    head_mask = np.where((p[:, None] % C // D) % 2 == np.arange(2), D ** -0.5, 0.0).astype(np.float32)
    head_rows = np.zeros((HEADS, C // D, D, 2, HEADS, D), np.float32)
    for h in range(HEADS):
        for k in range(2):
            head_rows[h, k, :, k, h, :] = np.eye(D)
    l0 = [put("w_q", w_qkv[0:C].T), put("w_k", w_qkv[C:2 * C].T), put("w_v", w_qkv[2 * C:3 * C].T),
          put("rel", np.tile(rel, (P // D, 1))), put("head_mask", head_mask),
          put("head_rows", head_rows.reshape(P, 2 * C)), identity]

    hid = a["L1_conv_W_hh"].shape[1]
    l1 = [put("w_ih", np.tile(a["L1_conv_W_ih"].T, (B, 1))), put("w_hh", a["L1_conv_W_hh"].T),
          put("b_ih", a["L1_conv_b_ih"].reshape(4, hid).T), put("b_hh", a["L1_conv_b_hh"].reshape(4, hid).T),
          put("w_lin", a["L1_conv_W_lin"].T), put("b_lin", np.tile(a["L1_conv_b_lin"], B)[:, None])]

    conv_w = np.concatenate([a["L2_conv_p_w"], a["L2_conv_m_w"]]).transpose(1, 2, 3, 0).reshape(C, NTAP * NOUT)
    bias = np.broadcast_to(np.concatenate([a["L2_conv_p_b"], a["L2_conv_m_b"]]), (P, NOUT))
    base = np.zeros((P, NCOL, 2, NTAP), np.float32)
    tap = np.arange(NTAP)
    base[:, :, 0, :] = 1 + (p // TILEW)[:, None, None] + (tap // 3 - 1)
    base[:, :, 1, :] = 1 + (p % TILEW)[:, None, None] + TILEW * np.arange(NCOL)[:, None] + (tap % 3 - 1)
    step = np.zeros((P, NCOL, 2, NTAP), np.float32)
    step[:, :, 0, :] = GROUP
    batch_base = np.broadcast_to(np.repeat(np.arange(B) * STRIDE, NTAP).astype(np.float32), (P, B * NTAP))
    out_w = a["L2_conv_conv_w"].transpose(2, 3, 1, 0).reshape(3, 3 * C, C).transpose(1, 0, 2).reshape(3 * C, 3 * C)
    l2 = [put("conv_w", conv_w), put("pix_bias", bias), put("pix_base", base.reshape(P, NCOL * NOFF)),
          put("group_step", step.reshape(P, NCOL * NOFF)), put("batch_base", batch_base), identity, put("out_w", out_w)]

    m = a["L3_conv_M"]
    bs = m.shape[0]
    full = (bs, 2, bs, bs, 2, bs)
    l3 = [put("m_left", np.broadcast_to(m.T[:, None, None, :, None, None], full).reshape(P, P)),
          put("m_right", np.broadcast_to(m.T[None, None, :, None, None, :], full).reshape(P, P)),
          put("same_block", np.broadcast_to(np.eye(2, dtype=np.float32)[None, :, None, None, :, None], full).reshape(P, P)),
          identity]

    x_in = put("x_in", a["x"])
    out = nc.dram_tensor("out", list(a["x"].shape), F32, kind="ExternalOutput").ap()
    network(nc, x_in, l0, l1, l2, l3, out)
    result = run_bass_kernel_spmd(nc, [arrays], core_ids=[0])
    return result.results[0]["out"]
```

```python
from contextlib import ExitStack
import concourse.bass as bass
from concourse import mybir

F32 = mybir.dt.float32
BF16 = mybir.dt.bfloat16
I32 = mybir.dt.int32
U32 = mybir.dt.uint32
ALU = mybir.AluOpType
ACT = mybir.ActivationFunctionType
AX = mybir.AxisListType

P = 128
B, C, H, W = 4, 32, 96, 96
HALO = 3
XROWS = HALO + H + 21
GN_EPS = 1e-5


def instance_stats(eng, x_rows, stats, mean_var, sem, start):
    flat = x_rows.rearrange("p h w -> p (h w)")
    n = H * W // 512
    for i in range(n):
        eng.bn_stats(stats[:, 6 * i:6 * i + 6], flat[:, 512 * i:512 * (i + 1)]).then_inc(sem, 1)
    eng.wait_ge(sem, start + n)
    eng.bn_aggr(mean_var, stats[:, 0:6 * n]).then_inc(sem, 1)
    return start + n + 1




def wait_apart(eng, sem, value, passed):
    eng.wait_ge(sem, value)
    eng.sem_inc(passed, 1)


BLOCK = 8
WIN = BLOCK + 2 * HALO
HEADS = 4
D = C // HEADS
NB = 6
KEYS = WIN * WIN
HKEYS = KEYS // 2
QS = BLOCK * BLOCK
NHB = H // BLOCK
SCOLS = NB * BLOCK + 2 * HALO
NTERM = 6
ROWS = NTERM * 2 * D
NFILL = 6
MISC = 13


def halo_attention_layer(nc, x, w_q, w_k, w_v, rel, head_mask, head_rows, identity, k_parts, q_parts):
    ctx = ExitStack()
    with ctx:
        def sb(name, shape, dt=F32):
            return ctx.enter_context(nc.sbuf_tensor("l0_" + name, shape, dt))

        def sem(name):
            return ctx.enter_context(nc.semaphore("l0_" + name))

        stats = sb("stats", [P, 6 * (H * W // 512)])
        mv = sb("mv", [P, 2])
        std = sb("std", [P, 1])
        rstd = sb("rstd", [P, 1])
        shift = sb("shift", [P, 1])
        eps = sb("eps", [P, 1])
        wq = sb("wq", [P, P])
        wk = sb("wk", [P, P])
        wv = sb("wv", [P, P])
        relb = sb("relb", [P, WIN, WIN])
        hmask = sb("hmask", [P, 2])
        ident = sb("ident", [P, P])
        strip = sb("strip", [P, 2, WIN, SCOLS])
        xwin = sb("xwin", [P, 2, NB, KEYS])
        k32 = sb("k32", [P, NB, KEYS])
        kp = sb("kp", [P, 3, NB, KEYS], BF16)
        q32 = sb("q32", [P, NB, 2, QS])
        qp = sb("qp", [P, 3, NB, 2, QS], BF16)
        kst = sb("kst", [P, 2, 2, 2, 2, NB, KEYS], BF16)
        qst = sb("qst", [P, 2, 2, 2, 2, NB, 2, QS], BF16)
        v = sb("v", [HKEYS, 2, NB * 2, B, HEADS, 2 * D])
        pt = sb("pt", [HKEYS, 2, 2, 2, 2, 2 * QS])
        mx = sb("mx", [P, 2, 2, NB])
        mparts = sb("mparts", [2 * NB, 2, 2, P], BF16)
        osb = sb("osb", [P, 2, B, BLOCK * NB * BLOCK])
        hrows = sb("hrows", [P, 2, C])
        sums_in = sb("sums_in", [P, 2, 2, BLOCK * NB * BLOCK // 2])

        def ps(name):
            return ctx.enter_context(nc.psum_tensor("l0_" + name, [P, 512], F32))

        s_ps = [ps(f"s{i}") for i in range(2)]
        st_ps = [ctx.enter_context(nc.psum_tensor(f"l0_st{i}", [P, 1024], F32)) for i in range(2)]
        pv_ps = ps("pv")
        misc_ps = ps("misc")

        consts_in = sem("consts_in")
        w_zero = sem("w_zero")
        pool_passed = sem("pool_passed")
        sp_passed = sem("sp_passed")
        fills_set = sem("fills_set")
        pv_zero = sem("pv_zero")
        eps_set = sem("eps_set")
        dve_prep = sem("dve_prep")
        pads_mean = sem("pads_mean")
        std_ready = sem("std_ready")
        strip_ready = sem("strip_ready")
        win_ready = sem("win_ready")
        misc_done = sem("misc_done")
        misc_read = sem("misc_read")
        k32_ready = sem("k32_ready")
        q32_ready = sem("q32_ready")
        q_part = sem("q_part")
        k_rest = sem("k_rest")
        q_rest = sem("q_rest")
        k_split = sem("k_split")
        q_split = sem("q_split")
        v_ready = sem("v_ready")
        parts_stored = sem("parts_stored")
        stacked = [[sem(f"stacked{i}{j}") for j in range(2)] for i in range(2)]
        s_filled = sem("s_filled")
        s_read = sem("s_read")
        m_split = sem("m_split")
        m_placed = [sem(f"m_placed{i}") for i in range(B)]
        st_done = sem("st_done")
        exp_done = sem("exp_done")
        pv_done = sem("pv_done")
        pv_read = sem("pv_read")
        sums_in_done = sem("sums_in_done")
        recip_done = sem("recip_done")
        quot_done = sem("quot_done")
        x_added = sem("x_added")

        EARLY = 13
        LOADS = 2
        STORES = 6
        USES = ([("k", 0), ("k", 1), ("k", 2)], [("q", 0), ("o", 0)], [("o", 1), ("v", 0)], [("v", 1), ("v", 2)])
        K_TERMS = (slice(0, 3), slice(3, 5), slice(5, 6))
        Q_TERMS = (slice(0, 3), slice(3, 5), slice(5, 6))
        x_img = x[:, HALO:HALO + H, :]

        def use_number(G, b, s):
            order = [u for u in (0, 1, "max", 2) if u == "max" or u < len(USES[b])]
            return G * MISC + (EARLY + sum(1 + len(USES[a]) for a in range(b)) + order.index(s))

        def last_use(b, s):
            b, s = (b, s - 1) if s else ((b - 1) % B, 2)
            return (b, s, *USES[b][s]) if s < len(USES[b]) else None

        block = ctx.enter_context(nc.Block())

        @block.sync
        def _(sp):
            sp.wait_ge(w_zero, 3)
            for b in range(B):
                for dst, src in ((wq, w_q), (wk, w_k), (wv, w_v)):
                    sp.dma_start(dst[C * b:C * (b + 1), C * b:C * (b + 1)], src).then_inc(consts_in, 16)
            for dst, src in ((relb[:, :, :].rearrange("p i j -> p (i j)"), rel), (hmask[:, :], head_mask), (ident[:, :], identity),
                             (hrows[:, :, :].rearrange("p k c -> p (k c)"), head_rows)):
                sp.dma_start(dst, src).then_inc(consts_in, 16)

            def store_k(G, half, i):
                sp.wait_ge(k_split, 3 * G + i + 1)
                terms = K_TERMS[i]
                sp.dma_start(k_parts[half, :, terms, :],
                             kp[:, i].rearrange("p b n -> p (b n)").unsqueeze(1).to_broadcast(
                                 [P, terms.stop - terms.start, NB * KEYS])).then_inc(parts_stored, 16)

            def store_q(G, half):
                sp.wait_ge(q_split, G + 1)
                for terms in Q_TERMS:
                    sp.dma_start(q_parts[half, :, terms, :],
                                 qp[:, 0:terms.stop - terms.start].rearrange("p i b s q -> p i (b s q)")).then_inc(parts_stored, 16)

            def load_stacks(G, half, load, used):
                wait_apart(sp, parts_stored, 16 * STORES * (G + 1), sp_passed)
                if used is not None:
                    sp.wait_ge(st_done, used)
                rows = slice(P // 2 * load, P // 2 * (load + 1))
                for stacks, parts in ((kst[0:ROWS, half, load].rearrange("p b a k n -> p (b a) (k n)"), k_parts),
                                      (qst[0:ROWS, half, load].rearrange("p b a k s q -> p (b a) (k s q)"), q_parts)):
                    sp.dma_start(stacks, parts[half, rows].rearrange("(g r) t n -> (r t) g n", r=2 * D)).then_inc(
                        stacked[half][load], 16)

            def place_maxima(U, par, half, b):
                sp.wait_ge(m_split, 2 * U + 2)
                for i in range(2):
                    sp.dma_start(qst[ROWS + i:ROWS + i + 1, half, b // 2, b % 2],
                                 mparts[0:2 * NB, par, i, :]).then_inc(m_placed[b], 16)

            for G in range(2):
                for i in range(3):
                    store_k(G, G, i)
                store_q(G, G)
                for load in range(2 - G):
                    load_stacks(G, G, load, None)
            for U in range(2):
                place_maxima(U, U, 0, U)
            with sp.Fori(0, NHB) as hb:
                for half in range(2):
                    G = hb * 2 + half
                    for b in range(B):
                        U = G * B + b
                        if b == 0:
                            load_stacks(G + 1, 1 - half, 1, G * 12 + 1)
                        if b == 2:
                            for load in range(2):
                                wait_apart(sp, stacked[half][load], 16 * LOADS * (hb + 1), sp_passed)
                            store_k(G + 2, half, 0)
                        if b == 3:
                            store_k(G + 2, half, 1)
                            store_q(G + 2, half)
                        place_maxima(U + 2, b % 2, (half + (b + 2) // B) % 2, (b + 2) % B)
                    store_k(G + 2, half, 2)
                    load_stacks(G + 2, half, 0, G * 12 + 7)
            for half in range(2):
                for load in range(2):
                    sp.wait_ge(stacked[half][load], 16 * LOADS * (NHB + (half + load < 2)))
            for b in range(B):
                sp.wait_ge(m_placed[b], 32 * (2 * NHB + (b < 2)))
            sp.wait_ge(parts_stored, 16 * STORES * (2 * NHB + 2))

        @block.gpsimd
        def _(pool):
            for w in (wq, wk, wv):
                pool.memset(w[:, :], 0.0).then_inc(w_zero, 1)
            pool.memset(eps[:, :], GN_EPS).then_inc(eps_set, 1)
            pool.memset(strip[:, :, :, :], 0.0).then_inc(fills_set, 1)
            pool.memset(v[:, :, :, :, :, :], 1.0).then_inc(fills_set, 1)
            pool.wait_ge(fills_set, 2)
            pool.memset(kst[ROWS:ROWS + 2].rearrange("p h l b a k n -> p (h l b a k n)"), 1.0).then_inc(fills_set, 1)
            pool.wait_ge(fills_set, 3)
            pool.memset(osb[:, 1], 1.0).then_inc(fills_set, 1)

            def windows(G, half):
                wait_apart(pool, strip_ready, G + 1, pool_passed)
                for blk in range(NB):
                    ins = pool.tensor_copy(xwin[:, half, blk, :].rearrange("p (i j) -> p i j", j=WIN),
                                           strip[:, half, :, BLOCK * blk:BLOCK * blk + WIN])
                ins.then_inc(win_ready, 1)

            def splits(G):
                if not (isinstance(G, int) and G == 0):
                    pool.wait_ge(parts_stored, 16 * STORES * G)
                wait_apart(pool, k32_ready, 3 * G + 3, pool_passed)
                pool.tensor_copy(kp[:, 0], k32[:, :, :]).then_inc(k_split, 1)
                pool.wait_ge(q_part, 2 * G + 1)
                pool.tensor_tensor(q32[:, :, :, :], q32[:, :, :, :], qp[:, 0], ALU.subtract).then_inc(q_rest, 1)
                pool.wait_ge(k_split, 3 * G + 1)
                pool.tensor_tensor(k32[:, :, :], k32[:, :, :], kp[:, 0], ALU.subtract).then_inc(k_rest, 1)
                pool.wait_ge(q_part, 2 * G + 2)
                pool.tensor_tensor(qp[:, 2], q32[:, :, :, :], qp[:, 1], ALU.subtract).then_inc(q_split, 1)
                pool.wait_ge(k_split, 3 * G + 2)
                pool.tensor_tensor(kp[:, 2], k32[:, :, :], kp[:, 1], ALU.subtract).then_inc(k_split, 1)

            for half in range(2):
                windows(half, half)
            for G in range(2):
                splits(G)
            pool.wait_ge(misc_done, 7)
            windows(2, 0)
            pool.sem_inc(x_added, 3)

            def add_attention(hb, G, half, i):
                if i == 0:
                    pool.wait_ge(strip_ready, G + 4 - half)
                pool.wait_ge(recip_done, 2 * G + i + 3)
                pool.tensor_tensor(sums_in[:, i, 0, :], sums_in[:, i, 0, :], sums_in[:, i, 1, :], ALU.mult).then_inc(quot_done, 1)
                pool.wait_ge(quot_done, 2 * G + i + 1)
                rows = x_img[:, bass.ds(hb * BLOCK + i * (BLOCK // 2), BLOCK // 2), NB * BLOCK * half:NB * BLOCK * (half + 1)]
                pool.tensor_tensor(rows, sums_in[:, i, 0, :].rearrange("p (i c) -> p i c", i=BLOCK // 2), rows,
                                   ALU.add).then_inc(x_added, 1)
                pool.wait_ge(x_added, 2 * G + i + 4)

            def body(hb, first=False):
                for half in range(2):
                    G = hb * 2 + half
                    splits(G + 2)
                    if not (first and half == 0):
                        for i in range(2):
                            add_attention(hb - (1 - half), G - 1, 1 - half, i)
                    pool.wait_ge(misc_done, use_number(G, 3, 1) + 1)
                    windows(G + 3, 1 - half)

            body(0, first=True)
            with pool.Fori(1, NHB) as hb:
                body(hb)
            for i in range(2):
                add_attention(NHB - 1, 2 * NHB - 1, 1, i)

        @block.scalar
        def _(act):
            act.wait_ge(eps_set, 1)
            act.wait_ge(dve_prep, 19)
            act.activation(std[:, :], mv[:, 1:2], ACT.Sqrt, bias=eps[:, :]).then_inc(std_ready, 1)
            act.wait_ge(consts_in, 16 * 16)
            act.sem_inc(exp_done, 1)
            act.sem_inc(misc_read, 1)

            def part_k(G):
                act.wait_ge(k_rest, G + 1)
                act.activation(kp[:, 1], k32[:, :, :], ACT.Copy).then_inc(k_split, 1)

            def part_q(G, i):
                if i == 0:
                    if not (isinstance(G, int) and G == 0):
                        act.wait_ge(parts_stored, 16 * STORES * G)
                    act.wait_ge(q32_ready, 2 * G + 2)
                else:
                    act.wait_ge(q_rest, G + 1)
                act.activation(qp[:, i], q32[:, :, :, :], ACT.Copy).then_inc(q_part, 1)

            def read_q(G, n):
                act.wait_ge(misc_done, n + 1)
                act.wait_ge(q_split, G)
                for slot in range(2):
                    ins = act.activation(q32[:, :, slot, :], misc_ps[:, 0:NB * QS].rearrange("p (k q) -> p k q", q=QS),
                                         ACT.Copy, scale=hmask[:, slot:slot + 1])
                    ins.then_inc(q32_ready, 1)
                act.wait_ge(q32_ready, 2 * G + 2)
                act.sem_inc(misc_read, 1)

            def read_v(G, half, i, n):
                act.wait_ge(misc_done, n + 1)
                act.wait_ge(fills_set, 4)
                if not isinstance(G, int):
                    act.wait_ge(pv_done, G * 12 - 11)
                act.activation(v[:, half, 4 * i:4 * i + 4, :, :, 0:D].rearrange("p t b h d -> p t (b h) d"),
                               misc_ps[0:HKEYS, :].rearrange("p (t m d) -> p t m d", t=4, d=D), ACT.Copy).then_inc(v_ready, 1)
                act.wait_ge(v_ready, 3 * G + i + 1)
                act.sem_inc(misc_read, 1)

            def read_o(G, i, n):
                act.wait_ge(misc_done, n + 1)
                act.wait_ge(x_added, 2 * G + 1)
                act.activation(sums_in[:, i].rearrange("p k n -> p (k n)"), misc_ps[:, 0:NB * QS], ACT.Copy).then_inc(sums_in_done, 1)
                act.wait_ge(sums_in_done, 2 * G + i + 1)
                act.sem_inc(misc_read, 1)

            def exps(st, slot):
                act.wait_ge(st_done, st + 2)
                act.wait_ge(pv_done, st)
                act.activation(pt[:, slot].rearrange("p k a c n -> p (k a c n)"), st_ps[slot][0:HKEYS, :], ACT.Exp).then_inc(exp_done, 1)

            read_q(0, 3)
            part_q(0, 0)
            for i in range(3):
                read_v(0, 0, i, 4 + i)
            part_q(0, 1)
            part_k(0)
            read_q(1, 10)
            part_q(1, 0)
            part_q(1, 1)
            part_k(1)
            PART_AT = {(1, 2): ("q", 0), (2, 2): ("q", 1), (3, 0): ("k", 1)}
            with act.Fori(0, NHB) as hb:
                for half in range(2):
                    G = hb * 2 + half
                    for b in range(B):
                        for s in range(3):
                            exps((G * B + b) * 3 + s, (b + s) % 2)
                            if last_use(b, s):
                                ub, us, kind, i = last_use(b, s)
                                if kind == "v":
                                    read_v(G + 1, 1 - half, i, use_number(G, ub, us))
                                if kind == "q":
                                    read_q(G + 2, use_number(G, ub, us))
                                if kind == "o":
                                    read_o(G, i, use_number(G, ub, us))
                            if (b, s) in PART_AT:
                                part, i = PART_AT[b, s]
                                part_k(G + 2) if part == "k" else part_q(G + 2, i)
            for i in range(2):
                read_o(2 * NHB, i, 2 * NHB * MISC + EARLY + i)

        @block.vector
        def _(dve):
            dve.memset(pv_ps[:, :], 0.0).then_inc(pv_zero, 1)
            n = instance_stats(dve, x_img, stats, mv[:, :], dve_prep, 0)
            dve.wait_ge(std_ready, 1)
            dve.wait_ge(dve_prep, n)
            dve.reciprocal(rstd[:, :], std[:, :]).then_inc(pads_mean, 1)
            dve.wait_ge(pads_mean, 1)
            dve.scalar_tensor_tensor(out=shift[:, :], in0=mv[:, 0:1], scalar=-1.0, in1=rstd[:, :],
                                     op0=ALU.mult, op1=ALU.mult).then_inc(pads_mean, 1)
            for rows in (slice(0, HALO), slice(HALO + H, XROWS)):
                dve.tensor_scalar(x[:, rows, :], x[:, rows, :], 0.0, mv[:, 0:1], ALU.mult, ALU.add).then_inc(pads_mean, 1)
            dve.wait_ge(consts_in, 16 * 16)
            dve.sem_inc(s_read, 2)
            dve.sem_inc(pv_read, 1)

            dve.wait_ge(fills_set, 4)
            dve.wait_ge(pads_mean, 4)

            def load(hb, half):
                to, of = (slice(HALO, SCOLS), slice(0, SCOLS - HALO)) if half == 0 else \
                         (slice(0, SCOLS - HALO), slice(W - (SCOLS - HALO), W))
                dve.tensor_scalar(strip[:, half, :, to], x[:, bass.ds(hb * BLOCK, WIN), of], rstd[:, 0:1], shift[:, 0:1],
                                  ALU.mult, ALU.add).then_inc(strip_ready, 1)

            def read_k(G, i, n):
                dve.wait_ge(misc_done, n + 1)
                if i == 0:
                    dve.wait_ge(k_split, 3 * G)
                dve.tensor_tensor(k32[:, 2 * i:2 * i + 2, :], misc_ps[:, 0:2 * KEYS].rearrange("p (k n) -> p k n", n=KEYS),
                                  relb[:, :, :].rearrange("p i j -> p (i j)").unsqueeze(1).to_broadcast([P, 2, KEYS]),
                                  ALU.add).then_inc(k32_ready, 1)
                dve.wait_ge(k32_ready, 3 * G + i + 1)
                dve.sem_inc(misc_read, 1)

            def row_max(U, par, j):
                f = U * NFILL + j
                dve.wait_ge(s_filled, f + 1)
                dve.tensor_reduce(mx[:, par, j // 3, 2 * (j % 3):2 * (j % 3) + 2],
                                  s_ps[j % 2][:, 0:2 * KEYS].rearrange("p (k n) -> p k n", n=KEYS), AX.X, ALU.max).then_inc(s_read, 1)

            def split_max(U, par, n, b_last, placed):
                dve.wait_ge(misc_done, n + 1)
                if placed is not None:
                    dve.wait_ge(m_placed[b_last], placed)
                src = misc_ps[0:2 * NB, 0:P]
                dve.tensor_scalar(mparts[:, par, 0, :], src, -1.0, None, ALU.mult).then_inc(m_split, 1)
                dve.wait_ge(m_split, 2 * U + 1)
                dve.scalar_tensor_tensor(out=mparts[:, par, 1, :], in0=src, scalar=-1.0, in1=mparts[:, par, 0, :],
                                         op0=ALU.mult, op1=ALU.subtract).then_inc(m_split, 1)
                dve.wait_ge(m_split, 2 * U + 2)
                dve.sem_inc(misc_read, 1)

            def read_sums(G, U, half, b):
                dve.wait_ge(misc_done, G * MISC + EARLY)
                dve.wait_ge(pv_done, U * 3 + 4)
                dve.tensor_copy(osb[:, half, b, :].rearrange("p (i k j) -> p k i j", i=BLOCK, j=BLOCK),
                                pv_ps[:, 0:NB * QS].rearrange("p (k i j) -> p k i j", i=BLOCK, j=BLOCK)).then_inc(pv_read, 1)

            def invert_sums(G, i):
                dve.wait_ge(sums_in_done, 2 * G + i + 1)
                dve.reciprocal(sums_in[:, i, 1, :], sums_in[:, i, 1, :]).then_inc(recip_done, 1)

            for half in range(2):
                load(0, half)
            for i in range(3):
                read_k(0, i, i)
            for i in range(3):
                read_k(1, i, 7 + i)
            dve.wait_ge(misc_done, 4)
            dve.wait_ge(win_ready, 1)
            load(1, 0)
            for U in range(2):
                for j in range(NFILL):
                    row_max(U, U, j)
            split_max(0, 0, 11, None, None)
            for j in range(2):
                row_max(2, 0, j)
            split_max(1, 1, 12, None, None)

            INVERT_AT = {(2, 0): 0, (3, 0): 1}
            with dve.Fori(0, NHB) as hb:
                for half in range(2):
                    G = hb * 2 + half
                    for b in range(B):
                        U = G * B + b
                        for s in range(3):
                            if last_use(b, s):
                                ub, us, kind, i = last_use(b, s)
                                n = use_number(G, ub, us)
                                if kind == "k":
                                    read_k(G + 2, i, n)
                            for k in range(2):
                                row_max(U + 2 + s // 2, (b + s // 2) % 2, (2 * s + 2 + k) % NFILL)
                            if (b, s) in INVERT_AT:
                                invert_sums(G, INVERT_AT[b, s])
                            if s == 2:
                                split_max(U + 2, b % 2, use_number(G, b, "max"), b, G * 32 + 32)
                        read_sums(G, U, half, b)
                        if b == 0:
                            dve.wait_ge(win_ready, G + 2)
                            load(hb + (1 + half), 1 - half)

            for i in range(2):
                invert_sums(2 * NHB, i)

        @block.tensor
        def _(pe):
            pe.wait_ge(consts_in, 16 * 16)
            pe.wait_ge(fills_set, 4)
            pe.wait_ge(pv_zero, 1)
            pe.sem_inc(pv_done, 1)
            pe.sem_inc(st_done, 1)

            def use(kind, half, i, n):
                pe.wait_ge(misc_read, n + 1)
                if kind == "v":
                    for t in range(4):
                        blk, chunk = (4 * i + t) // 2, t % 2
                        mm = pe.matmul(misc_ps[0:HKEYS, P * t:P * (t + 1)], xwin[:, half, blk, HKEYS * chunk:HKEYS * (chunk + 1)],
                                       wv[:, :], start=True, stop=True)
                elif kind == "o":
                    N = BLOCK * NB * BLOCK // 2
                    for k in range(2):
                        for b in range(B):
                            mm = pe.matmul(misc_ps[C * b:C * (b + 1), N * k:N * (k + 1)], hrows[:, k, :],
                                           osb[:, half, b, N * i:N * (i + 1)], start=True, stop=True)
                elif kind == "k":
                    for k in range(2):
                        at = BLOCK * (2 * i + k)
                        mm = pe.matmul(misc_ps[:, KEYS * k:KEYS * (k + 1)], wk[:, :], strip[:, half, :, at:at + WIN],
                                       start=True, stop=True)
                else:
                    for blk in range(NB):
                        mm = pe.matmul(misc_ps[:, QS * blk:QS * (blk + 1)], wq[:, :],
                                       strip[:, half, HALO:HALO + BLOCK, HALO + BLOCK * blk:HALO + BLOCK * (blk + 1)],
                                       start=True, stop=True)
                mm.then_inc(misc_done, 1)

            def maxima(U, par, n):
                pe.wait_ge(misc_read, n + 1)
                pe.wait_ge(s_read, U * NFILL + NFILL + 2)
                pe.transpose(misc_ps[0:2 * NB, 0:P], mx[:, par].rearrange("p a k -> p (a k)"), ident[:, :]).then_inc(misc_done, 1)

            def fill(U, half, b, j, uses):
                if j == 0 and b % 2 == 0:
                    pe.wait_ge(stacked[half][b // 2], 16 * LOADS * uses)
                f = U * NFILL + j
                pe.wait_ge(s_read, f + 1)
                for k in range(2):
                    blk = 2 * (j % 3) + k
                    mm = pe.matmul(s_ps[j % 2][:, KEYS * k:KEYS * (k + 1)],
                                   qst[0:ROWS, half, b // 2, b % 2, j // 3, blk].rearrange("p s q -> p (s q)"),
                                   kst[0:ROWS, half, b // 2, b % 2, j // 3, blk, :], start=True, stop=True)
                mm.then_inc(s_filled, 1)

            def turned_scores(st, slot, half, b, s, placed):
                if placed is not None:
                    pe.wait_ge(m_placed[b], placed)
                pe.wait_ge(exp_done, st)
                for k in range(2):
                    blk = 2 * s + k
                    for pair in range(2):
                        for chunk in range(2):
                            at = 512 * k + P * (2 * pair + chunk)
                            mm = pe.matmul(st_ps[slot][0:HKEYS, at:at + P],
                                           kst[0:ROWS + 2, half, b // 2, b % 2, pair, blk, HKEYS * chunk:HKEYS * (chunk + 1)],
                                           qst[0:ROWS + 2, half, b // 2, b % 2, pair, blk].rearrange("p s q -> p (s q)"), start=True, stop=True)
                mm.then_inc(st_done, 1)

            def sums(G, U, half, b, s, slot):
                if s == 0:
                    pe.wait_ge(v_ready, 3 * G + 3)
                    pe.wait_ge(pv_read, U + 1)
                pe.wait_ge(exp_done, U * 3 + s + 2)
                for k in range(2):
                    blk = 2 * s + k
                    for chunk in range(2):
                        for h in range(HEADS):
                            mm = pe.matmul(pv_ps[32 * h:32 * h + 2 * D, QS * blk:QS * (blk + 1)],
                                           v[:, half, 2 * blk + chunk, b, h, :],
                                           pt[:, slot, k, h // 2, chunk, QS * (h % 2):QS * (h % 2 + 1)],
                                           start=(chunk == 0), stop=(chunk == 1))
                mm.then_inc(pv_done, 1)

            for half in range(2):
                pe.wait_ge(strip_ready, half + 1)
                for i in range(3):
                    use("k", half, i, 7 * half + i)
                use("q", half, 0, 7 * half + 3)
                if half == 0:
                    pe.wait_ge(win_ready, 1)
                    for i in range(3):
                        use("v", 0, i, 4 + i)
            for U in range(3):
                for j in range(NFILL if U < 2 else 2):
                    fill(U, 0, U, j, 1)
                if U > 0:
                    maxima(U - 1, U - 1, 10 + U)
            turned_scores(0, 0, 0, 0, 0, 32)

            with pe.Fori(0, NHB) as hb:
                for half in range(2):
                    G = hb * 2 + half
                    for b in range(B):
                        U = G * B + b
                        for s in range(3):
                            ahead = b + 2 + s // 2
                            later = half + ahead // B
                            for k in range(2):
                                fill(U + 2 + s // 2, later % 2, ahead % B, (2 * s + 2 + k) % NFILL, hb + (1 + later // 2))
                            if s < 2:
                                turned_scores(U * 3 + s + 1, (b + s + 1) % 2, half, b, s + 1, None)
                            else:
                                turned_scores(U * 3 + 3, (b + 1) % 2, (half + (b + 1) // B) % 2, (b + 1) % B, 0,
                                              G * 32 + 32 * (1 + (b + 1) // B))
                            if s == 2:
                                maxima(U + 2, b % 2, use_number(G, b, "max"))
                            sums(G, U, half, b, s, (b + s) % 2)
                            if s < len(USES[b]):
                                kind, i = USES[b][s]
                                if kind == "k" and i == 0:
                                    pe.wait_ge(strip_ready, G + 3)
                                if kind == "v" and i == 0:
                                    pe.wait_ge(win_ready, G + 2)
                                if kind == "o" and i == 0:
                                    pe.wait_ge(pv_read, G * B + 1)
                                use(kind, 1 - half if kind in "vo" else half, i, use_number(G, b, s))
            pe.wait_ge(pv_read, 2 * NHB * B + 1)
            for i in range(2):
                use("o", 1, i, 2 * NHB * MISC + EARLY + i)


def lstm_layer(nc, x, w_ih_rep, w_hh_t, bias_ih, bias_hh, w_lin_t, b_lin_rep):
    HID = 128
    STEPS = 4
    CHUNK = 24
    NCH = W // CHUNK
    ctx = ExitStack()
    with ctx:
        def sb(name, shape, dt=F32):
            return ctx.enter_context(nc.sbuf_tensor("l1_" + name, shape, dt))

        def sem(name):
            return ctx.enter_context(nc.semaphore("l1_" + name))

        stats = sb("stats", [P, 6 * (H * W // 512)])
        mv = sb("mv", [P, 2])
        std = sb("std", [P, 1])
        rstd = sb("rstd", [P, 1])
        eps = sb("eps", [P, 1])
        xn = sb("xn", [P, 2, CHUNK, H])
        part = sb("part", [P, 2, 3, CHUNK, H], BF16)
        xs = sb("xs", [P, B, W, H], BF16)
        wih = sb("wih", [P, 4 * HID])
        wp = sb("wp", [P, 3, 4 * HID], BF16)
        wa = sb("wa", [P, 4 * HID], BF16)
        wb = sb("wb", [P, 4 * HID], BF16)
        whh = sb("whh", [HID, 4 * HID])
        bi = sb("bi", [HID, 4])
        bh = sb("bh", [HID, 4])
        bias = sb("bias", [HID, 4])
        wlin = sb("wlin", [HID, C])
        blin = sb("blin", [P, 1])
        gate = sb("gate", [HID, 2, 4, 2 * H])
        prod = sb("prod", [HID, 2, 2, 2 * H])
        cell = sb("cell", [HID, 2, 2 * H])
        tcell = sb("tcell", [HID, 2, 2 * H])
        hid = sb("hid", [HID, 2, 2, 2 * H])
        gates_ps = [ctx.enter_context(nc.psum_tensor(f"l1_g{i}", [P, 512], F32)) for i in range(6)]
        lin_ps = [ctx.enter_context(nc.psum_tensor(f"l1_l{i}", [P, 512], F32)) for i in range(2)]

        weights_in = sem("weights_in")
        dve_prep = sem("dve_prep")
        eps_set = sem("eps_set")
        std_ready = sem("std_ready")
        part_cast = sem("part_cast")
        part_ready = sem("part_ready")
        stacked = [sem(f"stacked{i}") for i in range(NCH)]
        state_zero = sem("state_zero")
        gates_done = [sem(f"gates_done{c}") for c in range(2)]
        gates_act = [sem(f"gates_act{c}") for c in range(2)]
        prods_done = [sem(f"prods_done{c}") for c in range(2)]
        cell_done = [sem(f"cell_done{c}") for c in range(2)]
        tanh_done = [sem(f"tanh_done{c}") for c in range(2)]
        hid_done = [sem(f"hid_done{c}") for c in range(2)]
        lin_done = sem("lin_done")
        lin_added = sem("lin_added")

        PREP = 19 + 1 + 2 * NCH + 11
        SLICE = [2, 0, 1, 3]
        FUNC = [ACT.Tanh, ACT.Sigmoid, ACT.Sigmoid, ACT.Sigmoid]
        x_img = x[:, HALO:HALO + H, :]

        def gate_ps(c, g):
            return gates_ps[3 * c + max(g - 1, 0)][:, (g == 1) * 2 * H:((g == 1) + 1) * 2 * H]

        block = ctx.enter_context(nc.Block())

        @block.sync
        def _(sp):
            for dst, src in ((wih, w_ih_rep), (whh, w_hh_t), (bi, bias_ih), (bh, bias_hh),
                             (wlin, w_lin_t), (blin, b_lin_rep)):
                sp.dma_start(dst[:, :], src).then_inc(weights_in, 16)
            for k in range(NCH):
                sp.wait_ge(part_ready, k + 1)
                for b in range(B):
                    for row, piece in enumerate((0, 1, 2, 0)):
                        sp.dma_start(xs[32 * row:32 * row + 32, b, CHUNK * k:CHUNK * (k + 1), :],
                                     part[32 * b:32 * b + 32, k % 2, piece, :, :]).then_inc(stacked[k], 16)
            for k in range(NCH):
                sp.wait_ge(stacked[k], 16 * 16)

        @block.gpsimd
        def _(pool):
            pool.memset(eps[:, :], GN_EPS).then_inc(eps_set, 1)
            pool.memset(cell[:, :, :], 0.0).then_inc(state_zero, 1)
            pool.memset(hid[:, :, :, :], 0.0).then_inc(state_zero, 1)

        @block.scalar
        def _(act):
            act.wait_ge(eps_set, 1)
            act.wait_ge(dve_prep, 19)
            act.activation(std[:, :], mv[:, 1:2], ACT.Sqrt, bias=eps[:, :]).then_inc(std_ready, 1)
            for k in range(NCH):
                act.wait_ge(dve_prep, 20 + 2 * k + 1)
                if k >= 2:
                    act.wait_ge(stacked[k - 2], 16 * 16)
                act.activation(part[:, k % 2, 0], xn[:, k % 2], ACT.Copy).then_inc(part_cast, 1)
                act.wait_ge(dve_prep, 20 + 2 * k + 2)
                act.activation(part[:, k % 2, 1], xn[:, k % 2], ACT.Copy).then_inc(part_cast, 1)
            act.wait_ge(dve_prep, PREP)

            def gates(i, c):
                for g in range(4):
                    act.wait_ge(gates_done[c], 4 * i + max(g + 1, 2))
                    if g == 0:
                        act.wait_ge(hid_done[c], i + 1)
                    act.activation(gate[:, c, g, :], gate_ps(c, g), FUNC[g],
                                   bias=bias[:, SLICE[g]:SLICE[g] + 1]).then_inc(gates_act[c], 1)

            def cells(i, c):
                act.wait_ge(cell_done[c], i + 1)
                act.activation(tcell[:, c, :], cell[:, c, :], ACT.Tanh).then_inc(tanh_done[c], 1)

            with act.Fori(0, W, STEPS) as t:
                for s in range(STEPS):
                    for c in range(2):
                        gates(t + s, c)
                        cells(t + s, c)

        @block.vector
        def _(dve):
            n = instance_stats(dve, x_img, stats, mv[:, :], dve_prep, 0)
            dve.wait_ge(std_ready, 1)
            dve.reciprocal(rstd[:, :], std[:, :]).then_inc(dve_prep, 1)
            n += 1
            dve.wait_ge(dve_prep, n)
            xt = x_img.rearrange("p f t -> p t f")
            for k in range(NCH):
                if k >= 2:
                    dve.wait_ge(part_ready, k - 1)
                dve.tensor_scalar(xn[:, k % 2], xt[:, CHUNK * k:CHUNK * (k + 1), :], mv[:, 0:1], rstd[:, 0:1],
                                  ALU.subtract, ALU.mult).then_inc(dve_prep, 1)
                n += 1
                dve.wait_ge(dve_prep, n)
                dve.wait_ge(part_cast, 2 * k + 1)
                dve.tensor_tensor(xn[:, k % 2], xn[:, k % 2], part[:, k % 2, 0], ALU.subtract).then_inc(dve_prep, 1)
                n += 1
                dve.wait_ge(dve_prep, n)
                dve.wait_ge(part_cast, 2 * k + 2)
                dve.tensor_tensor(part[:, k % 2, 2], xn[:, k % 2], part[:, k % 2, 1], ALU.subtract).then_inc(part_ready, 1)

            def then(ins):
                nonlocal n
                ins.then_inc(dve_prep, 1)
                n += 1
                dve.wait_ge(dve_prep, n)

            dve.wait_ge(weights_in, 96)
            then(dve.tensor_tensor(bias[:, :], bi[:, :], bh[:, :], ALU.add))
            then(dve.tensor_copy(wp[:, 0], wih[:, :]))
            then(dve.tensor_tensor(wih[:, :], wih[:, :], wp[:, 0], ALU.subtract))
            then(dve.tensor_copy(wp[:, 1], wih[:, :]))
            then(dve.tensor_tensor(wp[:, 2], wih[:, :], wp[:, 1], ALU.subtract))
            then(dve.tensor_copy(wa[0:96, :], wp[0:96, 0]))
            then(dve.tensor_copy(wa[96:128, :], wp[96:128, 1]))
            then(dve.tensor_copy(wb[0:32, :], wp[0:32, 2]))
            then(dve.tensor_copy(wb[32:64, :], wp[32:64, 1]))
            then(dve.tensor_copy(wb[64:96, :], wp[64:96, 1]))
            then(dve.memset(wb[96:128, :], 0.0))
            assert n == PREP
            dve.wait_ge(state_zero, 2)

            def cell_ops(i, c):
                dve.wait_ge(gates_act[c], 4 * i + 6)
                dve.tensor_tensor(prod[:, c, 0], gate[:, c, 0], gate[:, c, 1], ALU.mult).then_inc(prods_done[c], 1)
                dve.wait_ge(gates_act[c], 4 * i + 7)
                dve.tensor_tensor(prod[:, c, 1], gate[:, c, 2], cell[:, c], ALU.mult).then_inc(prods_done[c], 1)
                dve.wait_ge(prods_done[c], 2 * i + 2)
                dve.tensor_tensor(cell[:, c], prod[:, c, 0], prod[:, c, 1], ALU.add).then_inc(cell_done[c], 1)

            def hid_ops(i, c, s):
                dve.wait_ge(gates_act[c], 4 * i + 8)
                dve.wait_ge(tanh_done[c], i + 1)
                dve.tensor_tensor(hid[:, c, (s + 1) % 2], gate[:, c, 3], tcell[:, c], ALU.mult).then_inc(hid_done[c], 1)

            def add_linear(group, j):
                dve.wait_ge(lin_done, 2 * STEPS * (group + 1))
                cols = x_img[:, :, bass.ds(group * STEPS, STEPS)]
                ps = lin_ps[j][:, 0:STEPS * H].rearrange("p (t f) -> p f t", f=H)
                dve.scalar_tensor_tensor(out=cols, in0=ps, scalar=blin[:, 0:1], in1=cols,
                                         op0=ALU.add, op1=ALU.add).then_inc(lin_added, 1)

            def body(k, first=False):
                for j in range(2):
                    group = k * 2 + j
                    for s in range(STEPS):
                        for c in range(2):
                            cell_ops(group * STEPS + s, c)
                            hid_ops(group * STEPS + s, c, s)
                        if s == 1 and not (first and j == 0):
                            add_linear(group - 1, 1 - j)

            body(0, first=True)
            with dve.Fori(1, W // (2 * STEPS)) as k:
                body(k)
            add_linear(W // STEPS - 1, 1)

        @block.tensor
        def _(pe):
            for k in range(NCH):
                pe.wait_ge(stacked[k], 16 * 16)
            pe.wait_ge(dve_prep, PREP)
            pe.wait_ge(state_zero, 2)

            def step_gates(i, c, s):
                xin = xs[:, 2 * c:2 * c + 2, bass.ds(i, 1), :]
                for g in range(4):
                    w = slice(HID * SLICE[g], HID * (SLICE[g] + 1))
                    if g != 1:
                        pe.wait_ge(gates_act[c], 4 * i + max(g + 1, 2))
                    pe.matmul(gate_ps(c, g), wa[:, w], xin, start=True, stop=False)
                    pe.matmul(gate_ps(c, g), wb[:, w], xin, start=False, stop=False)
                    if g == 0:
                        pe.wait_ge(hid_done[c], i + 1)
                    pe.matmul(gate_ps(c, g), whh[:, w], hid[:, c, s % 2], start=False, stop=True).then_inc(gates_done[c], 1)

            def linear(i, c, s, j):
                pe.wait_ge(hid_done[c], i + 2)
                for b in (2 * c, 2 * c + 1):
                    mm = pe.matmul(lin_ps[j][32 * b:32 * b + 32, s * H:(s + 1) * H], wlin[:, :],
                                   hid[:, c, (s + 1) % 2, (b % 2) * H:(b % 2 + 1) * H], start=True, stop=True)
                mm.then_inc(lin_done, 1)

            def body(k, first=False):
                for j in range(2):
                    for s in range(STEPS):
                        i = (k * 2 + j) * STEPS + s
                        step_gates(i, 0, s)
                        if s > 0:
                            linear(i - 1, 1, s - 1, j)
                        elif not (first and j == 0):
                            linear(i - 1, 1, STEPS - 1, 1 - j)
                        step_gates(i, 1, s)
                        if s == 0:
                            pe.wait_ge(lin_added, k * 2 + j + 1)
                        linear(i, 0, s, j)

            pe.sem_inc(lin_added, 2)
            for c in range(2):
                pe.sem_inc(hid_done[c], 1)
                pe.sem_inc(gates_act[c], 4)
            body(0, first=True)
            with pe.Fori(1, W // (2 * STEPS)) as k:
                body(k)
            linear(W - 1, 1, STEPS - 1, 1)


NTAP = 9
PADW = W + 2
NOFF = 2 * NTAP
NOUT = NOFF + NTAP
GROUP = 4
TILEW = 32
NCOL = W // TILEW
NGROUP = H // GROUP
NPREP = NGROUP + 2
NTILE = NPREP * NCOL
TABROWS = GROUP * NPREP
STRIDE = TABROWS * PADW


def deformable_layer(nc, x, conv_w, pix_bias, pix_base, group_step, batch_base, identity, out_w, table):
    ROWS = GROUP + 2
    SW = PADW + 1
    TURNS = GROUP + 1
    COPIES = 2 * GROUP
    STEPS = 14
    PREP = 18 + 1 + 1 + 1
    ctx = ExitStack()
    with ctx:
        def sb(name, shape, dt=F32):
            return ctx.enter_context(nc.sbuf_tensor("l2_" + name, shape, dt))

        def sem(name):
            return ctx.enter_context(nc.semaphore("l2_" + name))

        stats = sb("stats", [P, 6 * (H * W // 512)])
        mv = sb("mv", [P, 2])
        std = sb("std", [P, 1])
        rstd = sb("rstd", [P, 1])
        shift = sb("shift", [P, 1])
        eps = sb("eps", [P, 1])
        ident = sb("ident", [P, P])
        cw = sb("cw", [P, NTAP, B * NOUT])
        pbias = sb("pbias", [P, NOUT])
        base = sb("base", [P, NCOL, NOFF])
        step4 = sb("step4", [P, NCOL, NOFF])
        bbase = sb("bbase", [P, B, NTAP])
        wout = sb("wout", [3 * C, 3, C])
        strip = sb("strip", [P, 2, ROWS, SW])
        tab = sb("tab", [PADW, 2, GROUP, B, 4 * C])
        ot = sb("ot", [B * NOUT, NCOL, P])
        raw = sb("raw", [P, NCOL, B, NOUT])
        pos = sb("pos", [P, NCOL, B, NOFF])
        posi = sb("posi", [P, NCOL, B, NOFF], I32)
        flo = sb("flo", [P, NCOL, B, NOFF])
        gt = sb("gt", [P, NCOL, B, NOFF])
        frac = sb("frac", [P, NCOL, B, NOFF])
        rest = sb("rest", [P, NCOL, B, NOFF])
        mask = sb("mask", [P, NCOL, B, NTAP])
        mx0 = sb("mx0", [P, NCOL, B, NTAP])
        mx1 = sb("mx1", [P, NCOL, B, NTAP])
        idxf = sb("idxf", [P, NCOL, B, NTAP])
        index = sb("index", [P, NTILE, B * NTAP], I32)
        weight = sb("weight", [P, NTILE, B, NTAP, 4])
        tidx = sb("tidx", [P, NCOL, B * NTAP], I32)
        RING = B
        got = sb("got", [P, RING, NTAP, 4 * C])
        red = sb("red", [P, 2, NTAP, 2 * C])
        samp = sb("samp", [P, 2, NTAP, C])
        sampt = sb("sampt", [3 * C, 2, 3, P])

        def ps(name):
            return ctx.enter_context(nc.psum_tensor("l2_" + name, [P, 512], F32))

        off_ps = ps("off")
        offt_ps = ps("offt")
        tab_ps = [ps(f"tab{i}") for i in range(2)]
        samp_ps = [ps(f"samp{i}") for i in range(2)]
        out_ps = [ps("out0"), ps("out1"), off_ps]

        consts_in = sem("consts_in")
        cw_zero = sem("cw_zero")
        pool_passed = sem("pool_passed")
        dve_prep = sem("dve_prep")
        pads_zero = sem("pads_zero")
        pads_mean = sem("pads_mean")
        eps_set = sem("eps_set")
        std_ready = sem("std_ready")
        strip_ready = sem("strip_ready")
        off_done = sem("off_done")
        off_out = sem("off_out")
        offt_done = sem("offt_done")
        raw_done = sem("raw_done")
        mask_done = sem("mask_done")
        chain = sem("chain")
        tab_turned = sem("tab_turned")
        tab_copied = sem("tab_copied")
        tab_stored = [sem(f"tab_stored{i}") for i in range(2)]
        tidx_ready = sem("tidx_ready")
        gathered = [sem(f"gathered{i}") for i in range(RING)]
        weighted = sem("weighted")
        reduced = sem("reduced")
        summed = sem("summed")
        x_added = sem("x_added")
        samp_turned = sem("samp_turned")
        sampt_ready = sem("sampt_ready")
        convolved = sem("convolved")

        x_img = x[:, HALO:HALO + H, :]
        x_pad = x[:, HALO - 1:XROWS, :]

        block = ctx.enter_context(nc.Block())

        @block.sync
        def _(sp):
            sp.wait_ge(cw_zero, 1)
            for b in range(B):
                sp.dma_start(cw[C * b:C * (b + 1), :, NOUT * b:NOUT * (b + 1)],
                             conv_w.rearrange("c (t o) -> c t o", t=NTAP)).then_inc(consts_in, 16)
            for dst, src in ((pbias[:, :], pix_bias), (base[:, :, :], pix_base.rearrange("p (c n) -> p c n", c=NCOL)),
                             (step4[:, :, :], group_step.rearrange("p (c n) -> p c n", c=NCOL)),
                             (bbase[:, :, :], batch_base.rearrange("p (b n) -> p b n", b=B)),
                             (ident[:, :], identity), (wout[:, :, :], out_w.rearrange("k (g o) -> k g o", g=3))):
                sp.dma_start(dst, src).then_inc(consts_in, 16)

            def store_table(g, j):
                sp.wait_ge(tab_copied, COPIES * (g + 2))
                for b in range(B):
                    sp.dma_start(table[b].rearrange("(r s) k -> s r k", s=PADW)[:, bass.ds(g * GROUP, GROUP), :],
                                 tab[:, j, :, b, :]).then_inc(tab_stored[j], 16)

            with sp.Fori(0, NPREP // 2) as g2:
                store_table(g2 * 2, 0)
                store_table(g2 * 2 + 1, 1)

        @block.gpsimd
        def _(pool):
            pool.memset(cw[:, :, :], 0.0).then_inc(cw_zero, 1)
            pool.memset(eps[:, :], GN_EPS).then_inc(eps_set, 1)
            pool.memset(strip[:, :, :, :], 0.0).then_inc(pads_zero, 1)
            for j in range(2):
                pool.wait_ge(tab_stored[j], 16 * B * (NPREP // 2 + 1))
            rows = table.rearrange("b r k -> (b r) k")

            with pool.Fori(0, NGROUP) as g:
                for c in range(NCOL):
                    t = g * NCOL + c
                    wait_apart(pool, tidx_ready, t + 1, pool_passed)
                    for b in range(B):
                        wait_apart(pool, reduced, t * B + b + 1, pool_passed)
                        for n in range(NTAP):
                            at = tidx[:, c, b * NTAP + n:b * NTAP + n + 1].bitcast(U32)
                            pool.indirect_dma_start(
                                out=got[:, b, n, :], out_offset=None, in_=rows,
                                in_offset=bass.IndirectOffsetOnAxis(ap=at, axis=0)).then_inc(gathered[b], 16)

        @block.scalar
        def _(act):
            act.wait_ge(eps_set, 1)
            act.wait_ge(dve_prep, 19)
            act.activation(std[:, :], mv[:, 1:2], ACT.Sqrt, bias=eps[:, :]).then_inc(std_ready, 1)
            act.wait_ge(dve_prep, PREP)
            act.wait_ge(pads_zero, 1)
            act.wait_ge(pads_mean, 2)
            act.sem_inc(off_out, 1)
            act.sem_inc(tab_copied, COPIES)
            for j in range(2):
                act.sem_inc(tab_stored[j], 16 * B)

            def prepare(g, j):
                act.wait_ge(tab_turned, TURNS * g)
                act.activation(strip[:, j, :, 1:1 + W], x_pad[:, bass.ds(g * GROUP, ROWS), :], ACT.Identity,
                               bias=shift[:, 0:1], scale=rstd[:, 0:1]).then_inc(strip_ready, 1)

            def table_rows(g2, g, j):
                act.wait_ge(tab_stored[j], 16 * B * (g2 + 1))
                for r in range(TURNS):
                    act.wait_ge(tab_turned, TURNS * (g + 1) + r + 1)
                    src = tab_ps[(j * TURNS + r) % 2][0:PADW, 0:2 * P].rearrange("p (s b c) -> p b s c", s=2, b=B)
                    if r > 0:
                        act.activation(tab[:, j, r - 1, :, 2 * C:4 * C].rearrange("p b (s c) -> p b s c", s=2), src,
                                       ACT.Copy).then_inc(tab_copied, 1)
                    if r < GROUP:
                        act.activation(tab[:, j, r, :, 0:2 * C].rearrange("p b (s c) -> p b s c", s=2), src,
                                       ACT.Copy).then_inc(tab_copied, 1)

            def offsets(g):
                act.wait_ge(off_done, g + 1)
                act.wait_ge(offt_done, g + 1)
                act.activation(ot[:, :, :], off_ps[0:B * NOUT, 0:NCOL * P].rearrange("p (c n) -> p c n", n=P),
                               ACT.Copy).then_inc(off_out, 1)

            def masks(g):
                act.wait_ge(raw_done, g + 2)
                act.wait_ge(chain, STEPS * g + 1)
                act.activation(mask[:, :, :, :], raw[:, :, :, NOFF:NOUT], ACT.Sigmoid).then_inc(mask_done, 1)

            prepare(0, 0)
            with act.Fori(0, NPREP // 2) as g2:
                for j in range(2):
                    g = g2 * 2 + j
                    prepare(g + 1, 1 - j)
                    offsets(g)
                    table_rows(g2, g, j)
                    masks(g)

            with act.Fori(0, NGROUP) as g:
                for c in range(NCOL):
                    for b in range(B):
                        u = (g * NCOL + c) * B + b
                        act.wait_ge(samp_turned, u + 1)
                        act.wait_ge(convolved, u + 1)
                        act.activation(sampt[:, b % 2, :, :], samp_ps[b % 2][0:3 * C, 0:3 * P].rearrange("p (g n) -> p g n", g=3),
                                       ACT.Copy).then_inc(sampt_ready, 1)

        @block.vector
        def _(dve):
            n = instance_stats(dve, x_img, stats, mv[:, :], dve_prep, 0)
            dve.wait_ge(std_ready, 1)
            dve.reciprocal(rstd[:, :], std[:, :]).then_inc(dve_prep, 1)
            dve.wait_ge(dve_prep, n + 1)
            dve.scalar_tensor_tensor(out=shift[:, :], in0=mv[:, 0:1], scalar=-1.0, in1=rstd[:, :],
                                     op0=ALU.mult, op1=ALU.mult).then_inc(dve_prep, 1)
            dve.tensor_scalar(x[:, 0:HALO, :], x[:, 0:HALO, :], 0.0, mv[:, 0:1], ALU.mult, ALU.add).then_inc(pads_mean, 1)
            dve.tensor_scalar(x[:, HALO + H:XROWS, :], x[:, HALO + H:XROWS, :], 0.0, mv[:, 0:1],
                              ALU.mult, ALU.add).then_inc(pads_mean, 1)
            dve.wait_ge(consts_in, 16 * 10)
            dve.sem_inc(raw_done, 1)
            dve.sem_inc(chain, 1)

            def both(one):
                return one.unsqueeze(2).to_broadcast([P, NCOL, B, one.shape[2]])

            def group_math(g):
                start = g * STEPS + 1
                k = 0

                def step(ins):
                    nonlocal k
                    ins.then_inc(chain, 1)
                    k += 1
                    dve.wait_ge(chain, start + k)

                dve.wait_ge(offt_done, g + 2)
                turned = offt_ps[:, 0:NCOL * P].rearrange("p (c n) -> p c n", n=P)[:, :, 0:B * NOUT].rearrange(
                    "p c (b o) -> p c b o", b=B)
                bias = pbias[:, :].unsqueeze(1).unsqueeze(1).to_broadcast([P, NCOL, B, NOUT])
                dve.tensor_tensor(raw[:, :, :, :], turned, bias, ALU.add).then_inc(raw_done, 1)
                dve.wait_ge(raw_done, g + 2)
                step(dve.tensor_tensor(pos[:, :, :, :], raw[:, :, :, 0:NOFF], both(base[:, :, :]), ALU.add))
                step(dve.tensor_scalar(pos[:, :, :, :], pos[:, :, :, :], 0.0, float(PADW - 1), ALU.max, ALU.min))
                step(dve.tensor_copy(posi[:, :, :, :], pos[:, :, :, :]))
                step(dve.tensor_copy(flo[:, :, :, :], posi[:, :, :, :]))
                step(dve.tensor_tensor(gt[:, :, :, :], flo[:, :, :, :], pos[:, :, :, :], ALU.is_gt))
                step(dve.tensor_tensor(flo[:, :, :, :], flo[:, :, :, :], gt[:, :, :, :], ALU.subtract))
                step(dve.tensor_tensor(frac[:, :, :, :], pos[:, :, :, :], flo[:, :, :, :], ALU.subtract))
                step(dve.tensor_scalar(rest[:, :, :, :], frac[:, :, :, :], -1.0, 1.0, ALU.mult, ALU.add))
                step(dve.scalar_tensor_tensor(out=idxf[:, :, :, :], in0=flo[:, :, :, 0:NTAP], scalar=float(PADW),
                                              in1=flo[:, :, :, NTAP:NOFF], op0=ALU.mult, op1=ALU.add))
                tiles = bass.ds(g * NCOL, NCOL)
                step(dve.tensor_tensor(index[:, tiles, :].rearrange("p c (b n) -> p c b n", b=B), idxf[:, :, :, :],
                                       bbase[:, :, :].unsqueeze(1).to_broadcast([P, NCOL, B, NTAP]), ALU.add))
                dve.wait_ge(mask_done, g + 1)
                step(dve.tensor_tensor(mx0[:, :, :, :], mask[:, :, :, :], rest[:, :, :, 0:NTAP], ALU.mult))
                step(dve.tensor_tensor(mx1[:, :, :, :], mask[:, :, :, :], frac[:, :, :, 0:NTAP], ALU.mult))
                for q, (mx, fy) in enumerate(((mx0, rest), (mx0, frac), (mx1, rest), (mx1, frac))):
                    for c in range(NCOL):
                        ins = dve.tensor_tensor(weight[:, bass.ds(g * NCOL + c, 1), :, :, q].rearrange("p o b n -> p (o b) n"),
                                                mx[:, c], fy[:, c, :, NTAP:NOFF], ALU.mult)
                step(ins)
                step(dve.tensor_tensor(base[:, :, :], base[:, :, :], step4[:, :, :], ALU.add))
                assert k == STEPS

            with dve.Fori(0, NPREP) as g:
                group_math(g)

            dve.sem_inc(reduced, RING)
            done = STEPS * NPREP + 1

            def tile_index(t, c):
                dve.tensor_copy(tidx[:, c, :], index[:, bass.ds(t, 1), :].rearrange("p o n -> p (o n)")).then_inc(tidx_ready, 1)

            def unit(t, c, b):
                u = t * B + b
                dve.wait_ge(gathered[b], 16 * NTAP * (t + 1))
                corners = got[:, b, :, :].rearrange("p n (k c) -> p (n k) c", c=C)
                w = weight[:, bass.ds(t, 1), b, :, :].rearrange("p o n k -> p (o n k)").unsqueeze(2).to_broadcast([P, NTAP * 4, C])
                dve.tensor_tensor(corners, corners, w, ALU.mult).then_inc(weighted, 1)
                dve.wait_ge(weighted, u + 1)
                dve.tensor_tensor(red[:, b % 2], got[:, b, :, 0:2 * C], got[:, b, :, 2 * C:4 * C], ALU.add).then_inc(reduced, 1)
                dve.wait_ge(reduced, u + 1 + RING)
                dve.tensor_tensor(samp[:, b % 2], red[:, b % 2, :, 0:C], red[:, b % 2, :, C:2 * C], ALU.add).then_inc(summed, 1)

            tile_index(0, 0)
            with dve.Fori(0, NGROUP) as g:
                for c in range(NCOL):
                    t = g * NCOL + c
                    tile_index(t + 1, (c + 1) % NCOL)
                    for b in range(B):
                        if b >= 2:
                            dve.wait_ge(samp_turned, t * B + b - 1)
                        unit(t, c, b)
                    dve.wait_ge(convolved, t * B + B + 2)
                    rows = x_img[:, bass.ds(g * GROUP, GROUP), TILEW * c:TILEW * (c + 1)]
                    dve.tensor_tensor(rows, out_ps[c][:, 0:P].rearrange("p (h w) -> p h w", w=TILEW), rows,
                                      ALU.add).then_inc(x_added, 1)

        @block.tensor
        def _(pe):
            pe.wait_ge(consts_in, 16 * 10)
            pe.wait_ge(dve_prep, PREP)
            pe.sem_inc(tab_turned, TURNS)
            pe.sem_inc(offt_done, 1)

            def group(g, j):
                pe.wait_ge(strip_ready, g + 1)
                pe.wait_ge(off_out, g + 1)
                dst = off_ps[0:B * NOUT, 0:NCOL * P]
                for tap in range(NTAP):
                    dy, dx = tap // 3, tap % 3
                    src = strip[:, j, dy:dy + GROUP, dx:dx + W].rearrange("p h (c w) -> p c h w", w=TILEW)
                    mm = pe.matmul(dst, cw[:, tap, :], src, start=(tap == 0), stop=(tap == NTAP - 1))
                mm.then_inc(off_done, 1)
                for r in range(TURNS):
                    pe.wait_ge(tab_copied, COPIES * g + (7, 8, 9, 11, 13)[r])
                    for s in range(2):
                        mm = pe.transpose(tab_ps[(j * TURNS + r) % 2][0:PADW, P * s:P * (s + 1)],
                                          strip[:, j, r, s:s + PADW], ident[:, :])
                    mm.then_inc(tab_turned, 1)
                pe.wait_ge(off_out, g + 2)
                pe.wait_ge(raw_done, g + 1)
                for c in range(NCOL):
                    mm = pe.transpose(offt_ps[:, P * c:P * c + B * NOUT], ot[:, c, :], ident[0:B * NOUT, 0:B * NOUT])
                mm.then_inc(offt_done, 1)

            with pe.Fori(0, NPREP // 2) as g2:
                group(g2 * 2, 0)
                group(g2 * 2 + 1, 1)

            pe.sem_inc(convolved, 2)
            with pe.Fori(0, NGROUP) as g:
                for c in range(NCOL):
                    t = g * NCOL + c
                    for b in range(B):
                        u = t * B + b
                        pe.wait_ge(summed, u + 1)
                        for q in range(3):
                            mm = pe.transpose(samp_ps[b % 2][0:3 * C, P * q:P * (q + 1)],
                                              samp[:, b % 2, 3 * q:3 * q + 3, :].rearrange("p n c -> p (n c)"), ident[:, :])
                        mm.then_inc(samp_turned, 1)
                        pe.wait_ge(sampt_ready, u + 1)
                        for q in range(3):
                            mm = pe.matmul(out_ps[c][C * b:C * (b + 1), 0:P], wout[:, q, :], sampt[:, b % 2, q, :],
                                           start=(q == 0), stop=(q == 2))
                        mm.then_inc(convolved, 1)


def block_transform_layer(nc, x, m_left, m_right, same_block, identity, out):
    BS = 8
    PAIR = 2 * BS
    NPAIR = W // PAIR
    NROW = H // BS
    FIRST = 4
    PREP = 18 + 1 + 1 + 1 + 2
    ctx = ExitStack()
    with ctx:
        def sb(name, shape, dt=F32):
            return ctx.enter_context(nc.sbuf_tensor("l3_" + name, shape, dt))

        def sem(name):
            return ctx.enter_context(nc.semaphore("l3_" + name))

        stats = sb("stats", [P, 6 * (H * W // 512)])
        mv = sb("mv", [P, 2])
        std = sb("std", [P, 1])
        rstd = sb("rstd", [P, 1])
        shift = sb("shift", [P, 1])
        eps = sb("eps", [P, 1])
        ml = sb("ml", [P, P])
        mr = sb("mr", [P, P])
        same = sb("same", [P, P])
        kron = sb("kron", [P, P])
        ident = sb("ident", [P, P])
        xr = sb("xr", [P, 2, NPAIR, P])
        xt = sb("xt", [P, 2, NPAIR, P])
        t_ps = [[ctx.enter_context(nc.psum_tensor(f"l3_t{j}{i}", [P, 512], F32)) for i in range(2)] for j in range(2)]
        o_ps = [[ctx.enter_context(nc.psum_tensor(f"l3_o{j}{i}", [P, 512], F32)) for i in range(2)] for j in range(2)]

        consts_in = sem("consts_in")
        dve_prep = sem("dve_prep")
        eps_set = sem("eps_set")
        std_ready = sem("std_ready")
        row_normed = sem("row_normed")
        row_turned = sem("row_turned")
        turned_out = sem("turned_out")
        row_multiplied = sem("row_multiplied")
        row_added = sem("row_added")
        stored = sem("stored")

        x_img = x[:, HALO:HALO + H, :]
        x_below = x[:, HALO:XROWS, :]
        out_rows = out.rearrange("b c h w -> (b c) h w")
        HALVES = ((0, FIRST), (FIRST, NPAIR))

        block = ctx.enter_context(nc.Block())

        @block.sync
        def _(sp):
            for dst, src in ((ml, m_left), (mr, m_right), (same, same_block), (ident, identity)):
                sp.dma_start(dst[:, :], src).then_inc(consts_in, 16)
            with sp.Fori(0, NROW) as r:
                sp.wait_ge(row_added, 2 * r + 6)
                sp.dma_start(out_rows[:, bass.ds(r * BS, BS), :], x_img[:, bass.ds(r * BS, BS), :]).then_inc(stored, 16)
            sp.wait_ge(stored, 16 * NROW)

        @block.gpsimd
        def _(pool):
            pool.memset(eps[:, :], GN_EPS).then_inc(eps_set, 1)

        @block.scalar
        def _(act):
            act.wait_ge(eps_set, 1)
            act.wait_ge(dve_prep, 19)
            act.activation(std[:, :], mv[:, 1:2], ACT.Sqrt, bias=eps[:, :]).then_inc(std_ready, 1)
            act.wait_ge(dve_prep, PREP)

            def normalise(r, j):
                act.wait_ge(row_turned, r + 1)
                rows = x_below[:, bass.ds(r * BS, BS), :].rearrange("p h (c w) -> p c h w", w=PAIR)
                act.activation(xr[:, j].rearrange("p c (h w) -> p c h w", w=PAIR), rows, ACT.Identity, bias=shift[:, 0:1],
                               scale=rstd[:, 0:1]).then_inc(row_normed, 1)

            def evacuate(r, j):
                act.wait_ge(row_turned, r + 3)
                act.wait_ge(row_multiplied, r + 1)
                for i, (a, b) in enumerate(HALVES):
                    act.activation(xt[:, j, a:b, :], t_ps[j][i][:, 0:P * (b - a)].rearrange("p (c n) -> p c n", n=P),
                                   ACT.Copy).then_inc(turned_out, 1)

            normalise(0, 0)
            with act.Fori(0, NROW // 2) as pair:
                r = pair * 2
                normalise(r + 1, 1)
                evacuate(r, 0)
                normalise(r + 2, 0)
                evacuate(r + 1, 1)

        @block.vector
        def _(dve):
            n = instance_stats(dve, x_img, stats, mv[:, :], dve_prep, 0)

            def then(ins):
                nonlocal n
                ins.then_inc(dve_prep, 1)
                n += 1
                dve.wait_ge(dve_prep, n)

            dve.wait_ge(std_ready, 1)
            then(dve.reciprocal(rstd[:, :], std[:, :]))
            then(dve.scalar_tensor_tensor(out=shift[:, :], in0=mv[:, 0:1], scalar=-1.0, in1=rstd[:, :],
                                          op0=ALU.mult, op1=ALU.mult))
            dve.wait_ge(consts_in, 64)
            then(dve.tensor_tensor(kron[:, :], ml[:, :], mr[:, :], ALU.mult))
            then(dve.tensor_tensor(kron[:, :], kron[:, :], same[:, :], ALU.mult))
            assert n == PREP
            dve.sem_inc(row_added, 4)

            def add(r, j):
                dve.wait_ge(row_multiplied, r + 3)
                for i, (a, b) in enumerate(HALVES):
                    rows = x_img[:, bass.ds(r * BS, BS), PAIR * a:PAIR * b].rearrange("p h (c w) -> p c h w", w=PAIR)
                    ps = o_ps[j][i][:, 0:P * (b - a)].rearrange("p (c h w) -> p c h w", h=BS, w=PAIR)
                    dve.wait_ge(row_normed, r + 1)
                    dve.tensor_tensor(rows, ps, rows, ALU.add).then_inc(row_added, 1)

            with dve.Fori(0, NROW // 2) as pair:
                r = pair * 2
                add(r, 0)
                add(r + 1, 1)

        @block.tensor
        def _(pe):
            pe.wait_ge(dve_prep, PREP)
            pe.wait_ge(consts_in, 64)
            pe.sem_inc(row_turned, 2)
            pe.sem_inc(row_multiplied, 2)
            pe.sem_inc(turned_out, 4)

            def turn(r, j):
                pe.wait_ge(row_normed, r + 1)
                pe.wait_ge(turned_out, 2 * r + 2)
                for c in range(NPAIR):
                    i = c // FIRST
                    mm = pe.transpose(t_ps[j][i][:, P * (c - FIRST * i):P * (c - FIRST * i + 1)],
                                      xr[:, j, c, :], ident[:, :])
                mm.then_inc(row_turned, 1)

            def multiply(r, j):
                pe.wait_ge(turned_out, 2 * r + 6)
                pe.wait_ge(row_added, 2 * r + 2)
                for c in range(NPAIR):
                    i = c // FIRST
                    mm = pe.matmul(o_ps[j][i][:, P * (c - FIRST * i):P * (c - FIRST * i + 1)],
                                   xt[:, j, c, :], kron[:, :], start=True, stop=True)
                mm.then_inc(row_multiplied, 1)

            turn(0, 0)
            with pe.Fori(0, NROW // 2) as pair:
                r = pair * 2
                turn(r + 1, 1)
                multiply(r, 0)
                turn(r + 2, 0)
                multiply(r + 1, 1)


def network(nc, x_in, l0, l1, l2, l3, out):
    table = nc.dram_tensor("sample_table", [B, STRIDE, 4 * C], F32, kind="Internal").ap()
    k_parts = nc.dram_tensor("k_parts", [2, P, NTERM, NB * KEYS], BF16, kind="Internal").ap()
    q_parts = nc.dram_tensor("q_parts", [2, P, NTERM, NB * 2 * QS], BF16, kind="Internal").ap()
    with ExitStack() as ctx:
        x = ctx.enter_context(nc.sbuf_tensor("x", [P, XROWS, W], F32))
        x_loaded = ctx.enter_context(nc.semaphore("x_loaded"))
        pads_set = ctx.enter_context(nc.semaphore("pads_set"))
        with nc.Block() as block:
            @block.gpsimd
            def _(pool):
                pool.memset(x[:, 0:HALO, :], 0.0).then_inc(pads_set, 1)
                pool.memset(x[:, HALO + H:XROWS, :], 0.0).then_inc(pads_set, 1)
                pool.wait_ge(pads_set, 2)

            @block.sync
            def _(sp):
                sp.dma_start(x[:, HALO:HALO + H, :], x_in.rearrange("b c h w -> (b c) h w")).then_inc(x_loaded, 16)
                sp.wait_ge(x_loaded, 16)
        halo_attention_layer(nc, x, *l0, k_parts, q_parts)
        lstm_layer(nc, x, *l1)
        deformable_layer(nc, x, *l2, table)
        block_transform_layer(nc, x, *l3, out)


def kernel(**inputs):
    import numpy as np
    import concourse.bacc as bacc
    from concourse.bass_utils import run_bass_kernel_spmd

    a = {k: np.asarray(v) for k, v in inputs.items()}
    nc = bacc.Bacc("TRN2", target_bir_lowering=False, num_devices=1)
    arrays = {}

    def put(name, array):
        array = np.ascontiguousarray(array)
        arrays[name] = array
        return nc.dram_tensor(name, array.shape, mybir.dt.from_np(array.dtype), kind="ExternalInput").ap()

    identity = put("identity", np.eye(P, dtype=np.float32))
    p = np.arange(P)

    w_qkv = a["L0_conv_w_qkv"]
    rel_h = np.broadcast_to(a["L0_conv_rel_h"][0], (WIN, WIN, D // 2))
    rel_w = np.broadcast_to(a["L0_conv_rel_w"][0], (WIN, WIN, D // 2))
    rel = np.concatenate([rel_h, rel_w], axis=-1).transpose(2, 0, 1).reshape(D, KEYS)
    head_mask = np.where((p[:, None] % C // D) % 2 == np.arange(2), D ** -0.5, 0.0).astype(np.float32)
    head_rows = np.zeros((HEADS, C // D, D, 2, HEADS, D), np.float32)
    for h in range(HEADS):
        for k in range(2):
            head_rows[h, k, :, k, h, :] = np.eye(D)
    l0 = [put("w_q", w_qkv[0:C].T), put("w_k", w_qkv[C:2 * C].T), put("w_v", w_qkv[2 * C:3 * C].T),
          put("rel", np.tile(rel, (P // D, 1))), put("head_mask", head_mask),
          put("head_rows", head_rows.reshape(P, 2 * C)), identity]

    hid = a["L1_conv_W_hh"].shape[1]
    l1 = [put("w_ih", np.tile(a["L1_conv_W_ih"].T, (B, 1))), put("w_hh", a["L1_conv_W_hh"].T),
          put("b_ih", a["L1_conv_b_ih"].reshape(4, hid).T), put("b_hh", a["L1_conv_b_hh"].reshape(4, hid).T),
          put("w_lin", a["L1_conv_W_lin"].T), put("b_lin", np.tile(a["L1_conv_b_lin"], B)[:, None])]

    conv_w = np.concatenate([a["L2_conv_p_w"], a["L2_conv_m_w"]]).transpose(1, 2, 3, 0).reshape(C, NTAP * NOUT)
    bias = np.broadcast_to(np.concatenate([a["L2_conv_p_b"], a["L2_conv_m_b"]]), (P, NOUT))
    base = np.zeros((P, NCOL, 2, NTAP), np.float32)
    tap = np.arange(NTAP)
    base[:, :, 0, :] = 1 + (p // TILEW)[:, None, None] + (tap // 3 - 1)
    base[:, :, 1, :] = 1 + (p % TILEW)[:, None, None] + TILEW * np.arange(NCOL)[:, None] + (tap % 3 - 1)
    step = np.zeros((P, NCOL, 2, NTAP), np.float32)
    step[:, :, 0, :] = GROUP
    batch_base = np.broadcast_to(np.repeat(np.arange(B) * STRIDE, NTAP).astype(np.float32), (P, B * NTAP))
    out_w = a["L2_conv_conv_w"].transpose(2, 3, 1, 0).reshape(3, 3 * C, C).transpose(1, 0, 2).reshape(3 * C, 3 * C)
    l2 = [put("conv_w", conv_w), put("pix_bias", bias), put("pix_base", base.reshape(P, NCOL * NOFF)),
          put("group_step", step.reshape(P, NCOL * NOFF)), put("batch_base", batch_base), identity, put("out_w", out_w)]

    m = a["L3_conv_M"]
    bs = m.shape[0]
    full = (bs, 2, bs, bs, 2, bs)
    l3 = [put("m_left", np.broadcast_to(m.T[:, None, None, :, None, None], full).reshape(P, P)),
          put("m_right", np.broadcast_to(m.T[None, None, :, None, None, :], full).reshape(P, P)),
          put("same_block", np.broadcast_to(np.eye(2, dtype=np.float32)[None, :, None, None, :, None], full).reshape(P, P)),
          identity]

    x_in = put("x_in", a["x"])
    out = nc.dram_tensor("out", list(a["x"].shape), F32, kind="ExternalOutput").ap()
    network(nc, x_in, l0, l1, l2, l3, out)
    result = run_bass_kernel_spmd(nc, [arrays], core_ids=[0])
    return result.results[0]["out"]
```

```python
from contextlib import ExitStack
import concourse.bass as bass
from concourse import mybir

F32 = mybir.dt.float32
BF16 = mybir.dt.bfloat16
I32 = mybir.dt.int32
U32 = mybir.dt.uint32
ALU = mybir.AluOpType
ACT = mybir.ActivationFunctionType
AX = mybir.AxisListType

P = 128
B, C, H, W = 4, 32, 96, 96
HALO = 3
XROWS = HALO + H + 21
GN_EPS = 1e-5
XPARTS = 3
STATS = 24


def instance_stats(eng, x_rows, stats, mean_var, sem, loaded):
    flat = x_rows.rearrange("p h w -> p (h w)")
    n = H * W // 512
    for i in range(n):
        if i % (n // len(loaded)) == 0:
            eng.wait_ge(loaded[i // (n // len(loaded))], 16)
        eng.bn_stats(stats[:, 6 * i:6 * i + 6], flat[:, 512 * i:512 * (i + 1)]).then_inc(sem, 1)
    eng.wait_ge(sem, n)
    eng.bn_aggr(mean_var, stats[:, 0:6 * n]).then_inc(sem, 1)
    return n + 1


def known_stats(eng, pieces, mean_var, sem):
    eng.bn_aggr(mean_var, pieces[:, :]).then_inc(sem, 1)
    return 1


def is_first(i):
    return isinstance(i, int) and i == 0


def wait_apart(eng, sem, value, passed):
    eng.wait_ge(sem, value)
    eng.sem_inc(passed, 1)


BLOCK = 8
WIN = BLOCK + 2 * HALO
HEADS = 4
D = C // HEADS
NB = 6
KEYS = WIN * WIN
HKEYS = KEYS // 2
QS = BLOCK * BLOCK
NHB = H // BLOCK
SCOLS = NB * BLOCK + 2 * HALO
NTERM = 6
ROWS = NTERM * 2 * D
NFILL = 6
MISC = 13


def halo_attention_layer(nc, x_in, x, w_q, w_k, w_v, rel, head_mask, head_rows, identity, k_parts, q_parts,
                         stats_out):
    ctx = ExitStack()
    with ctx:
        def sb(name, shape, dt=F32):
            return ctx.enter_context(nc.sbuf_tensor("l0_" + name, shape, dt))

        def sem(name):
            return ctx.enter_context(nc.semaphore("l0_" + name))

        stats = sb("stats", [P, 6 * (H * W // 512)])
        mv = sb("mv", [P, 2])
        std = sb("std", [P, 1])
        rstd = sb("rstd", [P, 1])
        shift = sb("shift", [P, 1])
        eps = sb("eps", [P, 1])
        wq = sb("wq", [P, P])
        wk = sb("wk", [P, P])
        wv = sb("wv", [P, P])
        relb = sb("relb", [P, WIN, WIN])
        hmask = sb("hmask", [P, 2])
        ident = sb("ident", [P, P])
        strip = sb("strip", [P, 2, WIN, SCOLS])
        xwin = sb("xwin", [P, 2, NB, KEYS])
        k32 = sb("k32", [P, NB, KEYS])
        kp = sb("kp", [P, 3, NB, KEYS], BF16)
        q32 = sb("q32", [P, NB, 2, QS])
        qp = sb("qp", [P, 3, NB, 2, QS], BF16)
        kst = sb("kst", [P, 2, 2, 2, 2, NB, KEYS], BF16)
        qst = sb("qst", [P, 2, 2, 2, 2, NB, 2, QS], BF16)
        v = sb("v", [HKEYS, 2, NB * 2, B, HEADS, 2 * D])
        pt = sb("pt", [HKEYS, 2, 2, 2, 2, 2 * QS])
        mx = sb("mx", [P, 2, 2, NB])
        mparts = sb("mparts", [2 * NB, 2, 2, P], BF16)
        osb = sb("osb", [P, 2, B, BLOCK * NB * BLOCK])
        hrows = sb("hrows", [P, 2, C])
        sums_in = sb("sums_in", [P, 2, 2, BLOCK * NB * BLOCK // 2])

        def ps(name):
            return ctx.enter_context(nc.psum_tensor("l0_" + name, [P, 512], F32))

        s_ps = [ps(f"s{i}") for i in range(2)]
        st_ps = [ctx.enter_context(nc.psum_tensor(f"l0_st{i}", [P, 1024], F32)) for i in range(2)]
        pv_ps = ps("pv")
        misc_ps = ps("misc")

        x_loaded = [sem(f"x_loaded{i}") for i in range(XPARTS)]
        x_pads_zero = sem("x_pads_zero")
        consts_in = sem("consts_in")
        w_zero = sem("w_zero")
        pool_passed = sem("pool_passed")
        sp_passed = sem("sp_passed")
        fills_set = sem("fills_set")
        pv_zero = sem("pv_zero")
        eps_set = sem("eps_set")
        dve_prep = sem("dve_prep")
        pads_mean = sem("pads_mean")
        std_ready = sem("std_ready")
        strip_ready = sem("strip_ready")
        win_ready = sem("win_ready")
        misc_done = sem("misc_done")
        misc_read = sem("misc_read")
        k32_ready = sem("k32_ready")
        q32_ready = sem("q32_ready")
        q_part = sem("q_part")
        k_rest = sem("k_rest")
        q_rest = sem("q_rest")
        k_split = sem("k_split")
        q_split = sem("q_split")
        v_ready = sem("v_ready")
        parts_stored = sem("parts_stored")
        stacked = [[sem(f"stacked{i}{j}") for j in range(2)] for i in range(2)]
        s_filled = sem("s_filled")
        s_read = sem("s_read")
        m_split = sem("m_split")
        m_placed = [sem(f"m_placed{i}") for i in range(B)]
        st_done = sem("st_done")
        exp_done = sem("exp_done")
        pv_done = sem("pv_done")
        pv_read = sem("pv_read")
        sums_in_done = sem("sums_in_done")
        recip_done = sem("recip_done")
        quot_done = sem("quot_done")
        x_added = sem("x_added")
        rows_counted = sem("rows_counted")

        EARLY = 13
        LOADS = 2
        STORES = 6
        USES = ([("q", 0), ("k", 0), ("k", 1)], [("k", 2), ("o", 0)], [("o", 1), ("v", 0)], [("v", 1), ("v", 2)])
        K_TERMS = (slice(0, 3), slice(3, 5), slice(5, 6))
        Q_TERMS = (slice(0, 3), slice(3, 5), slice(5, 6))
        x_img = x[:, HALO:HALO + H, :]

        def use_number(G, b, s):
            order = [u for u in (0, 1, "max", 2) if u == "max" or u < len(USES[b])]
            return G * MISC + (EARLY + sum(1 + len(USES[a]) for a in range(b)) + order.index(s))

        def last_use(b, s):
            b, s = (b, s - 1) if s else ((b - 1) % B, 2)
            return (b, s, *USES[b][s]) if s < len(USES[b]) else None

        block = ctx.enter_context(nc.Block())

        @block.sync
        def _(sp):
            rows_of = x_in.rearrange("b c h w -> (b c) h w")
            for i in range(XPARTS):
                rows = slice(H // XPARTS * i, H // XPARTS * (i + 1))
                sp.dma_start(x_img[:, rows, :], rows_of[:, rows, :]).then_inc(x_loaded[i], 16)
            sp.wait_ge(w_zero, 3)
            for b in range(B):
                for dst, src in ((wq, w_q), (wk, w_k), (wv, w_v)):
                    sp.dma_start(dst[C * b:C * (b + 1), C * b:C * (b + 1)], src).then_inc(consts_in, 16)
            for dst, src in ((relb[:, :, :].rearrange("p i j -> p (i j)"), rel), (hmask[:, :], head_mask), (ident[:, :], identity),
                             (hrows[:, :, :].rearrange("p k c -> p (k c)"), head_rows)):
                sp.dma_start(dst, src).then_inc(consts_in, 16)

            def store_k(G, half, i):
                sp.wait_ge(k_split, 3 * G + i + 1)
                terms = K_TERMS[i]
                sp.dma_start(k_parts[half, :, terms, :],
                             kp[:, i].rearrange("p b n -> p (b n)").unsqueeze(1).to_broadcast(
                                 [P, terms.stop - terms.start, NB * KEYS])).then_inc(parts_stored, 16)

            def store_q(G, half):
                sp.wait_ge(q_split, G + 1)
                for terms in Q_TERMS:
                    sp.dma_start(q_parts[half, :, terms, :],
                                 qp[:, 0:terms.stop - terms.start].rearrange("p i b s q -> p i (b s q)")).then_inc(parts_stored, 16)

            def load_stacks(G, half, load, used):
                wait_apart(sp, parts_stored, 16 * STORES * (G + 1), sp_passed)
                if used is not None:
                    sp.wait_ge(st_done, used)
                rows = slice(P // 2 * load, P // 2 * (load + 1))
                for stacks, parts in ((kst[0:ROWS, half, load].rearrange("p b a k n -> p (b a) (k n)"), k_parts),
                                      (qst[0:ROWS, half, load].rearrange("p b a k s q -> p (b a) (k s q)"), q_parts)):
                    sp.dma_start(stacks, parts[half, rows].rearrange("(g r) t n -> (r t) g n", r=2 * D)).then_inc(
                        stacked[half][load], 16)

            def place_maxima(U, par, half, b):
                sp.wait_ge(m_split, 2 * U + 2)
                for i in range(2):
                    sp.dma_start(qst[ROWS + i:ROWS + i + 1, half, b // 2, b % 2],
                                 mparts[0:2 * NB, par, i, :]).then_inc(m_placed[b], 16)

            for G in range(2):
                for i in range(3):
                    store_k(G, G, i)
                store_q(G, G)
                for load in range(2 - G):
                    load_stacks(G, G, load, None)
                if G == 0:
                    for U in range(2):
                        place_maxima(U, U, 0, U)
            with sp.Fori(0, NHB) as hb:
                for half in range(2):
                    G = hb * 2 + half
                    for b in range(B):
                        U = G * B + b
                        if b == 2:
                            for load in range(2):
                                wait_apart(sp, stacked[half][load], 16 * LOADS * (hb + 1), sp_passed)
                            store_k(G + 2, half, 0)
                        if b == 3:
                            store_k(G + 2, half, 1)
                            store_q(G + 2, half)
                        place_maxima(U + 2, b % 2, (half + (b + 2) // B) % 2, (b + 2) % B)
                        if b == 0:
                            load_stacks(G + 1, 1 - half, 1, G * 12 + 1)
                    store_k(G + 2, half, 2)
                    load_stacks(G + 2, half, 0, G * 12 + 7)
            for half in range(2):
                for load in range(2):
                    sp.wait_ge(stacked[half][load], 16 * LOADS * (NHB + (half + load < 2)))
            for b in range(B):
                sp.wait_ge(m_placed[b], 32 * (2 * NHB + (b < 2)))
            sp.wait_ge(parts_stored, 16 * STORES * (2 * NHB + 2))

        @block.gpsimd
        def _(pool):
            for rows in (slice(0, HALO), slice(HALO + H, XROWS)):
                pool.memset(x[:, rows, :], 0.0).then_inc(x_pads_zero, 1)
            for w in (wq, wk, wv):
                pool.memset(w[:, :], 0.0).then_inc(w_zero, 1)
            pool.memset(eps[:, :], GN_EPS).then_inc(eps_set, 1)
            pool.memset(strip[:, :, :, :], 0.0).then_inc(fills_set, 1)
            pool.memset(v[:, :, :, :, :, :], 1.0).then_inc(fills_set, 1)
            pool.wait_ge(fills_set, 2)
            pool.memset(kst[ROWS:ROWS + 2].rearrange("p h l b a k n -> p (h l b a k n)"), 1.0).then_inc(fills_set, 1)
            pool.wait_ge(fills_set, 3)
            pool.memset(osb[:, 1], 1.0).then_inc(fills_set, 1)

            def windows(G, half):
                wait_apart(pool, strip_ready, G + 1, pool_passed)
                for blk in range(NB):
                    ins = pool.tensor_copy(xwin[:, half, blk, :].rearrange("p (i j) -> p i j", j=WIN),
                                           strip[:, half, :, BLOCK * blk:BLOCK * blk + WIN])
                ins.then_inc(win_ready, 1)

            def splits(G):
                if not is_first(G):
                    pool.wait_ge(parts_stored, 16 * STORES * G)
                wait_apart(pool, k32_ready, 3 * G + 3, pool_passed)
                pool.tensor_copy(kp[:, 0], k32[:, :, :]).then_inc(k_split, 1)
                pool.wait_ge(q_part, 2 * G + 1)
                pool.tensor_tensor(q32[:, :, :, :], q32[:, :, :, :], qp[:, 0], ALU.subtract).then_inc(q_rest, 1)
                pool.wait_ge(k_split, 3 * G + 1)
                pool.tensor_tensor(k32[:, :, :], k32[:, :, :], kp[:, 0], ALU.subtract).then_inc(k_rest, 1)
                pool.wait_ge(q_part, 2 * G + 2)
                pool.tensor_tensor(qp[:, 2], q32[:, :, :, :], qp[:, 1], ALU.subtract).then_inc(q_split, 1)
                pool.wait_ge(k_split, 3 * G + 2)
                pool.tensor_tensor(kp[:, 2], k32[:, :, :], kp[:, 1], ALU.subtract).then_inc(k_split, 1)

            for G in range(2):
                windows(G, G)
                splits(G)
            pool.wait_ge(misc_done, 7)
            windows(2, 0)
            pool.sem_inc(x_added, 3)

            def add_attention(hb, G, half, i):
                if i == 0:
                    pool.wait_ge(strip_ready, G + 4 - half)
                pool.wait_ge(recip_done, 2 * G + i + 3)
                pool.tensor_tensor(sums_in[:, i, 0, :], sums_in[:, i, 0, :], sums_in[:, i, 1, :], ALU.mult).then_inc(quot_done, 1)
                pool.wait_ge(quot_done, 2 * G + i + 1)
                rows = x_img[:, bass.ds(hb * BLOCK + i * (BLOCK // 2), BLOCK // 2), NB * BLOCK * half:NB * BLOCK * (half + 1)]
                pool.tensor_tensor(rows, sums_in[:, i, 0, :].rearrange("p (i c) -> p i c", i=BLOCK // 2), rows,
                                   ALU.add).then_inc(x_added, 1)
                pool.wait_ge(x_added, 2 * G + i + 4)

            def body(hb, first=False):
                for half in range(2):
                    G = hb * 2 + half
                    splits(G + 2)
                    if not (first and half == 0):
                        for i in range(2):
                            add_attention(hb - (1 - half), G - 1, 1 - half, i)
                    pool.wait_ge(misc_done, use_number(G, 3, 1) + 1)
                    windows(G + 3, 1 - half)

            body(0, first=True)
            with pool.Fori(1, NHB) as hb:
                body(hb)
            for i in range(2):
                add_attention(NHB - 1, 2 * NHB - 1, 1, i)

        @block.scalar
        def _(act):
            act.wait_ge(eps_set, 1)
            act.wait_ge(dve_prep, 19)
            act.activation(std[:, :], mv[:, 1:2], ACT.Sqrt, bias=eps[:, :]).then_inc(std_ready, 1)
            act.wait_ge(consts_in, 16 * 16)
            act.sem_inc(exp_done, 1)
            act.sem_inc(misc_read, 1)

            def part_k(G):
                act.wait_ge(k_rest, G + 1)
                act.activation(kp[:, 1], k32[:, :, :], ACT.Copy).then_inc(k_split, 1)

            def part_q(G, i):
                if i == 0:
                    if not is_first(G):
                        act.wait_ge(parts_stored, 16 * STORES * G)
                    act.wait_ge(q32_ready, 2 * G + 2)
                else:
                    act.wait_ge(q_rest, G + 1)
                act.activation(qp[:, i], q32[:, :, :, :], ACT.Copy).then_inc(q_part, 1)

            def read_q(G, n):
                act.wait_ge(misc_done, n + 1)
                if not is_first(G):
                    act.wait_ge(q_split, G)
                for slot in range(2):
                    ins = act.activation(q32[:, :, slot, :], misc_ps[:, 0:NB * QS].rearrange("p (k q) -> p k q", q=QS),
                                         ACT.Copy, scale=hmask[:, slot:slot + 1])
                    ins.then_inc(q32_ready, 1)
                act.wait_ge(q32_ready, 2 * G + 2)
                act.sem_inc(misc_read, 1)

            def read_v(G, half, i, n):
                act.wait_ge(misc_done, n + 1)
                act.wait_ge(fills_set, 4)
                if not isinstance(G, int):
                    act.wait_ge(pv_done, G * 12 - 11)
                act.activation(v[:, half, 4 * i:4 * i + 4, :, :, 0:D].rearrange("p t b h d -> p t (b h) d"),
                               misc_ps[0:HKEYS, :].rearrange("p (t m d) -> p t m d", t=4, d=D), ACT.Copy).then_inc(v_ready, 1)
                act.wait_ge(v_ready, 3 * G + i + 1)
                act.sem_inc(misc_read, 1)

            def read_o(G, i, n):
                act.wait_ge(misc_done, n + 1)
                act.wait_ge(x_added, 2 * G + 1)
                act.activation(sums_in[:, i].rearrange("p k n -> p (k n)"), misc_ps[:, 0:NB * QS], ACT.Copy).then_inc(sums_in_done, 1)
                act.wait_ge(sums_in_done, 2 * G + i + 1)
                act.sem_inc(misc_read, 1)

            def exps(st, slot):
                act.wait_ge(st_done, st + 2)
                act.wait_ge(pv_done, st)
                act.activation(pt[:, slot].rearrange("p k a c n -> p (k a c n)"), st_ps[slot][0:HKEYS, :], ACT.Exp).then_inc(exp_done, 1)

            read_q(0, 3)
            part_q(0, 0)
            for i in range(3):
                read_v(0, 0, i, 4 + i)
            part_q(0, 1)
            part_k(0)
            read_q(1, 10)
            part_q(1, 0)
            part_q(1, 1)
            part_k(1)
            PART_AT = {(0, 2): ("q", 0), (2, 1): ("q", 1), (2, 2): ("k", 1)}
            with act.Fori(0, NHB) as hb:
                for half in range(2):
                    G = hb * 2 + half
                    for b in range(B):
                        for s in range(3):
                            exps((G * B + b) * 3 + s, (b + s) % 2)
                            if last_use(b, s):
                                ub, us, kind, i = last_use(b, s)
                                if kind == "v":
                                    read_v(G + 1, 1 - half, i, use_number(G, ub, us))
                                if kind == "q":
                                    read_q(G + 2, use_number(G, ub, us))
                                if kind == "o":
                                    read_o(G, i, use_number(G, ub, us))
                            if (b, s) in PART_AT:
                                part, i = PART_AT[b, s]
                                part_k(G + 2) if part == "k" else part_q(G + 2, i)
            for i in range(2):
                read_o(2 * NHB, i, 2 * NHB * MISC + EARLY + i)

        @block.vector
        def _(dve):
            dve.memset(pv_ps[:, :], 0.0).then_inc(pv_zero, 1)
            n = instance_stats(dve, x_img, stats, mv[:, :], dve_prep, x_loaded)
            dve.wait_ge(std_ready, 1)
            dve.wait_ge(dve_prep, n)
            dve.reciprocal(rstd[:, :], std[:, :]).then_inc(pads_mean, 1)
            dve.wait_ge(pads_mean, 1)
            dve.scalar_tensor_tensor(out=shift[:, :], in0=mv[:, 0:1], scalar=-1.0, in1=rstd[:, :],
                                     op0=ALU.mult, op1=ALU.mult).then_inc(pads_mean, 1)
            dve.wait_ge(x_pads_zero, 2)
            for rows in (slice(0, HALO), slice(HALO + H, XROWS)):
                dve.tensor_scalar(x[:, rows, :], x[:, rows, :], 0.0, mv[:, 0:1], ALU.mult, ALU.add).then_inc(pads_mean, 1)
            dve.wait_ge(consts_in, 16 * 16)
            dve.sem_inc(s_read, 2)
            dve.sem_inc(pv_read, 1)

            dve.wait_ge(fills_set, 4)
            dve.wait_ge(pads_mean, 4)

            def load(hb, half):
                to, of = (slice(HALO, SCOLS), slice(0, SCOLS - HALO)) if half == 0 else \
                         (slice(0, SCOLS - HALO), slice(W - (SCOLS - HALO), W))
                dve.tensor_scalar(strip[:, half, :, to], x[:, bass.ds(hb * BLOCK, WIN), of], rstd[:, 0:1], shift[:, 0:1],
                                  ALU.mult, ALU.add).then_inc(strip_ready, 1)

            def read_k(G, i, n):
                dve.wait_ge(misc_done, n + 1)
                if i == 0 and not is_first(G):
                    dve.wait_ge(k_split, 3 * G)
                dve.tensor_tensor(k32[:, 2 * i:2 * i + 2, :], misc_ps[:, 0:2 * KEYS].rearrange("p (k n) -> p k n", n=KEYS),
                                  relb[:, :, :].rearrange("p i j -> p (i j)").unsqueeze(1).to_broadcast([P, 2, KEYS]),
                                  ALU.add).then_inc(k32_ready, 1)
                dve.wait_ge(k32_ready, 3 * G + i + 1)
                dve.sem_inc(misc_read, 1)

            def row_stats(hb):
                dve.wait_ge(x_added, 4 * hb + 7)
                for i in range(2):
                    rows = x_img[:, bass.ds(hb * BLOCK + i * (BLOCK // 2), BLOCK // 2), :]
                    dve.bn_stats(stats_out[:, bass.ds((hb * 2 + i) * 6, 6)],
                                 rows.rearrange("p h w -> p (h w)")).then_inc(rows_counted, 1)

            def row_max(U, par, j):
                f = U * NFILL + j
                dve.wait_ge(s_filled, f + 1)
                dve.tensor_reduce(mx[:, par, j // 3, 2 * (j % 3):2 * (j % 3) + 2],
                                  s_ps[j % 2][:, 0:2 * KEYS].rearrange("p (k n) -> p k n", n=KEYS), AX.X, ALU.max).then_inc(s_read, 1)

            def split_max(U, par, n, b_last, placed):
                dve.wait_ge(misc_done, n + 1)
                if placed is not None:
                    dve.wait_ge(m_placed[b_last], placed)
                src = misc_ps[0:2 * NB, 0:P]
                dve.tensor_scalar(mparts[:, par, 0, :], src, -1.0, None, ALU.mult).then_inc(m_split, 1)
                dve.wait_ge(m_split, 2 * U + 1)
                dve.scalar_tensor_tensor(out=mparts[:, par, 1, :], in0=src, scalar=-1.0, in1=mparts[:, par, 0, :],
                                         op0=ALU.mult, op1=ALU.subtract).then_inc(m_split, 1)
                dve.wait_ge(m_split, 2 * U + 2)
                dve.sem_inc(misc_read, 1)

            def read_sums(G, U, half, b):
                dve.wait_ge(misc_done, G * MISC + EARLY)
                dve.wait_ge(pv_done, U * 3 + 4)
                dve.tensor_copy(osb[:, half, b, :].rearrange("p (i k j) -> p k i j", i=BLOCK, j=BLOCK),
                                pv_ps[:, 0:NB * QS].rearrange("p (k i j) -> p k i j", i=BLOCK, j=BLOCK)).then_inc(pv_read, 1)

            def invert_sums(G, i):
                dve.wait_ge(sums_in_done, 2 * G + i + 1)
                dve.reciprocal(sums_in[:, i, 1, :], sums_in[:, i, 1, :]).then_inc(recip_done, 1)

            for half in range(2):
                load(0, half)
            for i in range(3):
                read_k(0, i, i)
            for i in range(3):
                read_k(1, i, 7 + i)
            dve.wait_ge(misc_done, 4)
            dve.wait_ge(win_ready, 1)
            load(1, 0)
            for U in range(2):
                for j in range(NFILL):
                    row_max(U, U, j)
            split_max(0, 0, 11, None, None)
            for j in range(2):
                row_max(2, 0, j)
            split_max(1, 1, 12, None, None)

            INVERT_AT = {(2, 0): 0, (3, 0): 1}

            def body(hb, first=False):
                for half in range(2):
                    G = hb * 2 + half
                    for b in range(B):
                        U = G * B + b
                        for s in range(3):
                            if last_use(b, s):
                                ub, us, kind, i = last_use(b, s)
                                n = use_number(G, ub, us)
                                if kind == "k":
                                    read_k(G + 2, i, n)
                            for k in range(2):
                                row_max(U + 2 + s // 2, (b + s // 2) % 2, (2 * s + 2 + k) % NFILL)
                            if (b, s) in INVERT_AT:
                                invert_sums(G, INVERT_AT[b, s])
                            if s == 2:
                                split_max(U + 2, b % 2, use_number(G, b, "max"), b, G * 32 + 32)
                        read_sums(G, U, half, b)
                        if b == 0:
                            dve.wait_ge(win_ready, G + 2)
                            load(hb + (1 + half), 1 - half)
                        if b == 1 and half == 1 and not first:
                            row_stats(hb - 1)

            body(0, first=True)
            with dve.Fori(1, NHB) as hb:
                body(hb)
            for i in range(2):
                invert_sums(2 * NHB, i)
            row_stats(NHB - 1)
            dve.wait_ge(rows_counted, 2 * NHB)

        @block.tensor
        def _(pe):
            pe.wait_ge(consts_in, 16 * 16)
            pe.wait_ge(fills_set, 4)
            pe.wait_ge(pv_zero, 1)
            pe.sem_inc(pv_done, 1)
            pe.sem_inc(st_done, 1)

            def use(kind, half, i, n):
                pe.wait_ge(misc_read, n + 1)
                if kind == "v":
                    for t in range(4):
                        blk, chunk = (4 * i + t) // 2, t % 2
                        mm = pe.matmul(misc_ps[0:HKEYS, P * t:P * (t + 1)], xwin[:, half, blk, HKEYS * chunk:HKEYS * (chunk + 1)],
                                       wv[:, :], start=True, stop=True)
                elif kind == "o":
                    N = BLOCK * NB * BLOCK // 2
                    for k in range(2):
                        for b in range(B):
                            mm = pe.matmul(misc_ps[C * b:C * (b + 1), N * k:N * (k + 1)], hrows[:, k, :],
                                           osb[:, half, b, N * i:N * (i + 1)], start=True, stop=True)
                elif kind == "k":
                    for k in range(2):
                        at = BLOCK * (2 * i + k)
                        mm = pe.matmul(misc_ps[:, KEYS * k:KEYS * (k + 1)], wk[:, :], strip[:, half, :, at:at + WIN],
                                       start=True, stop=True)
                else:
                    for blk in range(NB):
                        mm = pe.matmul(misc_ps[:, QS * blk:QS * (blk + 1)], wq[:, :],
                                       strip[:, half, HALO:HALO + BLOCK, HALO + BLOCK * blk:HALO + BLOCK * (blk + 1)],
                                       start=True, stop=True)
                mm.then_inc(misc_done, 1)

            def maxima(U, par, n):
                pe.wait_ge(misc_read, n + 1)
                pe.wait_ge(s_read, U * NFILL + NFILL + 2)
                pe.transpose(misc_ps[0:2 * NB, 0:P], mx[:, par].rearrange("p a k -> p (a k)"), ident[:, :]).then_inc(misc_done, 1)

            def fill(U, half, b, j, uses):
                if j == 0 and b % 2 == 0:
                    pe.wait_ge(stacked[half][b // 2], 16 * LOADS * uses)
                f = U * NFILL + j
                pe.wait_ge(s_read, f + 1)
                for k in range(2):
                    blk = 2 * (j % 3) + k
                    mm = pe.matmul(s_ps[j % 2][:, KEYS * k:KEYS * (k + 1)],
                                   qst[0:ROWS, half, b // 2, b % 2, j // 3, blk].rearrange("p s q -> p (s q)"),
                                   kst[0:ROWS, half, b // 2, b % 2, j // 3, blk, :], start=True, stop=True)
                mm.then_inc(s_filled, 1)

            def turned_scores(st, slot, half, b, s, placed):
                if placed is not None:
                    pe.wait_ge(m_placed[b], placed)
                pe.wait_ge(exp_done, st)
                for k in range(2):
                    blk = 2 * s + k
                    for pair in range(2):
                        for chunk in range(2):
                            at = 512 * k + P * (2 * pair + chunk)
                            mm = pe.matmul(st_ps[slot][0:HKEYS, at:at + P],
                                           kst[0:ROWS + 2, half, b // 2, b % 2, pair, blk, HKEYS * chunk:HKEYS * (chunk + 1)],
                                           qst[0:ROWS + 2, half, b // 2, b % 2, pair, blk].rearrange("p s q -> p (s q)"), start=True, stop=True)
                mm.then_inc(st_done, 1)

            def sums(G, U, half, b, s, slot):
                if s == 0:
                    pe.wait_ge(v_ready, 3 * G + 3)
                    pe.wait_ge(pv_read, U + 1)
                pe.wait_ge(exp_done, U * 3 + s + 2)
                for k in range(2):
                    blk = 2 * s + k
                    for chunk in range(2):
                        for h in range(HEADS):
                            mm = pe.matmul(pv_ps[32 * h:32 * h + 2 * D, QS * blk:QS * (blk + 1)],
                                           v[:, half, 2 * blk + chunk, b, h, :],
                                           pt[:, slot, k, h // 2, chunk, QS * (h % 2):QS * (h % 2 + 1)],
                                           start=(chunk == 0), stop=(chunk == 1))
                mm.then_inc(pv_done, 1)

            for half in range(2):
                pe.wait_ge(strip_ready, half + 1)
                for i in range(3):
                    use("k", half, i, 7 * half + i)
                use("q", half, 0, 7 * half + 3)
                if half == 0:
                    pe.wait_ge(win_ready, 1)
                    for i in range(3):
                        use("v", 0, i, 4 + i)
            for U in range(3):
                for j in range(NFILL if U < 2 else 2):
                    fill(U, 0, U, j, 1)
                if U > 0:
                    maxima(U - 1, U - 1, 10 + U)
            turned_scores(0, 0, 0, 0, 0, 32)

            with pe.Fori(0, NHB) as hb:
                for half in range(2):
                    G = hb * 2 + half
                    for b in range(B):
                        U = G * B + b
                        for s in range(3):
                            ahead = b + 2 + s // 2
                            later = half + ahead // B
                            for k in range(2):
                                fill(U + 2 + s // 2, later % 2, ahead % B, (2 * s + 2 + k) % NFILL, hb + (1 + later // 2))
                            if s < 2:
                                turned_scores(U * 3 + s + 1, (b + s + 1) % 2, half, b, s + 1, None)
                            else:
                                turned_scores(U * 3 + 3, (b + 1) % 2, (half + (b + 1) // B) % 2, (b + 1) % B, 0,
                                              G * 32 + 32 * (1 + (b + 1) // B))
                            if s == 2:
                                maxima(U + 2, b % 2, use_number(G, b, "max"))
                            if s > 0:
                                sums(G, U, half, b, s, (b + s) % 2)
                            if s < len(USES[b]):
                                kind, i = USES[b][s]
                                if kind == "q":
                                    pe.wait_ge(strip_ready, G + 3)
                                if kind == "v" and i == 0:
                                    pe.wait_ge(win_ready, G + 2)
                                if kind == "o" and i == 0:
                                    pe.wait_ge(pv_read, G * B + 1)
                                use(kind, 1 - half if kind in "vo" else half, i, use_number(G, b, s))
                            if s == 0:
                                sums(G, U, half, b, s, (b + s) % 2)
            pe.wait_ge(pv_read, 2 * NHB * B + 1)
            for i in range(2):
                use("o", 1, i, 2 * NHB * MISC + EARLY + i)


def lstm_layer(nc, x, w_ih_rep, w_hh_t, bias_ih, bias_hh, w_lin_t, b_lin_rep, stats_in, stats_out):
    HID = 128
    STEPS = 4
    CHUNKS = ((0, 8), (8, 24), (24, 48), (48, 72), (72, 96))
    CHUNK = max(b - a for a, b in CHUNKS)
    NCH = len(CHUNKS)
    ctx = ExitStack()
    with ctx:
        def sb(name, shape, dt=F32):
            return ctx.enter_context(nc.sbuf_tensor("l1_" + name, shape, dt))

        def sem(name):
            return ctx.enter_context(nc.semaphore("l1_" + name))

        mv = sb("mv", [P, 2])
        std = sb("std", [P, 1])
        rstd = sb("rstd", [P, 1])
        eps = sb("eps", [P, 1])
        xn = sb("xn", [P, 2, CHUNK, H])
        part = sb("part", [P, 2, 3, CHUNK, H], BF16)
        xs = sb("xs", [P, B, W, H], BF16)
        wih = sb("wih", [P, 4 * HID])
        wp = sb("wp", [P, 3, 4 * HID], BF16)
        wa = sb("wa", [P, 4 * HID], BF16)
        wb = sb("wb", [P, 4 * HID], BF16)
        whh = sb("whh", [HID, 4 * HID])
        bi = sb("bi", [HID, 4])
        bh = sb("bh", [HID, 4])
        bias = sb("bias", [HID, 4])
        wlin = sb("wlin", [HID, C])
        blin = sb("blin", [P, 1])
        gate = sb("gate", [HID, 2, 4, 2 * H])
        prod = sb("prod", [HID, 2, 2, 2 * H])
        cell = sb("cell", [HID, 2, 2 * H])
        tcell = sb("tcell", [HID, 2, 2 * H])
        hid = sb("hid", [HID, 2, 2, 2 * H])
        gates_ps = [ctx.enter_context(nc.psum_tensor(f"l1_g{i}", [P, 512], F32)) for i in range(6)]
        lin_ps = [ctx.enter_context(nc.psum_tensor(f"l1_l{i}", [P, 512], F32)) for i in range(2)]

        weights_in = sem("weights_in")
        dve_prep = sem("dve_prep")
        eps_set = sem("eps_set")
        std_ready = sem("std_ready")
        part_cast = sem("part_cast")
        part_ready = sem("part_ready")
        pool_step = sem("pool_step")
        w_split = sem("w_split")
        stacked = [sem(f"stacked{i}") for i in range(NCH)]
        xs_ready = sem("xs_ready")
        first_ready = sem("first_ready")
        state_zero = sem("state_zero")
        gates_done = [sem(f"gates_done{c}") for c in range(2)]
        gates_act = [sem(f"gates_act{c}") for c in range(2)]
        prods_done = [sem(f"prods_done{c}") for c in range(2)]
        cell_done = [sem(f"cell_done{c}") for c in range(2)]
        tanh_done = [sem(f"tanh_done{c}") for c in range(2)]
        hid_done = [sem(f"hid_done{c}") for c in range(2)]
        lin_done = sem("lin_done")
        lin_added = sem("lin_added")
        columns_counted = sem("columns_counted")

        SLICE = [0, 2, 1, 3]
        FUNC = [ACT.Sigmoid, ACT.Tanh, ACT.Sigmoid, ACT.Sigmoid]
        x_img = x[:, HALO:HALO + H, :]

        def gate_ps(c, g):
            return gates_ps[3 * c + max(g - 1, 0)][:, (g == 1) * 2 * H:((g == 1) + 1) * 2 * H]

        block = ctx.enter_context(nc.Block())

        @block.sync
        def _(sp):
            for dst, src in ((wih, w_ih_rep), (whh, w_hh_t), (bi, bias_ih), (bh, bias_hh),
                             (wlin, w_lin_t), (blin, b_lin_rep)):
                sp.dma_start(dst[:, :], src).then_inc(weights_in, 16)
            def copied(k):
                sp.wait_ge(stacked[k], 16 * 16)
                sp.sem_inc(xs_ready, (CHUNKS[k][1] - CHUNKS[k][0]) // (2 * STEPS))

            for k in range(NCH):
                sp.wait_ge(*((part_ready, k) if k else (first_ready, 1)))
                first, last = CHUNKS[k]
                for b in range(B):
                    for row, piece in enumerate((0, 1, 2, 0)):
                        sp.dma_start(xs[32 * row:32 * row + 32, b, first:last, :],
                                     part[32 * b:32 * b + 32, k % 2, piece, 0:last - first, :]).then_inc(stacked[k], 16)
                copied(k)

        @block.gpsimd
        def _(pool):
            pool.memset(eps[:, :], GN_EPS).then_inc(eps_set, 1)
            pool.memset(cell[:, :, :], 0.0).then_inc(state_zero, 1)
            pool.memset(hid[:, :, :, :], 0.0).then_inc(state_zero, 1)
            n = 0

            def then(ins):
                nonlocal n
                ins.then_inc(pool_step, 1)
                n += 1
                pool.wait_ge(pool_step, n)

            pool.wait_ge(weights_in, 96)
            then(pool.tensor_tensor(bias[:, :], bi[:, :], bh[:, :], ALU.add))
            then(pool.tensor_copy(wp[:, 0], wih[:, :]))
            then(pool.tensor_tensor(wih[:, :], wih[:, :], wp[:, 0], ALU.subtract))
            then(pool.tensor_copy(wp[:, 1], wih[:, :]))
            then(pool.tensor_tensor(wp[:, 2], wih[:, :], wp[:, 1], ALU.subtract))
            then(pool.tensor_copy(wa[0:96, :], wp[0:96, 0]))
            then(pool.tensor_copy(wa[96:128, :], wp[96:128, 1]))
            then(pool.tensor_copy(wb[0:32, :], wp[0:32, 2]))
            then(pool.tensor_copy(wb[32:64, :], wp[32:64, 1]))
            then(pool.tensor_copy(wb[64:96, :], wp[64:96, 1]))
            then(pool.memset(wb[96:128, :], 0.0))
            pool.sem_inc(w_split, 1)

            pool.wait_ge(dve_prep, 2)
            xt = x_img.rearrange("p f t -> p t f")
            for k in range(1, NCH):
                if k == 2:
                    pool.wait_ge(first_ready, 1)
                if k >= 2:
                    pool.wait_ge(stacked[k - 2], 16 * 16)
                first, last = CHUNKS[k]
                y = xn[:, k % 2, 0:last - first]
                part0, part1, part2 = (part[:, k % 2, i, 0:last - first] for i in range(3))
                then(pool.tensor_scalar(y, xt[:, first:last, :], mv[:, 0:1], rstd[:, 0:1], ALU.subtract, ALU.mult))
                then(pool.tensor_copy(part0, y))
                then(pool.tensor_tensor(y, y, part0, ALU.subtract))
                then(pool.tensor_copy(part1, y))
                then(pool.tensor_tensor(part2, y, part1, ALU.subtract))
                pool.sem_inc(part_ready, 1)

        @block.scalar
        def _(act):
            act.wait_ge(eps_set, 1)
            act.wait_ge(dve_prep, 1)
            act.activation(std[:, :], mv[:, 1:2], ACT.Sqrt, bias=eps[:, :]).then_inc(std_ready, 1)
            act.wait_ge(dve_prep, 3)
            act.activation(part[:, 0, 0, 0:CHUNKS[0][1]], xn[:, 0, 0:CHUNKS[0][1]], ACT.Copy).then_inc(part_cast, 1)
            act.wait_ge(dve_prep, 4)
            act.activation(part[:, 0, 1, 0:CHUNKS[0][1]], xn[:, 0, 0:CHUNKS[0][1]], ACT.Copy).then_inc(part_cast, 1)
            act.wait_ge(w_split, 1)

            def gates(i, c):
                for g in range(4):
                    act.wait_ge(gates_done[c], 4 * i + max(g + 1, 2))
                    if g == 0:
                        act.wait_ge(hid_done[c], i + 1)
                    act.activation(gate[:, c, g, :], gate_ps(c, g), FUNC[g],
                                   bias=bias[:, SLICE[g]:SLICE[g] + 1]).then_inc(gates_act[c], 1)

            def cells(i, c):
                act.wait_ge(cell_done[c], i + 1)
                act.activation(tcell[:, c, :], cell[:, c, :], ACT.Tanh).then_inc(tanh_done[c], 1)

            with act.Fori(0, W, 2 * STEPS) as t:
                for s in range(2 * STEPS):
                    for c in range(2):
                        gates(t + s, c)
                        cells(t + s, c)

        @block.vector
        def _(dve):
            n = known_stats(dve, stats_in, mv[:, :], dve_prep)
            dve.wait_ge(std_ready, 1)
            dve.reciprocal(rstd[:, :], std[:, :]).then_inc(dve_prep, 1)
            n += 1
            dve.wait_ge(dve_prep, n)
            xt = x_img.rearrange("p f t -> p t f")
            y = xn[:, 0, 0:CHUNKS[0][1]]
            part0, part1, part2 = (part[:, 0, i, 0:CHUNKS[0][1]] for i in range(3))
            dve.tensor_scalar(y, xt[:, 0:CHUNKS[0][1], :], mv[:, 0:1], rstd[:, 0:1], ALU.subtract, ALU.mult).then_inc(dve_prep, 1)
            dve.wait_ge(part_cast, 1)
            dve.tensor_tensor(y, y, part0, ALU.subtract).then_inc(dve_prep, 1)
            dve.wait_ge(dve_prep, n + 2)
            dve.wait_ge(part_cast, 2)
            dve.tensor_tensor(part2, y, part1, ALU.subtract).then_inc(first_ready, 1)
            dve.wait_ge(state_zero, 2)

            def cell_ops(i, c):
                dve.wait_ge(gates_act[c], 4 * i + 6)
                dve.tensor_tensor(prod[:, c, 0], gate[:, c, 0], gate[:, c, 1], ALU.mult).then_inc(prods_done[c], 1)
                dve.wait_ge(gates_act[c], 4 * i + 7)
                dve.tensor_tensor(prod[:, c, 1], gate[:, c, 2], cell[:, c], ALU.mult).then_inc(prods_done[c], 1)
                dve.wait_ge(prods_done[c], 2 * i + 2)
                dve.tensor_tensor(cell[:, c], prod[:, c, 0], prod[:, c, 1], ALU.add).then_inc(cell_done[c], 1)

            def hid_ops(i, c, s):
                dve.wait_ge(gates_act[c], 4 * i + 8)
                dve.wait_ge(tanh_done[c], i + 1)
                dve.tensor_tensor(hid[:, c, (s + 1) % 2], gate[:, c, 3], tcell[:, c], ALU.mult).then_inc(hid_done[c], 1)

            def add_linear(group, j):
                dve.wait_ge(lin_done, 2 * STEPS * (group + 1))
                cols = x_img[:, :, bass.ds(group * STEPS, STEPS)]
                ps = lin_ps[j][:, 0:STEPS * H].rearrange("p (t f) -> p f t", f=H)
                dve.scalar_tensor_tensor(out=cols, in0=ps, scalar=blin[:, 0:1], in1=cols,
                                         op0=ALU.add, op1=ALU.add).then_inc(lin_added, 1)

            def column_stats(group):
                dve.wait_ge(lin_added, group + 3)
                dve.bn_stats(stats_out[:, bass.ds(group * 6, 6)],
                             x_img[:, :, bass.ds(group * STEPS, STEPS)]).then_inc(columns_counted, 1)

            def body(k, first=False):
                for j in range(2):
                    group = k * 2 + j
                    for s in range(STEPS):
                        for c in range(2):
                            cell_ops(group * STEPS + s, c)
                            hid_ops(group * STEPS + s, c, s)
                        if s == 1 and not (first and j == 0):
                            add_linear(group - 1, 1 - j)
                        if s == 2 and not (first and j == 0):
                            column_stats(group - 1)

            body(0, first=True)
            with dve.Fori(1, W // (2 * STEPS)) as k:
                body(k)
            add_linear(W // STEPS - 1, 1)
            column_stats(W // STEPS - 1)
            dve.wait_ge(columns_counted, W // STEPS)

        @block.tensor
        def _(pe):
            pe.wait_ge(w_split, 1)
            pe.wait_ge(state_zero, 2)

            def step_gates(i, c, s):
                xin = xs[:, 2 * c:2 * c + 2, bass.ds(i, 1), :]
                for g in range(4):
                    w = slice(HID * SLICE[g], HID * (SLICE[g] + 1))
                    if g != 1:
                        pe.wait_ge(gates_act[c], 4 * i + max(g + 1, 2))
                    pe.matmul(gate_ps(c, g), wa[:, w], xin, start=True, stop=False)
                    pe.matmul(gate_ps(c, g), wb[:, w], xin, start=False, stop=False)
                    if g == 0:
                        pe.wait_ge(hid_done[c], i + 1)
                    pe.matmul(gate_ps(c, g), whh[:, w], hid[:, c, s % 2], start=False, stop=True).then_inc(gates_done[c], 1)

            def linear(i, c, s, j):
                pe.wait_ge(hid_done[c], i + 2)
                for b in (2 * c, 2 * c + 1):
                    mm = pe.matmul(lin_ps[j][32 * b:32 * b + 32, s * H:(s + 1) * H], wlin[:, :],
                                   hid[:, c, (s + 1) % 2, (b % 2) * H:(b % 2 + 1) * H], start=True, stop=True)
                mm.then_inc(lin_done, 1)

            def body(k, first=False):
                pe.wait_ge(xs_ready, k + 1)
                for j in range(2):
                    for s in range(STEPS):
                        i = (k * 2 + j) * STEPS + s
                        step_gates(i, 0, s)
                        if s > 0:
                            linear(i - 1, 1, s - 1, j)
                        elif not (first and j == 0):
                            linear(i - 1, 1, STEPS - 1, 1 - j)
                        step_gates(i, 1, s)
                        if s == 0:
                            pe.wait_ge(lin_added, k * 2 + j + 1)
                        linear(i, 0, s, j)

            pe.sem_inc(lin_added, 2)
            for c in range(2):
                pe.sem_inc(hid_done[c], 1)
                pe.sem_inc(gates_act[c], 4)
            body(0, first=True)
            with pe.Fori(1, W // (2 * STEPS)) as k:
                body(k)
            linear(W - 1, 1, STEPS - 1, 1)


NTAP = 9
PADW = W + 2
NOFF = 2 * NTAP
NOUT = NOFF + NTAP
GROUP = 4
TILEW = 32
NCOL = W // TILEW
NGROUP = H // GROUP
NPREP = NGROUP + 2
NTILE = NPREP * NCOL
TABROWS = GROUP * NPREP
TABLE = TABROWS * PADW * B


def deformable_layer(nc, x, conv_w, pix_bias, pix_base, group_step, batch_base, identity, out_w, table,
                     stats_in, stats_out):
    ROWS = GROUP + 2
    SW = PADW + 1
    TURNS = GROUP + 1
    HALF = GROUP // 2
    COPIES = GROUP
    STEPS = 14
    PREP = 3
    ctx = ExitStack()
    with ctx:
        def sb(name, shape, dt=F32):
            return ctx.enter_context(nc.sbuf_tensor("l2_" + name, shape, dt))

        def sem(name):
            return ctx.enter_context(nc.semaphore("l2_" + name))

        mv = sb("mv", [P, 2])
        std = sb("std", [P, 1])
        rstd = sb("rstd", [P, 1])
        shift = sb("shift", [P, 1])
        eps = sb("eps", [P, 1])
        ident = sb("ident", [P, P])
        cw = sb("cw", [P, NTAP, B * NOUT])
        pbias = sb("pbias", [P, NOUT])
        base = sb("base", [P, NCOL, NOFF])
        step4 = sb("step4", [P, NCOL, NOFF])
        bbase = sb("bbase", [P, B, NTAP])
        wout = sb("wout", [3 * C, 3, C])
        strip = sb("strip", [P, 2, ROWS, SW])
        tab = sb("tab", [PADW, 2, GROUP, B, 4 * C])
        ot = sb("ot", [B * NOUT, NCOL, P])
        raw = sb("raw", [P, NCOL, B, NOUT])
        pos = sb("pos", [P, NCOL, B, NOFF])
        posi = sb("posi", [P, NCOL, B, NOFF], I32)
        flo = sb("flo", [P, NCOL, B, NOFF])
        gt = sb("gt", [P, NCOL, B, NOFF])
        frac = sb("frac", [P, NCOL, B, NOFF])
        rest = sb("rest", [P, NCOL, B, NOFF])
        mask = sb("mask", [P, NCOL, B, NTAP])
        mx0 = sb("mx0", [P, NCOL, B, NTAP])
        mx1 = sb("mx1", [P, NCOL, B, NTAP])
        idxf = sb("idxf", [P, NCOL, B, NTAP])
        index = sb("index", [P, NTILE, B * NTAP], I32)
        weight = sb("weight", [P, NTILE, B, NTAP, 4])
        tidx = sb("tidx", [P, NCOL, B * NTAP], I32)
        RING = B
        got = sb("got", [P, RING, NTAP, 4 * C])
        red = sb("red", [P, 2, NTAP, 2 * C])
        samp = sb("samp", [P, 2, NTAP, C])
        sampt = sb("sampt", [3 * C, 2, 3, P])

        def ps(name):
            return ctx.enter_context(nc.psum_tensor("l2_" + name, [P, 512], F32))

        off_ps = ps("off")
        offt_ps = ps("offt")
        tab_ps = [ps(f"tab{i}") for i in range(2)]
        samp_ps = [ps(f"samp{i}") for i in range(2)]
        out_ps = [ps("out0"), ps("out1"), tab_ps[0]]
        turn_ps = [*tab_ps, *samp_ps, out_ps[0]]

        ident_in = sem("ident_in")
        consts_in = sem("consts_in")
        cw_zero = sem("cw_zero")
        pool_passed = sem("pool_passed")
        dve_prep = sem("dve_prep")
        pads_zero = sem("pads_zero")
        pads_mean = sem("pads_mean")
        eps_set = sem("eps_set")
        std_ready = sem("std_ready")
        strip_ready = sem("strip_ready")
        off_done = sem("off_done")
        off_out = sem("off_out")
        offt_done = sem("offt_done")
        raw_done = sem("raw_done")
        mask_done = sem("mask_done")
        chain = sem("chain")
        tab_turned = sem("tab_turned")
        tab_copied = [sem(f"tab_copied{i}") for i in range(2)]
        tab_stored = [[sem(f"tab_stored{i}{h}") for h in range(2)] for i in range(2)]
        tidx_ready = sem("tidx_ready")
        gathered = [sem(f"gathered{i}") for i in range(RING)]
        weighted = sem("weighted")
        reduced = sem("reduced")
        summed = sem("summed")
        x_added = sem("x_added")
        rows_counted = sem("rows_counted")
        samp_turned = sem("samp_turned")
        sampt_ready = sem("sampt_ready")
        convolved = sem("convolved")

        x_img = x[:, HALO:HALO + H, :]
        x_pad = x[:, HALO - 1:XROWS, :]

        PREPARED = NPREP + 1

        def turns(engine):
            found, copies = {}, 0
            for r in range(engine, TURNS, 2):
                copies += (r > 0) + (r < GROUP)
                found[r] = copies
            return found

        def table_rows(eng, g2, g, j, engine, copy):
            started = 0
            for r in turns(engine):
                for above in (1, 0):
                    if 0 <= r - above < GROUP:
                        if (r - above) // HALF >= started:
                            eng.wait_ge(tab_stored[j][started], 16 * (g2 + 1))
                            started += 1
                        src = turn_ps[r][0:PADW, 0:2 * P].rearrange("p (s b c) -> p b s c", s=2, b=B)
                        half = slice(2 * C, 4 * C) if above else slice(0, 2 * C)
                        copy(tab[:, j, r - above, :, half].rearrange("p b (s c) -> p b s c", s=2), src,
                             TURNS * (g + 1) + r + 1).then_inc(tab_copied[engine], 1)

        block = ctx.enter_context(nc.Block())

        @block.sync
        def _(sp):
            sp.dma_start(ident[:, :], identity).then_inc(ident_in, 16)
            sp.wait_ge(cw_zero, 1)
            for b in range(B):
                sp.dma_start(cw[C * b:C * (b + 1), :, NOUT * b:NOUT * (b + 1)],
                             conv_w.rearrange("c (t o) -> c t o", t=NTAP)).then_inc(consts_in, 16)
            for dst, src in ((pbias[:, :], pix_bias), (base[:, :, :], pix_base.rearrange("p (c n) -> p c n", c=NCOL)),
                             (step4[:, :, :], group_step.rearrange("p (c n) -> p c n", c=NCOL)),
                             (bbase[:, :, :], batch_base.rearrange("p (b n) -> p b n", b=B)),
                             (wout[:, :, :], out_w.rearrange("k (g o) -> k g o", g=3))):
                sp.dma_start(dst, src).then_inc(consts_in, 16)

            def store_table(g, j):
                for h in range(2):
                    for engine in range(2):
                        sp.wait_ge(tab_copied[engine], COPIES * (g + 1) + (h + 1) * COPIES // 2)
                    sp.dma_start(table.rearrange("(r s b) k -> s r (b k)", s=PADW, b=B)[:, bass.ds(g * GROUP + HALF * h, HALF), :],
                                 tab[:, j, HALF * h:HALF * (h + 1)].rearrange("s r b k -> s r (b k)")).then_inc(tab_stored[j][h], 16)

            with sp.Fori(0, NPREP // 2) as g2:
                store_table(g2 * 2, 0)
                store_table(g2 * 2 + 1, 1)

        @block.gpsimd
        def _(pool):
            pool.memset(cw[:, :, :], 0.0).then_inc(cw_zero, 1)
            pool.memset(eps[:, :], GN_EPS).then_inc(eps_set, 1)
            pool.memset(strip[:, :, :, :], 0.0).then_inc(pads_zero, 1)
            for j in range(2):
                for h in range(2):
                    pool.wait_ge(tab_stored[j][h], 16 * (NPREP // 2 + 1))

            with pool.Fori(0, NGROUP) as g:
                for c in range(NCOL):
                    t = g * NCOL + c
                    wait_apart(pool, tidx_ready, t + 1, pool_passed)
                    for b in range(B):
                        wait_apart(pool, reduced, t * B + b + 1, pool_passed)
                        for n in range(NTAP):
                            at = tidx[:, c, b * NTAP + n:b * NTAP + n + 1].bitcast(U32)
                            pool.indirect_dma_start(
                                out=got[:, b, n, :], out_offset=None, in_=table,
                                in_offset=bass.IndirectOffsetOnAxis(ap=at, axis=0)).then_inc(gathered[b], 16)

        @block.scalar
        def _(act):
            act.wait_ge(eps_set, 1)
            act.wait_ge(dve_prep, 1)
            act.activation(std[:, :], mv[:, 1:2], ACT.Sqrt, bias=eps[:, :]).then_inc(std_ready, 1)
            act.wait_ge(dve_prep, PREP)
            act.wait_ge(pads_zero, 1)
            act.wait_ge(pads_mean, 2)
            act.sem_inc(off_out, 1)
            for engine in range(2):
                act.sem_inc(tab_copied[engine], COPIES)
            for j in range(2):
                for h in range(2):
                    act.sem_inc(tab_stored[j][h], 16)

            def prepare(g, j):
                if not is_first(g):
                    act.wait_ge(tab_turned, TURNS * g)
                act.activation(strip[:, j, :, 1:1 + W], x_pad[:, bass.ds(g * GROUP, ROWS), :], ACT.Identity,
                               bias=shift[:, 0:1], scale=rstd[:, 0:1]).then_inc(strip_ready, 1)

            def copy(out, src, turned):
                act.wait_ge(tab_turned, turned)
                return act.activation(out, src, ACT.Copy)

            def prepare_again(g):
                if not is_first(g):
                    act.wait_ge(off_done, g)
                act.activation(strip[:, 0, :, 1:1 + W], x_pad[:, bass.ds(g * GROUP, ROWS), :], ACT.Identity,
                               bias=shift[:, 0:1], scale=rstd[:, 0:1]).then_inc(strip_ready, 1)

            def offsets(g):
                act.wait_ge(off_done, g + 1)
                act.wait_ge(offt_done, g + 1)
                act.activation(ot[:, :, :], off_ps[0:B * NOUT, 0:NCOL * P].rearrange("p (c n) -> p c n", n=P),
                               ACT.Copy).then_inc(off_out, 1)

            def masks(g):
                act.wait_ge(raw_done, g + 2)
                act.wait_ge(chain, STEPS * g + 1)
                act.activation(mask[:, :, :, :], raw[:, :, :, NOFF:NOUT], ACT.Sigmoid).then_inc(mask_done, 1)

            prepare(0, 0)
            with act.Fori(0, NPREP // 2) as g2:
                for j in range(2):
                    g = g2 * 2 + j
                    prepare(g + 1, 1 - j)
                    table_rows(act, g2, g, j, 0, copy)

            act.wait_ge(tab_turned, TURNS * (NPREP + 1))
            act.wait_ge(strip_ready, PREPARED)
            for g in range(2):
                prepare_again(g)
                offsets(g)
                masks(g)
            with act.Fori(0, NGROUP) as g:
                prepare_again(g + 2)
                for c in range(NCOL):
                    for b in range(B):
                        u = (g * NCOL + c) * B + b
                        act.wait_ge(samp_turned, u + 1)
                        act.wait_ge(convolved, u + 1)
                        act.activation(sampt[:, b % 2, :, :], samp_ps[b % 2][0:3 * C, 0:3 * P].rearrange("p (g n) -> p g n", g=3),
                                       ACT.Copy).then_inc(sampt_ready, 1)
                    if c == 0:
                        offsets(g + 2)
                    if c == 1:
                        masks(g + 2)

        @block.vector
        def _(dve):
            n = known_stats(dve, stats_in, mv[:, :], dve_prep)
            dve.wait_ge(std_ready, 1)
            dve.reciprocal(rstd[:, :], std[:, :]).then_inc(dve_prep, 1)
            dve.wait_ge(dve_prep, n + 1)
            dve.scalar_tensor_tensor(out=shift[:, :], in0=mv[:, 0:1], scalar=-1.0, in1=rstd[:, :],
                                     op0=ALU.mult, op1=ALU.mult).then_inc(dve_prep, 1)
            dve.tensor_scalar(x[:, 0:HALO, :], x[:, 0:HALO, :], 0.0, mv[:, 0:1], ALU.mult, ALU.add).then_inc(pads_mean, 1)
            dve.tensor_scalar(x[:, HALO + H:XROWS, :], x[:, HALO + H:XROWS, :], 0.0, mv[:, 0:1],
                              ALU.mult, ALU.add).then_inc(pads_mean, 1)
            dve.sem_inc(raw_done, 1)
            dve.sem_inc(chain, 1)

            def both(one):
                return one.unsqueeze(2).to_broadcast([P, NCOL, B, one.shape[2]])

            def group_math(g):
                start = g * STEPS + 1
                k = 0

                def step(ins):
                    nonlocal k
                    ins.then_inc(chain, 1)
                    k += 1
                    dve.wait_ge(chain, start + k)

                dve.wait_ge(offt_done, g + 2)
                turned = offt_ps[:, 0:NCOL * P].rearrange("p (c n) -> p c n", n=P)[:, :, 0:B * NOUT].rearrange(
                    "p c (b o) -> p c b o", b=B)
                bias = pbias[:, :].unsqueeze(1).unsqueeze(1).to_broadcast([P, NCOL, B, NOUT])
                dve.tensor_tensor(raw[:, :, :, :], turned, bias, ALU.add).then_inc(raw_done, 1)
                dve.wait_ge(raw_done, g + 2)
                step(dve.tensor_tensor(pos[:, :, :, :], raw[:, :, :, 0:NOFF], both(base[:, :, :]), ALU.add))
                step(dve.tensor_scalar(pos[:, :, :, :], pos[:, :, :, :], 0.0, float(PADW - 1), ALU.max, ALU.min))
                step(dve.tensor_copy(posi[:, :, :, :], pos[:, :, :, :]))
                step(dve.tensor_copy(flo[:, :, :, :], posi[:, :, :, :]))
                step(dve.tensor_tensor(gt[:, :, :, :], flo[:, :, :, :], pos[:, :, :, :], ALU.is_gt))
                step(dve.tensor_tensor(flo[:, :, :, :], flo[:, :, :, :], gt[:, :, :, :], ALU.subtract))
                step(dve.tensor_tensor(frac[:, :, :, :], pos[:, :, :, :], flo[:, :, :, :], ALU.subtract))
                step(dve.tensor_scalar(rest[:, :, :, :], frac[:, :, :, :], -1.0, 1.0, ALU.mult, ALU.add))
                step(dve.scalar_tensor_tensor(out=idxf[:, :, :, :], in0=flo[:, :, :, 0:NTAP], scalar=float(PADW),
                                              in1=flo[:, :, :, NTAP:NOFF], op0=ALU.mult, op1=ALU.add))
                for c in range(NCOL):
                    ins = dve.scalar_tensor_tensor(
                        out=index[:, bass.ds(g * NCOL + c, 1), :].rearrange("p o (b n) -> p (o b) n", b=B), in0=idxf[:, c],
                        scalar=float(B), in1=bbase[:, :, :], op0=ALU.mult, op1=ALU.add)
                step(ins)
                dve.wait_ge(mask_done, g + 1)
                step(dve.tensor_tensor(mx0[:, :, :, :], mask[:, :, :, :], rest[:, :, :, 0:NTAP], ALU.mult))
                step(dve.tensor_tensor(mx1[:, :, :, :], mask[:, :, :, :], frac[:, :, :, 0:NTAP], ALU.mult))
                for q, (mx, fy) in enumerate(((mx0, rest), (mx0, frac), (mx1, rest), (mx1, frac))):
                    for c in range(NCOL):
                        ins = dve.tensor_tensor(weight[:, bass.ds(g * NCOL + c, 1), :, :, q].rearrange("p o b n -> p (o b) n"),
                                                mx[:, c], fy[:, c, :, NTAP:NOFF], ALU.mult)
                step(ins)
                step(dve.tensor_tensor(base[:, :, :], base[:, :, :], step4[:, :, :], ALU.add))
                assert k == STEPS

            def copy(out, src, turned):
                dve.wait_ge(tab_turned, turned)
                return dve.tensor_copy(out, src)

            with dve.Fori(0, NPREP // 2) as g2:
                for j in range(2):
                    table_rows(dve, g2, g2 * 2 + j, j, 1, copy)
            dve.wait_ge(consts_in, 16 * 9)
            group_math(0)

            dve.sem_inc(reduced, RING)
            def tile_index(t, c):
                dve.tensor_copy(tidx[:, c, :], index[:, bass.ds(t, 1), :].rearrange("p o n -> p (o n)")).then_inc(tidx_ready, 1)

            def unit(t, c, b):
                u = t * B + b
                dve.wait_ge(gathered[b], 16 * NTAP * (t + 1))
                corners = got[:, b, :, :].rearrange("p n (k c) -> p (n k) c", c=C)
                w = weight[:, bass.ds(t, 1), b, :, :].rearrange("p o n k -> p (o n k)").unsqueeze(2).to_broadcast([P, NTAP * 4, C])
                dve.tensor_tensor(corners, corners, w, ALU.mult).then_inc(weighted, 1)
                dve.wait_ge(weighted, u + 1)
                dve.tensor_tensor(red[:, b % 2], got[:, b, :, 0:2 * C], got[:, b, :, 2 * C:4 * C], ALU.add).then_inc(reduced, 1)
                dve.wait_ge(reduced, u + 1 + RING)
                dve.tensor_tensor(samp[:, b % 2], red[:, b % 2, :, 0:C], red[:, b % 2, :, C:2 * C], ALU.add).then_inc(summed, 1)

            tile_index(0, 0)
            group_math(1)
            with dve.Fori(0, NGROUP) as g:
                for c in range(NCOL):
                    t = g * NCOL + c
                    tile_index(t + 1, (c + 1) % NCOL)
                    for b in range(B):
                        if b >= 2:
                            dve.wait_ge(samp_turned, t * B + b - 1)
                        unit(t, c, b)
                    dve.wait_ge(convolved, t * B + B + 2)
                    dve.wait_ge(strip_ready, PREPARED + 2 + g)
                    rows = x_img[:, bass.ds(g * GROUP, GROUP), TILEW * c:TILEW * (c + 1)]
                    dve.tensor_tensor(rows, out_ps[c][:, 0:P].rearrange("p (h w) -> p h w", w=TILEW), rows,
                                      ALU.add).then_inc(x_added, 1)
                    if c == 1:
                        group_math(g + 2)
                dve.wait_ge(x_added, g * NCOL + NCOL)
                dve.bn_stats(stats_out[:, bass.ds(g * 6, 6)],
                             x_img[:, bass.ds(g * GROUP, GROUP), :].rearrange("p h w -> p (h w)")).then_inc(rows_counted, 1)

        @block.tensor
        def _(pe):
            pe.wait_ge(ident_in, 16)
            pe.wait_ge(dve_prep, PREP)
            pe.sem_inc(tab_turned, TURNS)
            pe.sem_inc(offt_done, 1)

            def turn_rows(g, j):
                pe.wait_ge(strip_ready, g + 1)
                for r in range(TURNS):
                    pe.wait_ge(tab_copied[r % 2], COPIES * g + turns(r % 2)[r])
                    for s in range(2):
                        mm = pe.transpose(turn_ps[r][0:PADW, P * s:P * (s + 1)], strip[:, j, r, s:s + PADW], ident[:, :])
                    mm.then_inc(tab_turned, 1)

            def offsets(g):
                pe.wait_ge(strip_ready, PREPARED + 1 + g)
                pe.wait_ge(off_out, g + 1)
                dst = off_ps[0:B * NOUT, 0:NCOL * P]
                for tap in range(NTAP):
                    dy, dx = tap // 3, tap % 3
                    src = strip[:, 0, dy:dy + GROUP, dx:dx + W].rearrange("p h (c w) -> p c h w", w=TILEW)
                    mm = pe.matmul(dst, cw[:, tap, :], src, start=(tap == 0), stop=(tap == NTAP - 1))
                mm.then_inc(off_done, 1)

            def turn_offsets(g):
                pe.wait_ge(off_out, g + 2)
                pe.wait_ge(raw_done, g + 1)
                for c in range(NCOL):
                    mm = pe.transpose(offt_ps[:, P * c:P * c + B * NOUT], ot[:, c, :], ident[0:B * NOUT, 0:B * NOUT])
                mm.then_inc(offt_done, 1)

            with pe.Fori(0, NPREP // 2) as g2:
                for j in range(2):
                    turn_rows(g2 * 2 + j, j)
            pe.wait_ge(consts_in, 16 * 9)
            for g in range(2):
                offsets(g)
                turn_offsets(g)

            for engine in range(2):
                pe.wait_ge(tab_copied[engine], COPIES * (NPREP + 1))
            pe.sem_inc(convolved, 2)
            with pe.Fori(0, NGROUP) as g:
                offsets(g + 2)
                for c in range(NCOL):
                    t = g * NCOL + c
                    for b in range(B):
                        u = t * B + b
                        pe.wait_ge(summed, u + 1)
                        for q in range(3):
                            mm = pe.transpose(samp_ps[b % 2][0:3 * C, P * q:P * (q + 1)],
                                              samp[:, b % 2, 3 * q:3 * q + 3, :].rearrange("p n c -> p (n c)"), ident[:, :])
                        mm.then_inc(samp_turned, 1)
                        pe.wait_ge(sampt_ready, u + 1)
                        for q in range(3):
                            mm = pe.matmul(out_ps[c][C * b:C * (b + 1), 0:P], wout[:, q, :], sampt[:, b % 2, q, :],
                                           start=(q == 0), stop=(q == 2))
                        mm.then_inc(convolved, 1)
                    if c == 0:
                        turn_offsets(g + 2)


def block_transform_layer(nc, x, m_left, m_right, same_block, identity, out, stats_in):
    BS = 8
    PAIR = 2 * BS
    NPAIR = W // PAIR
    NROW = H // BS
    FIRST = 4
    PREP = 3 + 2
    ctx = ExitStack()
    with ctx:
        def sb(name, shape, dt=F32):
            return ctx.enter_context(nc.sbuf_tensor("l3_" + name, shape, dt))

        def sem(name):
            return ctx.enter_context(nc.semaphore("l3_" + name))

        mv = sb("mv", [P, 2])
        std = sb("std", [P, 1])
        rstd = sb("rstd", [P, 1])
        shift = sb("shift", [P, 1])
        eps = sb("eps", [P, 1])
        ml = sb("ml", [P, P])
        mr = sb("mr", [P, P])
        same = sb("same", [P, P])
        kron = sb("kron", [P, P])
        ident = sb("ident", [P, P])
        xr = sb("xr", [P, 2, NPAIR, P])
        xt = sb("xt", [P, 2, NPAIR, P])
        t_ps = [[ctx.enter_context(nc.psum_tensor(f"l3_t{j}{i}", [P, 512], F32)) for i in range(2)] for j in range(2)]
        o_ps = [[ctx.enter_context(nc.psum_tensor(f"l3_o{j}{i}", [P, 512], F32)) for i in range(2)] for j in range(2)]

        consts_in = sem("consts_in")
        dve_prep = sem("dve_prep")
        eps_set = sem("eps_set")
        std_ready = sem("std_ready")
        row_normed = sem("row_normed")
        row_turned = sem("row_turned")
        turned_out = sem("turned_out")
        row_multiplied = sem("row_multiplied")
        row_added = sem("row_added")
        stored = sem("stored")

        x_img = x[:, HALO:HALO + H, :]
        x_below = x[:, HALO:XROWS, :]
        out_rows = out.rearrange("b c h w -> (b c) h w")
        HALVES = ((0, FIRST), (FIRST, NPAIR))

        block = ctx.enter_context(nc.Block())

        @block.sync
        def _(sp):
            for dst, src in ((ml, m_left), (mr, m_right), (same, same_block), (ident, identity)):
                sp.dma_start(dst[:, :], src).then_inc(consts_in, 16)
            with sp.Fori(0, NROW) as r:
                sp.wait_ge(row_added, 2 * r + 6)
                sp.dma_start(out_rows[:, bass.ds(r * BS, BS), :], x_img[:, bass.ds(r * BS, BS), :]).then_inc(stored, 16)
            sp.wait_ge(stored, 16 * NROW)

        @block.gpsimd
        def _(pool):
            pool.memset(eps[:, :], GN_EPS).then_inc(eps_set, 1)

        @block.scalar
        def _(act):
            act.wait_ge(eps_set, 1)
            act.wait_ge(dve_prep, 1)
            act.activation(std[:, :], mv[:, 1:2], ACT.Sqrt, bias=eps[:, :]).then_inc(std_ready, 1)
            act.wait_ge(dve_prep, PREP)

            def normalise(r, j):
                act.wait_ge(row_turned, r + 1)
                rows = x_below[:, bass.ds(r * BS, BS), :].rearrange("p h (c w) -> p c h w", w=PAIR)
                act.activation(xr[:, j].rearrange("p c (h w) -> p c h w", w=PAIR), rows, ACT.Identity, bias=shift[:, 0:1],
                               scale=rstd[:, 0:1]).then_inc(row_normed, 1)

            def evacuate(r, j):
                act.wait_ge(row_turned, r + 3)
                act.wait_ge(row_multiplied, r + 1)
                for i, (a, b) in enumerate(HALVES):
                    act.activation(xt[:, j, a:b, :], t_ps[j][i][:, 0:P * (b - a)].rearrange("p (c n) -> p c n", n=P),
                                   ACT.Copy).then_inc(turned_out, 1)

            normalise(0, 0)
            with act.Fori(0, NROW // 2) as pair:
                r = pair * 2
                normalise(r + 1, 1)
                evacuate(r, 0)
                normalise(r + 2, 0)
                evacuate(r + 1, 1)

        @block.vector
        def _(dve):
            n = known_stats(dve, stats_in, mv[:, :], dve_prep)

            def then(ins):
                nonlocal n
                ins.then_inc(dve_prep, 1)
                n += 1
                dve.wait_ge(dve_prep, n)

            dve.wait_ge(std_ready, 1)
            then(dve.reciprocal(rstd[:, :], std[:, :]))
            then(dve.scalar_tensor_tensor(out=shift[:, :], in0=mv[:, 0:1], scalar=-1.0, in1=rstd[:, :],
                                          op0=ALU.mult, op1=ALU.mult))
            dve.wait_ge(consts_in, 64)
            then(dve.tensor_tensor(kron[:, :], ml[:, :], mr[:, :], ALU.mult))
            then(dve.tensor_tensor(kron[:, :], kron[:, :], same[:, :], ALU.mult))
            assert n == PREP
            dve.sem_inc(row_added, 4)

            def add(r, j):
                dve.wait_ge(row_multiplied, r + 3)
                for i, (a, b) in enumerate(HALVES):
                    rows = x_img[:, bass.ds(r * BS, BS), PAIR * a:PAIR * b].rearrange("p h (c w) -> p c h w", w=PAIR)
                    ps = o_ps[j][i][:, 0:P * (b - a)].rearrange("p (c h w) -> p c h w", h=BS, w=PAIR)
                    dve.wait_ge(row_normed, r + 1)
                    dve.tensor_tensor(rows, ps, rows, ALU.add).then_inc(row_added, 1)

            with dve.Fori(0, NROW // 2) as pair:
                r = pair * 2
                add(r, 0)
                add(r + 1, 1)

        @block.tensor
        def _(pe):
            pe.wait_ge(dve_prep, PREP)
            pe.wait_ge(consts_in, 64)
            pe.sem_inc(row_turned, 2)
            pe.sem_inc(row_multiplied, 2)
            pe.sem_inc(turned_out, 4)

            def turn(r, j):
                pe.wait_ge(row_normed, r + 1)
                pe.wait_ge(turned_out, 2 * r + 2)
                for c in range(NPAIR):
                    i = c // FIRST
                    mm = pe.transpose(t_ps[j][i][:, P * (c - FIRST * i):P * (c - FIRST * i + 1)],
                                      xr[:, j, c, :], ident[:, :])
                mm.then_inc(row_turned, 1)

            def multiply(r, j):
                pe.wait_ge(turned_out, 2 * r + 6)
                pe.wait_ge(row_added, 2 * r + 2)
                for c in range(NPAIR):
                    i = c // FIRST
                    mm = pe.matmul(o_ps[j][i][:, P * (c - FIRST * i):P * (c - FIRST * i + 1)],
                                   xt[:, j, c, :], kron[:, :], start=True, stop=True)
                mm.then_inc(row_multiplied, 1)

            turn(0, 0)
            with pe.Fori(0, NROW // 2) as pair:
                r = pair * 2
                turn(r + 1, 1)
                multiply(r, 0)
                turn(r + 2, 0)
                multiply(r + 1, 1)


def network(nc, x_in, l0, l1, l2, l3, out):
    table = nc.dram_tensor("sample_table", [TABLE, 4 * C], F32, kind="Internal").ap()
    k_parts = nc.dram_tensor("k_parts", [2, P, NTERM, NB * KEYS], BF16, kind="Internal").ap()
    q_parts = nc.dram_tensor("q_parts", [2, P, NTERM, NB * 2 * QS], BF16, kind="Internal").ap()
    with ExitStack() as ctx:
        x = ctx.enter_context(nc.sbuf_tensor("x", [P, XROWS, W], F32))
        counted = [ctx.enter_context(nc.sbuf_tensor(f"counted{i}", [P, 6 * STATS], F32)) for i in range(3)]
        halo_attention_layer(nc, x_in, x, *l0, k_parts, q_parts, counted[0])
        lstm_layer(nc, x, *l1, counted[0], counted[1])
        deformable_layer(nc, x, *l2, table, counted[1], counted[2])
        block_transform_layer(nc, x, *l3, out, counted[2])


def kernel(**inputs):
    import numpy as np
    import concourse.bacc as bacc
    from concourse.bass_utils import run_bass_kernel_spmd

    a = {k: np.asarray(v) for k, v in inputs.items()}
    nc = bacc.Bacc("TRN2", target_bir_lowering=False, num_devices=1)
    arrays = {}

    def put(name, array):
        array = np.ascontiguousarray(array)
        arrays[name] = array
        return nc.dram_tensor(name, array.shape, mybir.dt.from_np(array.dtype), kind="ExternalInput").ap()

    identity = put("identity", np.eye(P, dtype=np.float32))
    p = np.arange(P)

    w_qkv = a["L0_conv_w_qkv"]
    rel_h = np.broadcast_to(a["L0_conv_rel_h"][0], (WIN, WIN, D // 2))
    rel_w = np.broadcast_to(a["L0_conv_rel_w"][0], (WIN, WIN, D // 2))
    rel = np.concatenate([rel_h, rel_w], axis=-1).transpose(2, 0, 1).reshape(D, KEYS)
    head_mask = np.where((p[:, None] % C // D) % 2 == np.arange(2), D ** -0.5, 0.0).astype(np.float32)
    head_rows = np.zeros((HEADS, C // D, D, 2, HEADS, D), np.float32)
    for h in range(HEADS):
        for k in range(2):
            head_rows[h, k, :, k, h, :] = np.eye(D)
    l0 = [put("w_q", w_qkv[0:C].T), put("w_k", w_qkv[C:2 * C].T), put("w_v", w_qkv[2 * C:3 * C].T),
          put("rel", np.tile(rel, (P // D, 1))), put("head_mask", head_mask),
          put("head_rows", head_rows.reshape(P, 2 * C)), identity]

    hid = a["L1_conv_W_hh"].shape[1]
    l1 = [put("w_ih", np.tile(a["L1_conv_W_ih"].T, (B, 1))), put("w_hh", a["L1_conv_W_hh"].T),
          put("b_ih", a["L1_conv_b_ih"].reshape(4, hid).T), put("b_hh", a["L1_conv_b_hh"].reshape(4, hid).T),
          put("w_lin", a["L1_conv_W_lin"].T), put("b_lin", np.tile(a["L1_conv_b_lin"], B)[:, None])]

    conv_w = np.concatenate([a["L2_conv_p_w"], a["L2_conv_m_w"]]).transpose(1, 2, 3, 0).reshape(C, NTAP * NOUT)
    bias = np.broadcast_to(np.concatenate([a["L2_conv_p_b"], a["L2_conv_m_b"]]), (P, NOUT))
    base = np.zeros((P, NCOL, 2, NTAP), np.float32)
    tap = np.arange(NTAP)
    base[:, :, 0, :] = 1 + (p // TILEW)[:, None, None] + (tap // 3 - 1)
    base[:, :, 1, :] = 1 + (p % TILEW)[:, None, None] + TILEW * np.arange(NCOL)[:, None] + (tap % 3 - 1)
    step = np.zeros((P, NCOL, 2, NTAP), np.float32)
    step[:, :, 0, :] = GROUP
    batch_base = np.broadcast_to(np.repeat(np.arange(B), NTAP).astype(np.float32), (P, B * NTAP))
    out_w = a["L2_conv_conv_w"].transpose(2, 3, 1, 0).reshape(3, 3 * C, C).transpose(1, 0, 2).reshape(3 * C, 3 * C)
    l2 = [put("conv_w", conv_w), put("pix_bias", bias), put("pix_base", base.reshape(P, NCOL * NOFF)),
          put("group_step", step.reshape(P, NCOL * NOFF)), put("batch_base", batch_base), identity, put("out_w", out_w)]

    m = a["L3_conv_M"]
    bs = m.shape[0]
    full = (bs, 2, bs, bs, 2, bs)
    l3 = [put("m_left", np.broadcast_to(m.T[:, None, None, :, None, None], full).reshape(P, P)),
          put("m_right", np.broadcast_to(m.T[None, None, :, None, None, :], full).reshape(P, P)),
          put("same_block", np.broadcast_to(np.eye(2, dtype=np.float32)[None, :, None, None, :, None], full).reshape(P, P)),
          identity]

    x_in = put("x_in", a["x"])
    out = nc.dram_tensor("out", list(a["x"].shape), F32, kind="ExternalOutput").ap()
    network(nc, x_in, l0, l1, l2, l3, out)
    result = run_bass_kernel_spmd(nc, [arrays], core_ids=[0])
    return result.results[0]["out"]
```
